# Optimizing a Trainium2 kernel written in Bass

```python
import numpy as np
import jax
import jax.numpy as jnp

def _softmax(x, axis=-1):
    return jax.nn.softmax(x, axis=axis)

def _gelu(x):
    return jax.nn.gelu(x, approximate=True)

def _silu(x):
    return jax.nn.silu(x)

def _sigmoid(x):
    return jax.nn.sigmoid(x)

def _layernorm(x, axis=-1, eps=1e-05):
    m = jnp.mean(x, axis=axis, keepdims=True)
    v = jnp.var(x, axis=axis, keepdims=True)
    return (x - m) / jnp.sqrt(v + eps)

def _scatter_add(tgt, idx, src, axis=0):
    return tgt.at[idx].add(src)

def _segment_sum(src, seg, n):
    return jax.ops.segment_sum(src, seg, n)
kernel_name = 'mk_gnn_preln_d4_gnn_r32_a3ace4'

def setup_inputs(seed: int=0):
    np.random.seed(seed)
    _w = jnp.asarray

    def _rec_inputs():
        import jax
        import jax.numpy as jnp
        _gk = jax.random.key(seed)
        x = -0.0003713 + 1 * jax.random.normal(jax.random.fold_in(_gk, 1), (3125, 256), jnp.float32)
        _s = jax.random.randint(jax.random.fold_in(_gk, 2), (25000,), 0, 3125, jnp.int32)
        _d = jax.random.randint(jax.random.fold_in(_gk, 3), (25000,), 0, 3125, jnp.int32)
        _loop = jnp.arange(3125, dtype=jnp.int32)
        src = jnp.concatenate([_s, _d, _loop])
        dst = jnp.concatenate([_d, _s, _loop])
        _o = jnp.argsort(dst, stable=True)
        src = src[_o]
        dst = dst[_o]
        edge_attr_64 = 0.000102155 + 1.00015 * jax.random.normal(jax.random.fold_in(_gk, 11), (53125, 64), jnp.float32)
        edge_type_64 = jax.random.randint(jax.random.fold_in(_gk, 13), (53125,), 0, 64, jnp.int32)
        return (x, src, dst, edge_attr_64, edge_type_64)
    x, src, dst, edge_attr_64, edge_type_64 = _rec_inputs()

    def _L0_gnn_setup():
        import jax, jax.numpy as jnp
        import numpy as np
        N_NODES = 50000
        N_EDGES = 15625
        HDIM = 256
        EDIM = 64
        MSG_H = 512
        UPD_H = 512
        LN_EPS = 1e-05

        def _mlp(x, W1, b1, W2, b2):
            return jax.nn.relu(x @ W1 + b1) @ W2 + b2

        def _layer_norm(x, gamma, beta):
            mu = jnp.mean(x, axis=-1, keepdims=True)
            var = jnp.mean(jnp.square(x - mu), axis=-1, keepdims=True)
            return (x - mu) * jax.lax.rsqrt(var + LN_EPS) * gamma + beta
        key = jax.random.key(seed)
        ks = jax.random.split(key, 12)

        def lin_init(k, fan_in, fan_out):
            bound = 1.0 / np.sqrt(fan_in)
            return jax.random.uniform(k, (fan_in, fan_out), jnp.float32, -bound, bound)
        h = jax.random.normal(ks[0], (N_NODES, HDIM), jnp.float32)
        edge_index = jax.random.randint(ks[1], (2, N_EDGES), 0, N_NODES, jnp.int64)
        edge_attr = jax.random.normal(ks[2], (N_EDGES, EDIM), jnp.float32)
        eW1 = lin_init(ks[3], 2 * HDIM + EDIM, MSG_H)
        eb1 = jnp.zeros((MSG_H,), jnp.float32)
        eW2 = lin_init(ks[4], MSG_H, HDIM)
        eb2 = jnp.zeros((HDIM,), jnp.float32)
        nW1 = lin_init(ks[5], 2 * HDIM, UPD_H)
        nb1 = jnp.zeros((UPD_H,), jnp.float32)
        nW2 = lin_init(ks[6], UPD_H, HDIM)
        nb2 = jnp.zeros((HDIM,), jnp.float32)
        ln_gamma = jnp.ones((HDIM,), jnp.float32)
        ln_beta = jnp.zeros((HDIM,), jnp.float32)
        return {'h': h, 'edge_index': edge_index, 'edge_attr': edge_attr, 'eW1': eW1, 'eb1': eb1, 'eW2': eW2, 'eb2': eb2, 'nW1': nW1, 'nb1': nb1, 'nW2': nW2, 'nb2': nb2, 'ln_gamma': ln_gamma, 'ln_beta': ln_beta}
    _L0_gnn_all = _L0_gnn_setup()
    _L0_gnn_in = {k: v for k, v in _L0_gnn_all.items() if k in ('eW1', 'eb1', 'eW2', 'eb2', 'nW1', 'nb1', 'nW2', 'nb2', 'ln_gamma', 'ln_beta')}
    del _L0_gnn_all

    def _L1_gnn_setup():
        import jax, jax.numpy as jnp
        import numpy as np
        N_NODES = 50000
        N_EDGES = 15625
        IN_DIM = 256
        HID = 64
        HEADS = 4
        N_REL = 64
        key = jax.random.key(seed)
        ks = jax.random.split(key, 16)
        s = 0.02
        return {'node_features': jax.random.normal(ks[0], (N_NODES, IN_DIM), jnp.float32), 'edge_index': jax.random.randint(ks[1], (2, N_EDGES), 0, N_NODES, jnp.int32), 'edge_relations': jax.random.randint(ks[2], (N_EDGES,), 0, N_REL, jnp.int32), 'query_emb': jax.random.normal(ks[3], (IN_DIM,), jnp.float32), 'Wq': jax.random.normal(ks[4], (IN_DIM, HID * HEADS), jnp.float32) * s, 'bq': jnp.zeros((HID * HEADS,), jnp.float32), 'Wk': jax.random.normal(ks[5], (IN_DIM, HID * HEADS), jnp.float32) * s, 'bk': jnp.zeros((HID * HEADS,), jnp.float32), 'Wv': jax.random.normal(ks[6], (IN_DIM, HID * HEADS), jnp.float32) * s, 'bv': jnp.zeros((HID * HEADS,), jnp.float32), 'rel_w': jax.random.normal(ks[7], (N_REL, HID), jnp.float32) * s, 'Wo': jax.random.normal(ks[8], (HID * HEADS, IN_DIM), jnp.float32) * s, 'bo': jnp.zeros((IN_DIM,), jnp.float32), 'gamma': jnp.ones((IN_DIM,), jnp.float32), 'beta': jnp.zeros((IN_DIM,), jnp.float32)}
    _L1_gnn_all = _L1_gnn_setup()
    _L1_gnn_in = {k: v for k, v in _L1_gnn_all.items() if k in ('query_emb', 'Wq', 'bq', 'Wk', 'bk', 'Wv', 'bv', 'rel_w', 'Wo', 'bo', 'gamma', 'beta')}
    del _L1_gnn_all

    def _L2_gnn_setup():
        import jax, jax.numpy as jnp
        import numpy as np
        import math
        N, E = (50000, 25000)
        IN_CH, EDGE_DIM, H, C = (256, 64, 8, 32)
        key = jax.random.key(seed)
        ks = jax.random.split(key, 12)

        def xavier(k, shape):
            fan_in, fan_out = (shape[0], shape[1])
            a = math.sqrt(6.0 / (fan_in + fan_out))
            return jax.random.uniform(k, shape, jnp.float32, -a, a)
        x = jax.random.normal(ks[0], (N, IN_CH), jnp.float32)
        edge_attr = jax.random.normal(ks[1], (E, EDGE_DIM), jnp.float32)
        edge_index = jax.random.randint(ks[2], (2, E), 0, N, jnp.int64)
        Wq = xavier(ks[3], (IN_CH, H * C))
        bq = jnp.zeros((H * C,), jnp.float32)
        Wk = xavier(ks[4], (IN_CH, H * C))
        bk = jnp.zeros((H * C,), jnp.float32)
        Wv = xavier(ks[5], (IN_CH, H * C))
        bv = jnp.zeros((H * C,), jnp.float32)
        We = xavier(ks[6], (EDGE_DIM, H * C))
        be = jnp.zeros((H * C,), jnp.float32)
        bias = jnp.zeros((H * C,), jnp.float32)
        return {'x': x, 'edge_attr': edge_attr, 'Wq': Wq, 'bq': bq, 'Wk': Wk, 'bk': bk, 'Wv': Wv, 'bv': bv, 'We': We, 'be': be, 'bias': bias, 'edge_index': edge_index}
    _L2_gnn_all = _L2_gnn_setup()
    _L2_gnn_in = {k: v for k, v in _L2_gnn_all.items() if k in ('Wq', 'bq', 'Wk', 'bk', 'Wv', 'bv', 'We', 'be', 'bias')}
    del _L2_gnn_all

    def _L3_gnn_setup():
        import jax, jax.numpy as jnp
        import numpy as np
        NEG_SLOPE = 0.2
        key = jax.random.key(seed)
        ks = jax.random.split(key, 8)
        N, E, D, H = (3125, 9375, 256, 256)
        x = jax.random.normal(ks[0], (N, D), dtype=jnp.float32)
        edge_index = jax.random.randint(ks[1], (2, E), 0, N, dtype=jnp.int64)
        s = 0.06
        W = jax.random.normal(ks[2], (H, D), dtype=jnp.float32) * s
        att_src = jax.random.normal(ks[3], (H,), dtype=jnp.float32) * s
        att_dst = jax.random.normal(ks[4], (H,), dtype=jnp.float32) * s
        bias = jnp.zeros((H,), dtype=jnp.float32)
        W_ih = jax.random.normal(ks[5], (4 * H, H), dtype=jnp.float32) * s
        W_hh = jax.random.normal(ks[6], (4 * H, H), dtype=jnp.float32) * s
        return {'x': x, 'edge_index': edge_index, 'W': W, 'att_src': att_src, 'att_dst': att_dst, 'bias': bias, 'W_ih': W_ih, 'W_hh': W_hh}
    _L3_gnn_all = _L3_gnn_setup()
    _L3_gnn_in = {k: v for k, v in _L3_gnn_all.items() if k in ('W', 'att_src', 'att_dst', 'bias', 'W_ih', 'W_hh')}
    del _L3_gnn_all
    return {'x': x, 'src': src, 'dst': dst, 'edge_attr_64': edge_attr_64, 'edge_type_64': edge_type_64, 'L0_gnn_eW1': _L0_gnn_in['eW1'], 'L0_gnn_eb1': _L0_gnn_in['eb1'], 'L0_gnn_eW2': _L0_gnn_in['eW2'], 'L0_gnn_eb2': _L0_gnn_in['eb2'], 'L0_gnn_nW1': _L0_gnn_in['nW1'], 'L0_gnn_nb1': _L0_gnn_in['nb1'], 'L0_gnn_nW2': _L0_gnn_in['nW2'], 'L0_gnn_nb2': _L0_gnn_in['nb2'], 'L0_gnn_ln_gamma': _L0_gnn_in['ln_gamma'], 'L0_gnn_ln_beta': _L0_gnn_in['ln_beta'], 'L1_gnn_query_emb': _L1_gnn_in['query_emb'], 'L1_gnn_Wq': _L1_gnn_in['Wq'], 'L1_gnn_bq': _L1_gnn_in['bq'], 'L1_gnn_Wk': _L1_gnn_in['Wk'], 'L1_gnn_bk': _L1_gnn_in['bk'], 'L1_gnn_Wv': _L1_gnn_in['Wv'], 'L1_gnn_bv': _L1_gnn_in['bv'], 'L1_gnn_rel_w': _L1_gnn_in['rel_w'], 'L1_gnn_Wo': _L1_gnn_in['Wo'], 'L1_gnn_bo': _L1_gnn_in['bo'], 'L1_gnn_gamma': _L1_gnn_in['gamma'], 'L1_gnn_beta': _L1_gnn_in['beta'], 'L2_gnn_Wq': _L2_gnn_in['Wq'], 'L2_gnn_bq': _L2_gnn_in['bq'], 'L2_gnn_Wk': _L2_gnn_in['Wk'], 'L2_gnn_bk': _L2_gnn_in['bk'], 'L2_gnn_Wv': _L2_gnn_in['Wv'], 'L2_gnn_bv': _L2_gnn_in['bv'], 'L2_gnn_We': _L2_gnn_in['We'], 'L2_gnn_be': _L2_gnn_in['be'], 'L2_gnn_bias': _L2_gnn_in['bias'], 'L3_gnn_W': _L3_gnn_in['W'], 'L3_gnn_att_src': _L3_gnn_in['att_src'], 'L3_gnn_att_dst': _L3_gnn_in['att_dst'], 'L3_gnn_bias': _L3_gnn_in['bias'], 'L3_gnn_W_ih': _L3_gnn_in['W_ih'], 'L3_gnn_W_hh': _L3_gnn_in['W_hh']}

def reference(x, src, dst, edge_attr_64, edge_type_64, L0_gnn_eW1, L0_gnn_eb1, L0_gnn_eW2, L0_gnn_eb2, L0_gnn_nW1, L0_gnn_nb1, L0_gnn_nW2, L0_gnn_nb2, L0_gnn_ln_gamma, L0_gnn_ln_beta, L1_gnn_query_emb, L1_gnn_Wq, L1_gnn_bq, L1_gnn_Wk, L1_gnn_bk, L1_gnn_Wv, L1_gnn_bv, L1_gnn_rel_w, L1_gnn_Wo, L1_gnn_bo, L1_gnn_gamma, L1_gnn_beta, L2_gnn_Wq, L2_gnn_bq, L2_gnn_Wk, L2_gnn_bk, L2_gnn_Wv, L2_gnn_bv, L2_gnn_We, L2_gnn_be, L2_gnn_bias, L3_gnn_W, L3_gnn_att_src, L3_gnn_att_dst, L3_gnn_bias, L3_gnn_W_ih, L3_gnn_W_hh):
    import jax
    import jax.numpy as jnp

    def _L0_gnn_ref(h, edge_index, edge_attr, eW1, eb1, eW2, eb2, nW1, nb1, nW2, nb2, ln_gamma, ln_beta):
        import jax, jax.numpy as jnp
        import numpy as np
        N_NODES = 50000
        N_EDGES = 15625
        HDIM = 256
        EDIM = 64
        MSG_H = 512
        UPD_H = 512
        LN_EPS = 1e-05

        def _mlp(x, W1, b1, W2, b2):
            return jax.nn.relu(x @ W1 + b1) @ W2 + b2

        def _layer_norm(x, gamma, beta):
            mu = jnp.mean(x, axis=-1, keepdims=True)
            var = jnp.mean(jnp.square(x - mu), axis=-1, keepdims=True)
            return (x - mu) * jax.lax.rsqrt(var + LN_EPS) * gamma + beta
        src = edge_index[0]
        dst = edge_index[1]
        m_in = jnp.concatenate([h[src], h[dst], edge_attr], axis=1)
        m = _mlp(m_in, eW1, eb1, eW2, eb2)
        agg = jax.ops.segment_sum(m, dst, num_segments=h.shape[0])
        h_upd = _mlp(jnp.concatenate([h, agg], axis=1), nW1, nb1, nW2, nb2)
        return _layer_norm(h + h_upd, ln_gamma, ln_beta)

    def _L1_gnn_ref(node_features, edge_index, edge_relations, query_emb, Wq, bq, Wk, bk, Wv, bv, rel_w, Wo, bo, gamma, beta):
        import jax, jax.numpy as jnp
        import numpy as np
        N_NODES = 50000
        N_EDGES = 15625
        IN_DIM = 256
        HID = 64
        HEADS = 4
        N_REL = 64
        N = node_features.shape[0]
        D = rel_w.shape[1]
        H = Wq.shape[1] // D
        enh = node_features + 0.1 * query_emb[None, :]
        Q = (enh @ Wq + bq).reshape(N, H, D)
        K = (enh @ Wk + bk).reshape(N, H, D)
        V = (enh @ Wv + bv).reshape(N, H, D)
        src, dst = (edge_index[0], edge_index[1])
        rel = rel_w[edge_relations]
        mod_k = K[src] + 0.2 * rel[:, None, :]
        scores = jnp.einsum('ehd,ehd->eh', Q[dst], mod_k) / D ** 0.5
        seg_max = jax.ops.segment_max(scores, dst, num_segments=N)
        ex = jnp.exp(scores - seg_max[dst])
        denom = jax.ops.segment_sum(ex, dst, num_segments=N)
        w = ex / denom[dst]
        agg = jax.ops.segment_sum(w[:, :, None] * V[src], dst, num_segments=N)
        deg = jax.ops.segment_sum(jnp.ones((src.shape[0],), jnp.float32), dst, num_segments=N)
        msgs = jnp.where(deg[:, None, None] > 0, agg, V)
        out = msgs.reshape(N, H * D) @ Wo + bo
        x = out + node_features
        mu = jnp.mean(x, axis=-1, keepdims=True)
        var = jnp.var(x, axis=-1, keepdims=True)
        return (x - mu) / jnp.sqrt(var + 1e-05) * gamma + beta

    def _L2_gnn_ref(x, edge_attr, Wq, bq, Wk, bk, Wv, bv, We, be, bias, edge_index):
        import jax, jax.numpy as jnp
        import numpy as np
        import math
        N, E = (50000, 25000)
        IN_CH, EDGE_DIM, H, C = (256, 64, 8, 32)
        n = x.shape[0]
        q = (x @ Wq + bq).reshape(n, H, C)
        k = (x @ Wk + bk).reshape(n, H, C)
        v = (x @ Wv + bv).reshape(n, H, C)
        dst = edge_index[0]
        src = edge_index[1]
        e = (edge_attr @ We + be).reshape(-1, H, C)
        key_j = k[src] + e
        alpha = (q[dst] * key_j).sum(-1) / math.sqrt(C)
        alpha = jax.nn.softmax(alpha, axis=0)
        out = v[src] * alpha[:, :, None]
        out = jax.ops.segment_sum(out, dst, num_segments=n)
        return out.reshape(n, H * C) + bias

    def _L3_gnn_ref(x, edge_index, W, att_src, att_dst, bias, W_ih, W_hh):
        import jax, jax.numpy as jnp
        import numpy as np
        NEG_SLOPE = 0.2
        N = x.shape[0]
        loops = jnp.arange(N, dtype=edge_index.dtype)
        src = jnp.concatenate([edge_index[0], loops])
        dst = jnp.concatenate([edge_index[1], loops])
        xp = x @ W.T
        a_src = xp @ att_src
        a_dst = xp @ att_dst
        e = jax.nn.leaky_relu(a_src[src] + a_dst[dst], NEG_SLOPE)
        emax = jax.ops.segment_max(e, dst, num_segments=N)
        ex = jnp.exp(e - emax[dst])
        denom = jax.ops.segment_sum(ex, dst, num_segments=N)
        alpha = ex / denom[dst]
        agg = jax.ops.segment_sum(alpha[:, None] * xp[src], dst, num_segments=N)
        hb = jnp.tanh(agg + bias)
        h0 = jnp.zeros_like(hb)
        gates = hb @ W_ih.T + h0 @ W_hh.T
        i, f, g, o = jnp.split(gates, 4, axis=-1)
        c1 = jax.nn.sigmoid(i) * jnp.tanh(g)
        h1 = jax.nn.sigmoid(o) * jnp.tanh(c1)
        return h1
    edge_index = jnp.stack([src, dst])
    h = jnp.maximum(_layernorm(x, axis=-1), 0.0)
    x = x + _L0_gnn_ref(h, edge_index, edge_attr_64, L0_gnn_eW1, L0_gnn_eb1, L0_gnn_eW2, L0_gnn_eb2, L0_gnn_nW1, L0_gnn_nb1, L0_gnn_nW2, L0_gnn_nb2, L0_gnn_ln_gamma, L0_gnn_ln_beta)
    h = jnp.maximum(_layernorm(x, axis=-1), 0.0)
    x = x + _L1_gnn_ref(h, edge_index, edge_type_64, L1_gnn_query_emb, L1_gnn_Wq, L1_gnn_bq, L1_gnn_Wk, L1_gnn_bk, L1_gnn_Wv, L1_gnn_bv, L1_gnn_rel_w, L1_gnn_Wo, L1_gnn_bo, L1_gnn_gamma, L1_gnn_beta)
    h = jnp.maximum(_layernorm(x, axis=-1), 0.0)
    x = x + _L2_gnn_ref(h, edge_attr_64, L2_gnn_Wq, L2_gnn_bq, L2_gnn_Wk, L2_gnn_bk, L2_gnn_Wv, L2_gnn_bv, L2_gnn_We, L2_gnn_be, L2_gnn_bias, edge_index)
    h = jnp.maximum(_layernorm(x, axis=-1), 0.0)
    x = x + _L3_gnn_ref(h, edge_index, L3_gnn_W, L3_gnn_att_src, L3_gnn_att_dst, L3_gnn_bias, L3_gnn_W_ih, L3_gnn_W_hh)
    return x

_drawn_inputs = setup_inputs


def setup_inputs(seed=0):
    import zlib

    import numpy as np

    out = dict(_drawn_inputs(seed))
    spreads = {'L0_gnn_eb1': (0.0, 0.1),
     'L0_gnn_eb2': (0.0, 0.1),
     'L0_gnn_nb1': (0.0, 0.292),
     'L0_gnn_nb2': (0.0, 0.1),
     'L0_gnn_ln_gamma': (1.0, 0.2),
     'L0_gnn_ln_beta': (0.0, 0.1),
     'L1_gnn_bq': (0.0, 2.0),
     'L1_gnn_bk': (0.0, 2.0),
     'L1_gnn_bv': (0.0, 0.471),
     'L1_gnn_bo': (0.0, 0.1),
     'L1_gnn_gamma': (1.0, 0.2),
     'L1_gnn_beta': (0.0, 0.1),
     'L2_gnn_bq': (0.0, 2.0),
     'L2_gnn_bk': (0.0, 2.0),
     'L2_gnn_bv': (0.0, 2.0),
     'L2_gnn_be': (0.0, 2.0),
     'L2_gnn_bias': (0.0, 0.1),
     'L3_gnn_bias': (0.0, 0.8)}
    factors = {'L1_gnn_query_emb': 8.0,
     'L1_gnn_Wq': 8.0,
     'L1_gnn_Wk': 8.0,
     'L1_gnn_rel_w': 64.0,
     'L2_gnn_Wq': 8.0,
     'L2_gnn_Wk': 8.0,
     'L2_gnn_Wv': 8.0,
     'L2_gnn_We': 8.0,
     'L3_gnn_att_src': 21.615,
     'L3_gnn_att_dst': 64.0}
    for name, (base, spread) in spreads.items():
        noise = np.random.default_rng([zlib.crc32(name.encode()), seed]).standard_normal(out[name].shape)
        drawn = base * np.exp(spread * noise) if base else spread * noise
        out[name] = jnp.asarray(drawn.astype(out[name].dtype))
    for name, factor in factors.items():
        out[name] = (out[name] * factor).astype(out[name].dtype)
    return out
```

```python
import concourse.bass as bass
from concourse import mybir
from contextlib import ExitStack
import numpy as np

F32 = mybir.dt.float32
BF16 = mybir.dt.bfloat16
I32 = mybir.dt.int32
ALU = mybir.AluOpType
ACT = mybir.ActivationFunctionType
AX = mybir.AxisListType

P = 128
N_NODES = 3125
N_EDGES = 53125
D = 256
D2 = 2 * D
ED = 64
NB = -(-N_NODES // P)
NL = NB * P
QE = 4
NQ = -(-N_EDGES // QE)
EDGE_P = 125
EDGE_C = N_EDGES // EDGE_P
SPAN = 85
COLS = 17
HERE = 5
KEY_MAIN = 2.0
QUADS_MAX = NQ + NL + NB
UNROLL = 4
GRID_C = -(-(QUADS_MAX + UNROLL) // P)
NG_PAD = GRID_C * P
DUMMY = NL
KEY_STEP = 4096
KEY_CAP = 1023
BIG = 3.0e38
LOW = -1.0e30
EPS = 1e-5
REC = 16
R_SRC, R_REL, R_MASK, R_QUAD, R_BLOCK = 0, 4, 8, 12, 13
LANE = 9
SROW = ED + 4
XROW = D + 4


class Phase:

    def __init__(self, nc, ctx, name):
        self.nc, self.ctx, self.sems, self.name = nc, ctx, [], name

    def sb(self, name, shape, dt=F32):
        return self.ctx.enter_context(self.nc.sbuf_tensor(f"{self.name}_{name}", shape, dt))

    def ps(self, name, shape, dt=F32):
        return self.ctx.enter_context(self.nc.psum_tensor(f"{self.name}_{name}", shape, dt))

    def sem(self, name):
        s = self.nc.alloc_semaphore(f"{self.name}_{name}")
        self.sems.append(s)
        return s

    def close(self):
        self.nc.clear_and_free_semaphores(self.sems)
        self.nc.all_engine_barrier()


class Chain:

    def __init__(self, eng, sem, base=0):
        self.eng, self.sem, self.base, self.n = eng, sem, base, 0

    def __call__(self, ins):
        self.n += 1
        ins.then_inc(self.sem, 1)
        self.eng.wait_ge(self.sem, self.base + self.n)


def bc(ap, axis, shape):
    return ap.unsqueeze(axis).broadcast_to(shape)


def blk(ap, b):
    v = ap[:, bass.ds(b, 1)]
    return v.rearrange("p a f -> p (a f)") if len(v.shape) == 3 else v


def first_steps(nc, S, A):
    with ExitStack() as ctx:
        ph = Phase(nc, ctx, "first")
        rows = ph.sb("rows", [SPAN, 2, EDGE_C // SPAN, EDGE_P], I32)
        rows_f = ph.sb("rows_f", [SPAN, 2, EDGE_C // SPAN, EDGE_P])
        ps = [ph.ps(f"ps{i}", [P, 512]) for i in range(2)]
        s_ld, s_iota, s_v, s_f, s_t = (ph.sem(n) for n in ("list_loaded", "iota_done", "dve_step", "rows_ready", "turned"))
        parts = EDGE_C // SPAN
        with nc.Block() as block:
            @block.sync
            def _(sp):
                for i, n in enumerate(("src", "dst")):
                    sp.dma_start(rows[:, i, :, :], A[n].rearrange("(c t p) -> t c p", t=SPAN, p=EDGE_P)).then_inc(s_ld, 16)

            @block.gpsimd
            def _(pool):
                kw = dict(allow_small_or_imprecise_dtypes=True)
                pool.iota(S["iota_c"][:, :], [[1, P]], base=0, channel_multiplier=0, **kw).then_inc(s_iota, 1)
                pool.iota(S["iota_p"][:, :], [[0, 1]], base=0, channel_multiplier=1, **kw).then_inc(s_iota, 1)

            @block.tensor
            def _(pe):
                pe.wait_ge(s_f, 1)
                for i in range(2):
                    for c in range(parts):
                        last = pe.transpose(ps[i][0:EDGE_P, c * SPAN:(c + 1) * SPAN], rows_f[:, i, c, :], S["ident"][0:SPAN, 0:SPAN])
                last.then_inc(s_t, 1)

            @block.vector
            def _(dve):
                step = Chain(dve, s_v)
                dve.wait_ge(s_iota, 2)
                step(dve.tensor_scalar(S["ident"][:, :], S["iota_c"][:, :], S["iota_p"][:, 0:1], None, ALU.is_equal))
                step(dve.tensor_scalar(S["tri"][:, :], S["iota_c"][:, :], S["iota_p"][:, 0:1], None, ALU.is_gt))
                step(dve.memset(S["ones"][:, :], 1.0))
                dve.wait_ge(s_ld, 32)
                step(dve.tensor_copy(rows_f[:, :, :, :], rows[:, :, :, :]))
                dve.nop().then_inc(s_f, 1)
                dve.wait_ge(s_t, 1)
                step(dve.tensor_copy(S["src_i"][:, :], ps[0][0:EDGE_P, 0:EDGE_C]))
                step(dve.tensor_copy(S["dst_i"][:, :], ps[1][0:EDGE_P, 0:EDGE_C]))
        ph.close()


def rank_edges(nc, S, A):
    TURNS = EDGE_C // COLS
    with ExitStack() as ctx:
        ph = Phase(nc, ctx, "rank")
        part_i = ph.sb("part_i", [EDGE_P, EDGE_C], I32)
        src_f = ph.sb("src_f", [EDGE_P, EDGE_C])
        slo = ph.sb("slo", [EDGE_P, EDGE_C], BF16)
        shi = ph.sb("shi", [EDGE_P, EDGE_C], BF16)
        iota_b = ph.sb("iota_b", [P, P], BF16)
        tri_b = ph.sb("tri_b", [P, P], BF16)
        row_i = ph.sb("row_i", [P, 2, COLS, EDGE_P], I32)
        same = ph.sb("same", [EDGE_P, COLS, EDGE_P], BF16)
        oh_lo = ph.sb("oh_lo", [EDGE_P, COLS, P], BF16)
        oh_hi = ph.sb("oh_hi", [EDGE_P, COLS, NB], BF16)
        above = ph.sb("above", [EDGE_P, EDGE_C])
        place = ph.sb("place", [EDGE_P, EDGE_C])
        zeros = ph.sb("zeros", [P, EDGE_C])
        scan = ph.sb("scan", [P, 2, EDGE_C])
        tot = ph.sb("tot", [P, NB])
        cum = ph.sb("cum", [P, NB])
        look = ph.sb("look", [EDGE_P, COLS, NB])
        W = EDGE_C * EDGE_P // 2
        flat = S["state"]
        oh_loT = flat[:, 0:W + 1].bitcast(BF16)[:, 0:2 * W + 1]
        HW = (EDGE_C * NB + 1) // 2
        before = [flat[:, W + 1 + h * HW:W + 1 + (h + 1) * HW].bitcast(BF16)[:, 0:EDGE_C * NB].rearrange("p (t n) -> p t n", n=NB)
                  for h in range(2)]
        hist = before[0]
        psH = [ph.ps(f"psH{i}", [P, 512]) for i in range(2)]
        psS = ph.ps("psS", [P, 512])
        psL = [ph.ps(f"psL{i}", [P, 512]) for i in range(2)]
        s_v, s_row, s_rused, s_oh, s_H, s_hist, s_deg, s_pre, s_L, s_lk, s_bf, s_a = (ph.sem(n) for n in (
            "dve_step", "row_loaded", "row_used", "onehot_ready", "hist_summed", "hist_copied", "deg_ready",
            "prefix_done", "lookup_done", "lookup_used", "before_ready", "constants_ready"))
        s_row = [s_row, ph.sem("row_loaded_b")]
        IN_A, IN_B = 7, 4

        with nc.Block() as block:
            @block.sync
            def _(sp):
                def load(t, h):
                    sp.dma_start(row_i[:, h, :, :].rearrange("p c n -> p (c n)"),
                                 A["src"][bass.ds(t * (COLS * EDGE_P), COLS * EDGE_P)].rearrange("(a n) -> a n", a=1).broadcast_to([P, COLS * EDGE_P])).then_inc(s_row[h], 16)
                with sp.Fori(0, TURNS // 2) as u:
                    for h in range(2):
                        sp.wait_ge(s_rused, u * 2 + h)
                        load(u * 2 + h, h)
                sp.wait_ge(s_rused, TURNS - 1)
                load(TURNS - 1, 0)

            @block.tensor
            def _(pe):
                def histograms(t, h):
                    pe.wait_ge(s_oh, t + 1)
                    for j in range(COLS):
                        last = pe.matmul(psH[h][:, j * NB:(j + 1) * NB], oh_lo[:, j, :],
                                         oh_hi[:, j, :], start=True, stop=True)
                    last.then_inc(s_H, 1)
                with pe.Fori(0, TURNS // 2) as u:
                    for h in range(2):
                        pe.wait_ge(s_hist, u * 2 + h)
                        histograms(u * 2 + h, h)
                histograms(TURNS - 1, 0)
                pe.wait_ge(s_deg, 1)
                pe.matmul(psS[:, 0:NB], S["tri"][:, :], S["deg2"][:, :], start=True, stop=True)
                pe.matmul(psS[:, 64:64 + NB], S["ones"][:, :], S["deg2"][:, :], start=True, stop=True).then_inc(s_pre, 1)
                pe.wait_ge(s_bf, 1)

                def lookup(g, h):
                    for j in range(COLS):
                        for i in range(2):
                            last = pe.matmul(psL[h][0:EDGE_P, j * NB:(j + 1) * NB],
                                             oh_loT[:, bass.ds((g * COLS + j) * EDGE_P, EDGE_P)],
                                             before[i][:, bass.ds(g * COLS + j, 1), :].rearrange("p a n -> p (a n)"), start=(i == 0), stop=(i == 1))
                    last.then_inc(s_L, 1)
                lookup(0, 0)
                with pe.Fori(0, TURNS // 2) as u:
                    for h in range(2):
                        pe.wait_ge(s_lk, u * 2 + h)
                        lookup(u * 2 + (h + 1), 1 - h)

            @block.scalar
            def _(act):
                def copy(t, h):
                    hold(act, s_H, t + 1)
                    act.activation(hist[:, bass.ds(t * COLS, COLS), :], psH[h][:, 0:COLS * NB].rearrange("p (c n) -> p c n", n=NB), ACT.Copy).then_inc(s_hist, 1)
                with act.Fori(0, TURNS // 2) as u:
                    for h in range(2):
                        copy(u * 2 + h, h)
                copy(TURNS - 1, 0)

            @block.vector
            def _(dve):
                step = Chain(dve, s_v)
                step(dve.tensor_copy(iota_b[:, :], S["iota_c"][:, :]))
                step(dve.tensor_scalar(tri_b[:, :], S["iota_c"][:, :], S["iota_p"][:, 0:1], None, ALU.is_lt))
                step(dve.tensor_copy(src_f[:, :], S["src_i"][:, :]))
                step(dve.tensor_scalar(part_i[:, :], S["src_i"][:, :], P - 1, None, ALU.bitwise_and))
                step(dve.tensor_copy(slo[:, :], part_i[:, :]))
                step(dve.tensor_scalar(part_i[:, :], S["src_i"][:, :], 7, None, ALU.logical_shift_right))
                step(dve.tensor_copy(shi[:, :], part_i[:, :]))
                step(dve.memset(zeros[:, :], 0.0))
                n0 = step.n

                def one_hot_hi(t):
                    return dve.tensor_tensor(oh_hi[:, :, :], bc(iota_b[0:EDGE_P, 0:NB], 1, [EDGE_P, COLS, NB]),
                                             bc(shi[:, bass.ds(t * COLS, COLS)], 2, [EDGE_P, COLS, NB]), ALU.is_equal)

                def turn(t, h, half_turns):
                    step = Chain(dve, s_v, t * IN_A + n0)
                    cols = lambda ap: ap[:, bass.ds(t * COLS, COLS)]
                    hold(dve, s_H, t)
                    step(one_hot_hi(t))
                    dve.tensor_tensor(oh_lo[:, :, :], bc(iota_b[0:EDGE_P, :], 1, [EDGE_P, COLS, P]),
                                      bc(cols(slo), 2, [EDGE_P, COLS, P]), ALU.is_equal).then_inc(s_oh, 1)
                    hold(dve, s_row[h], half_turns * 16 + 16)
                    step(dve.tensor_tensor(same[:, :, :], row_i[0:EDGE_P, h, :, :], bc(cols(src_f), 2, [EDGE_P, COLS, EDGE_P]), ALU.is_equal))
                    step(dve.tensor_tensor(same[:, :, :], same[:, :, :], bc(tri_b[0:EDGE_P, 0:EDGE_P], 1, [EDGE_P, COLS, EDGE_P]), ALU.mult))
                    dve.nop(nofuse=True)
                    step(dve.tensor_reduce(cols(above), same[:, :, :], AX.X, ALU.add))
                    rows = row_i[:, h, :, :].rearrange("p c n -> p (c n)")
                    step(dve.tensor_scalar(rows, rows, P - 1, None, ALU.bitwise_and))
                    dve.nop(nofuse=True)
                    step(dve.tensor_scalar(oh_loT[:, bass.ds(t * (COLS * EDGE_P), COLS * EDGE_P)], rows, S["iota_p"][:, 0:1], None, ALU.is_equal))
                    step(dve.nop())
                    dve.nop().then_inc(s_rused, 1)
                    assert step.n == IN_A

                with dve.Fori(0, TURNS // 2) as u:
                    for h in range(2):
                        turn(u * 2 + h, h, u)
                turn(TURNS - 1, 0, TURNS // 2)
                step = Chain(dve, s_v, n0 + TURNS * IN_A)
                dve.wait_ge(s_hist, TURNS)
                step(dve.tensor_reduce(S["deg2"][:, :], hist[:, :, :].rearrange("p t n -> p n t"), AX.X, ALU.add))
                dve.nop().then_inc(s_deg, 1)
                dve.wait_ge(s_pre, 1)
                starts(dve, step, S["start2"], tot, cum, zeros, psS[:, 0:NB], psS[:, 64:64 + NB])
                base = step.base + step.n
                with dve.Fori(0, NB) as b:
                    step = Chain(dve, s_v, b * IN_B + base)
                    one = hist[:, :, bass.ds(b, 1)].rearrange("p t a -> p (t a)")
                    to = lambda h: before[h][:, :, bass.ds(b, 1)].rearrange("p t a -> p (t a)")
                    step(dve.tensor_tensor_scan(scan[:, 0, :], one, zeros[:, :], S["start2"][:, bass.ds(b, 1)], ALU.add, ALU.add))
                    step(dve.tensor_tensor(scan[:, 1, :], scan[:, 0, :], one, ALU.subtract))
                    step(dve.tensor_scalar(to(0), scan[:, 1, :], 0.0, None, ALU.add))
                    step(dve.tensor_tensor(to(1), scan[:, 1, :], to(0), ALU.subtract))
                    assert step.n == IN_B
                dve.nop().then_inc(s_bf, 1)
                base = base + IN_B * NB

                def found(g, h):
                    step = Chain(dve, s_v, g * 3 + base)
                    step(one_hot_hi(g))
                    hold(dve, s_L, g + 1)
                    step(dve.tensor_tensor(look[:, :, :], psL[h][0:EDGE_P, 0:COLS * NB].rearrange("p (j n) -> p j n", n=NB),
                                           oh_hi[:, :, :], ALU.mult))
                    dve.nop().then_inc(s_lk, 1)
                    dve.nop(nofuse=True)
                    step(dve.tensor_reduce(place[:, bass.ds(g * COLS, COLS)], look[:, :, :], AX.X, ALU.add))
                with dve.Fori(0, TURNS // 2) as u:
                    for h in range(2):
                        found(u * 2 + h, h)
                found(TURNS - 1, 0)
                step = Chain(dve, s_v, base + 3 * TURNS)
                step(dve.tensor_tensor(place[:, :], place[:, :], above[:, :], ALU.add))
                step(dve.tensor_copy(S["place_i"][:, :], place[:, :]))
        ph.close()


def starts(dve, step, start, tot, cum, zeros, ps_within, ps_tot):
    step(dve.tensor_copy(tot[:, :], ps_tot))
    step(dve.tensor_tensor_scan(cum[:, :], tot[:, :], zeros[:, 0:NB], 0.0, ALU.add, ALU.add))
    step(dve.tensor_tensor(cum[:, :], cum[:, :], tot[:, :], ALU.subtract))
    step(dve.tensor_tensor(start[:, :], cum[:, :], ps_within, ALU.add))


def sort_edges(nc, S, A):
    RING = 5
    TURNS = EDGE_C // (HERE * RING)
    with ExitStack() as ctx:
        ph = Phase(nc, ctx, "sort")
        row = ph.sb("row", [EDGE_P, RING, HERE, SROW])
        feat = ph.sb("feat", [EDGE_P, RING, HERE, ED])
        idx = ph.sb("idx", [EDGE_P, RING, HERE], I32)
        pad = ph.sb("pad", [NQ * QE - N_EDGES, SROW])
        s_ld = [ph.sem(f"loaded{k}") for k in range(RING)]
        s_st = [ph.sem(f"stored{k}") for k in range(RING)]
        s_row, s_pad, s_pd, s_v = (ph.sem(n) for n in ("rows_ready", "pad_ready", "pad_stored", "dve_step"))
        of = A["edge_attr_64"].rearrange("(t p) f -> p t f", p=EDGE_P)
        with nc.Block() as block:
            @block.sync
            def _(sp):
                with sp.Fori(0, TURNS) as t:
                    for k in range(RING):
                        sp.wait_ge(s_row, t * RING + k + 1 if k else t * RING + 1)
                        sp.dma_start(feat[:, k, :, :], of[:, bass.ds((t * RING + k) * HERE, HERE), :]).then_inc(s_ld[k], 16)
                sp.wait_ge(s_pad, 1)
                sp.dma_start(S["sorted_d"][N_EDGES:NQ * QE, :], pad[:, :]).then_inc(s_pd, 16)
                sp.wait_ge(s_pd, 16)

            @block.vector
            def _(dve):
                dve.memset(pad[:, :], 0.0).then_inc(s_pad, 1)
                step = Chain(dve, s_v)
                step(dve.memset(row[:, :, :, :], 0.0))
                dve.nop().then_inc(s_row, RING)
                with dve.Fori(0, TURNS) as t:
                    step = Chain(dve, s_v, t * (3 * RING) + 1)
                    for k in range(RING):
                        at = bass.ds((t * RING + k) * HERE, HERE)
                        hold(dve, s_st[k], t * (16 * HERE))
                        step(dve.tensor_copy(idx[:, k, :], S["place_i"][:, at]))
                        step(dve.tensor_copy(row[:, k, :, ED].bitcast(I32), S["dst_i"][:, at]))
                        dve.wait_ge(s_ld[k], (t + 1) * 16)
                        step(dve.tensor_copy(row[:, k, :, 0:ED], feat[:, k, :, :]))
                        dve.nop().then_inc(s_row, 1)

            @block.gpsimd
            def _(pool):
                with pool.Fori(0, TURNS) as t:
                    for k in range(RING):
                        hold(pool, s_row, t * RING + (RING + k + 1))
                        for j in range(HERE):
                            pool.indirect_dma_start(
                                out=S["sorted_d"][:, :], out_offset=bass.IndirectOffsetOnAxis(ap=idx[:, k, j:j + 1], axis=0),
                                in_=row[:, k, j, :], in_offset=None).then_inc(s_st[k], 16)
                for k in range(RING):
                    pool.wait_ge(s_st[k], TURNS * HERE * 16)
        ph.close()


def order_nodes(nc, S, A):
    with ExitStack() as ctx:
        ph = Phase(nc, ctx, "order")
        part_i = ph.sb("part_i", [EDGE_P, EDGE_C], I32)
        dlo = ph.sb("dlo", [EDGE_P, EDGE_C], BF16)
        dhi = ph.sb("dhi", [EDGE_P, EDGE_C], BF16)
        iota_b = ph.sb("iota_b", [P, P], BF16)
        node_of = ph.sb("node_of", [P, NB])
        grid = ph.sb("grid", [P, GRID_C])
        PARTS = 5
        PC = EDGE_C // PARTS
        onehot_hi = ph.sb("onehot_hi", [EDGE_P, EDGE_C, NB], BF16)
        flat = S["state"]
        W = PC * P
        onehot_lo = flat[0:EDGE_P, 0:W].bitcast(BF16).rearrange("p (a c n) -> p a c n", a=2, n=P)
        diag = flat[:, W:W + NL].rearrange("p (b n) -> p b n", n=P)
        keyrow = flat[:, W + NL:W + 2 * NL]
        above = flat[:, W + 2 * NL:W + 3 * NL]
        zeros = ph.sb("zeros_b", [EDGE_P, P], BF16)
        deg = ph.sb("deg", [P, NB])
        tot = ph.sb("tot", [P, NB])
        cum = ph.sb("cum", [P, NB])
        zrow = ph.sb("zrow", [P, NB])
        start = ph.sb("start", [P, NB])
        w0 = ph.sb("w0", [P, NB])
        w1 = ph.sb("w1", [P, NB])
        i0 = ph.sb("i0", [P, NB], I32)
        i1 = ph.sb("i1", [P, NB], I32)
        q0 = ph.sb("q0", [P, 2, NB])
        nq = ph.sb("nq", [P, 2, NB])
        key = ph.sb("key", [P, NB])
        pos = ph.sb("pos", [P, NB])
        pos_i = ph.sb("pos_i", [P, NB], I32)
        lane_w = ph.sb("lane_w", [P, NB, LANE], I32)
        lane_f = ph.sb("lane_f", [P, NB, LANE])
        wide = ph.sb("wide", [P, 64])
        mcol = ph.sb("mcol", [64, 1])
        mcols = ph.sb("mcols", [64, P])
        mrow = ph.sb("mrow", [P, 64])
        mend = ph.sb("mend", [P, 2, NB])
        bid = ph.sb("bid", [P, GRID_C])
        bid_i = ph.sb("bid_i", [P, 2, GRID_C], I32)
        pk = ph.ps("pk", [P, 7 * 512])
        ph_ = ph.ps("phist", [P, 512])

        s_iota, s_v, s_part, s_used = (ph.sem(n) for n in ("iota_done", "dve_step", "part_ready", "part_used"))
        s_deg, s_pre, s_diag, s_key, s_keyrow = (ph.sem(n) for n in (
            "deg_ready", "prefix_done", "diag_ready", "key_spread", "keyrow_ready"))
        s_lane, s_scat, s_back, s_m, s_mt, s_mr, s_md = (ph.sem(n) for n in (
            "lanes_ready", "lanes_scattered", "lanes_loaded", "quads_ready", "quads_turned",
            "mcol_ready", "mrow_done"))
        s_out, s_bi = (ph.sem(n) for n in ("block_list_stored", "bid_ready"))

        with nc.Block() as block:
            @block.sync
            def _(sp):
                sp.wait_ge(s_scat, 16 * NB)
                sp.dma_start(S["lane_i"][:, :, :], S["lane_d"].rearrange("(b p) f -> p b f", p=P)).then_inc(s_back, 16)
                for i in range(2):
                    sp.wait_ge(s_bi, i + 1)
                    sp.dma_start(S[f"bid_d{i}"].rearrange("(p c) -> p c", p=P), bid_i[:, i, :]).then_inc(s_out, 16)
                sp.wait_ge(s_out, 32)

            @block.gpsimd
            def _(pool):
                kw = dict(allow_small_or_imprecise_dtypes=True)
                pool.iota(iota_b[:, :], [[1, P]], base=0, channel_multiplier=0, **kw).then_inc(s_iota, 1)
                pool.iota(node_of[:, :], [[P, NB]], base=0, channel_multiplier=1, **kw).then_inc(s_iota, 1)
                pool.iota(grid[:, :], [[1, GRID_C]], base=0, channel_multiplier=GRID_C, **kw).then_inc(s_iota, 1)
                pool.wait_ge(s_lane, 1)
                for b in range(NB):
                    pool.indirect_dma_start(
                        out=S["lane_d"][:, :], out_offset=bass.IndirectOffsetOnAxis(ap=pos_i[:, b:b + 1], axis=0),
                        in_=lane_w[:, b, :], in_offset=None).then_inc(s_scat, 16)

            @block.vector
            def _(dve):
                step = Chain(dve, s_v)
                dve.wait_ge(s_iota, 3)
                step(dve.memset(zrow[:, :], 0.0))
                step(dve.memset(zeros[:, :], 0.0))
                step(dve.tensor_scalar(part_i[:, :], S["dst_i"][:, :], P - 1, None, ALU.bitwise_and))
                step(dve.tensor_copy(dlo[:, :], part_i[:, :]))
                step(dve.tensor_scalar(part_i[:, :], S["dst_i"][:, :], 7, None, ALU.logical_shift_right))
                step(dve.tensor_copy(dhi[:, :], part_i[:, :]))
                step(dve.tensor_tensor(onehot_hi[:, :, :], bc(iota_b[0:EDGE_P, 0:NB], 1, [EDGE_P, EDGE_C, NB]),
                                       bc(dhi[:, :], 2, [EDGE_P, EDGE_C, NB]), ALU.is_equal))
                for c in range(PARTS):
                    if c >= 2:
                        dve.wait_ge(s_used, c - 1)
                    dve.tensor_tensor(onehot_lo[:, c % 2, :, :], bc(iota_b[0:EDGE_P, :], 1, [EDGE_P, PC, P]),
                                      bc(dlo[:, c * PC:(c + 1) * PC], 2, [EDGE_P, PC, P]),
                                      ALU.is_equal).then_inc(s_part, 1)
                dve.wait_ge(s_used, PARTS)
                step(dve.tensor_copy(deg[:, :], ph_[:, 0:NB]))
                dve.nop().then_inc(s_deg, 1)
                dve.wait_ge(s_pre, 1)
                starts(dve, step, start, tot, cum, zrow, ph_[:, 64:64 + NB], ph_[:, 128:128 + NB])
                for i, (st, dg) in enumerate(((start, deg), (S["start2"], S["deg2"]))):
                    step(dve.tensor_copy(i0[:, :], st[:, :]))
                    step(dve.tensor_scalar(i1[:, :], i0[:, :], 2, None, ALU.logical_shift_right))
                    step(dve.tensor_copy(q0[:, i, :], i1[:, :]))
                    step(dve.tensor_tensor(w0[:, :], st[:, :], dg[:, :], ALU.add))
                    step(dve.tensor_scalar(w0[:, :], w0[:, :], -1.0, 0.0, ALU.add, ALU.max))
                    step(dve.tensor_copy(i0[:, :], w0[:, :]))
                    step(dve.tensor_scalar(i1[:, :], i0[:, :], 2, None, ALU.logical_shift_right))
                    step(dve.tensor_copy(w1[:, :], i1[:, :]))
                    step(dve.tensor_tensor(nq[:, i, :], w1[:, :], q0[:, i, :], ALU.subtract))
                    step(dve.tensor_scalar(w0[:, :], dg[:, :], 0.0, None, ALU.is_gt))
                    step(dve.scalar_tensor_tensor(nq[:, i, :], nq[:, i, :], 1.0, w0[:, :], ALU.add, ALU.mult))
                step(dve.scalar_tensor_tensor(key[:, :], nq[:, 0, :], KEY_MAIN, nq[:, 1, :], ALU.mult, ALU.add))
                step(dve.tensor_scalar(key[:, :], key[:, :], float(KEY_CAP), float(KEY_STEP), ALU.min, ALU.mult))
                step(dve.tensor_tensor(key[:, :], key[:, :], node_of[:, :], ALU.subtract))
                step(dve.tensor_scalar(key[:, :], key[:, :], float(KEY_STEP - 1), None, ALU.add))
                dve.tensor_tensor(diag, bc(S["ident"][:, :], 1, [P, NB, P]),
                                  bc(key[:, :], 2, [P, NB, P]), ALU.mult).then_inc(s_diag, 1)
                dve.wait_ge(s_keyrow, 1)
                for b in range(NB):
                    step(dve.tensor_scalar(above, keyrow, key[:, b:b + 1], 0.0, ALU.is_gt, ALU.add,
                                           accum_out=pos[:, b:b + 1]))
                step(dve.tensor_copy(pos_i[:, :], pos[:, :]))
                for c, v in enumerate((node_of[:, :], start[:, :], deg[:, :], q0[:, 0, :], nq[:, 0, :],
                                       S["start2"][:, :], S["deg2"][:, :], q0[:, 1, :], nq[:, 1, :])):
                    step(dve.tensor_copy(lane_w[:, :, c], v))
                dve.nop().then_inc(s_lane, 1)
                dve.wait_ge(s_back, 16)
                step(dve.tensor_copy(lane_f[:, :, :], S["lane_i"][:, :, :]))
                step(dve.tensor_copy(S["deg_l"][:, :], lane_f[:, :, 2]))
                step(dve.memset(wide[:, :], 0.0))
                for i in range(2):
                    step(dve.tensor_copy(wide[:, 32 * i:32 * i + NB], lane_f[:, :, 4 + 4 * i]))
                dve.nop().then_inc(s_m, 1)
                dve.wait_ge(s_mt, 1)
                step(dve.tensor_reduce(mcol[:, :], ph_[0:64, 192:192 + P], AX.X, ALU.max))
                step(dve.tensor_scalar(mcol[:, :], mcol[:, :], 1.0, None, ALU.max))
                step(dve.tensor_scalar(mcols[:, :], S["ones"][0:64, :], mcol[:, 0:1], None, ALU.mult))
                dve.nop().then_inc(s_mr, 1)
                dve.wait_ge(s_md, 1)
                step(dve.tensor_copy(mrow[:, :], ph_[:, 384:448]))
                for i in range(2):
                    m, me, lq = mrow[:, 32 * i:32 * i + NB], mend[:, i, :], S[f"lane_q{i}"]
                    step(dve.tensor_tensor_scan(me, m, zrow[:, :], 0.0, ALU.add, ALU.add))
                    step(dve.tensor_tensor(w0[:, :], me, m, ALU.subtract))
                    first, begin, count = (lane_f[:, :, 4 * i + j] for j in (3, 1, 2))
                    step(dve.tensor_tensor(lq[:, :, 0], first, w0[:, :], ALU.subtract))
                    step(dve.tensor_copy(lq[:, :, 1], begin))
                    step(dve.tensor_tensor(lq[:, :, 2], begin, count, ALU.add))
                    step(dve.tensor_scalar(w1[:, 0:1], mend[:, i, NB - 1:NB], float(UNROLL - 1), None, ALU.add))
                    step(dve.tensor_copy(i0[:, 0:1], w1[:, 0:1]))
                    step(dve.tensor_scalar(S[f"turns{i}"][:, :], i0[:, 0:1], 2, None, ALU.logical_shift_right))
                    step(dve.memset(bid[:, :], 0.0))
                    for b in range(NB):
                        step(dve.scalar_tensor_tensor(bid[:, :], grid[:, :], mend[:, i, b:b + 1], bid[:, :], ALU.is_ge, ALU.add))
                    step(dve.tensor_scalar(bid[:, :], bid[:, :], float(NB - 1), None, ALU.min))
                    step(dve.tensor_copy(bid_i[:, i, :], bid[:, :]))
                    dve.nop().then_inc(s_bi, 1)

            @block.tensor
            def _(pe):
                pe.wait_ge(s_part, 1)
                pe.matmul(ph_[:, 0:NB], zeros[:, :], onehot_hi[:, 0, :], start=True, stop=False)
                for c in range(PARTS):
                    pe.wait_ge(s_part, c + 1)
                    with pe.Fori(0, PC // HERE) as t:
                        for u in range(HERE):
                            pe.matmul(ph_[:, 0:NB],
                                      onehot_lo[:, c % 2, bass.ds(t * HERE + u, 1), :].rearrange("p a f -> p (a f)"),
                                      onehot_hi[:, bass.ds(t * HERE + (c * PC + u), 1), :].rearrange("p a f -> p (a f)"),
                                      start=False, stop=False)
                    pe.matmul(ph_[:, 0:NB], zeros[:, :], onehot_hi[:, 0, :], start=False,
                              stop=(c == PARTS - 1)).then_inc(s_used, 1)
                pe.wait_ge(s_deg, 1)
                pe.matmul(ph_[:, 64:64 + NB], S["tri"][:, :], deg[:, :], start=True, stop=True)
                pe.matmul(ph_[:, 128:128 + NB], S["ones"][:, :], deg[:, :], start=True, stop=True).then_inc(s_pre, 1)
                pe.wait_ge(s_diag, 1)
                for b in range(NB):
                    last = pe.matmul(pk[:, b * P:(b + 1) * P], S["ones"][:, :], diag[:, b, :], start=True, stop=True)
                last.then_inc(s_key, 1)
                pe.wait_ge(s_m, 1)
                pe.transpose(ph_[0:64, 192:192 + P], wide[:, :], S["ident"][:, :]).then_inc(s_mt, 1)
                pe.wait_ge(s_mr, 1)
                pe.matmul(ph_[:, 384:448], mcols[:, :], S["ident"][0:64, 0:64], start=True, stop=True).then_inc(s_md, 1)

            @block.scalar
            def _(act):
                act.wait_ge(s_key, 1)
                act.activation(keyrow, pk[:, 0:NB * P], ACT.Copy).then_inc(s_keyrow, 1)
        ph.close()


def build_records(nc, S, A, i):
    with ExitStack() as ctx:
        ph = Phase(nc, ctx, f"rec{i}")
        GOT = (2 * QE, QE * SROW)[i]
        of = (A["edge_q"], S["sorted_d"].rearrange("(q e) f -> q (e f)", e=QE).bitcast(I32))[i]
        bids = ph.sb("bids", [1, UNROLL], I32)
        cols = ph.sb("cols", [P, UNROLL, 3])
        place = ph.sb("place", [P, UNROLL])
        slot = ph.sb("slot", [P, UNROLL, QE])
        quad = ph.sb("quad", [P, UNROLL])
        quad_c = ph.sb("quad_c", [P, UNROLL])
        quad_i = ph.sb("quad_i", [P, UNROLL], I32)
        edge = ph.sb("edge", [P, UNROLL, QE])
        valid = ph.sb("valid", [P, UNROLL, QE])
        below = ph.sb("below", [P, UNROLL, QE])
        got = ph.sb("got", [P, UNROLL, GOT], I32)
        src_f = ph.sb("src_f", [P, UNROLL, QE])
        rec = ph.sb("rec_w", [P, UNROLL, REC], I32)
        rec_f = rec[:, :, :].bitcast(F32)
        s_iota, s_bid, s_v, s_idx, s_got, s_rec, s_st = (ph.sem(n) for n in (
            "iota_done", "bids_loaded", "dve_step", "index_ready", "edges_gathered", "record_ready", "record_stored"))
        PRE = 1
        CH = 4 * 1 + 20

        with nc.Block() as block:
            @block.sync
            def _(sp):
                n = sp.value_load(S[f"turns{i}"][0:1, 0:1], min_val=1, max_val=NG_PAD // UNROLL)
                with sp.Fori(0, n) as t:
                    sp.wait_ge(s_rec, t + 1)
                    sp.dma_start(bids[:, :], S[f"bid_d{i}"][bass.ds(t * UNROLL, UNROLL)].rearrange("(a f) -> a f", a=1)).then_inc(s_bid, 16)
                    sp.wait_ge(s_rec, t + 2)
                    sp.dma_start(S[f"rec_d{i}"][bass.ds(t * UNROLL, UNROLL), :, :].rearrange("k p f -> p k f"),
                                 rec[:, :, :]).then_inc(s_st, 16)
                    sp.wait_ge(s_st, (t + 1) * 16)
                    sp.nop(nofuse=True)

            @block.gpsimd
            def _(pool):
                kw = dict(allow_small_or_imprecise_dtypes=True)
                pool.iota(place[:, :], [[1, UNROLL]], base=0, channel_multiplier=0, **kw).then_inc(s_iota, 1)
                pool.iota(slot[:, :, :], [[0, UNROLL], [1, QE]], base=0, channel_multiplier=0, **kw).then_inc(s_iota, 1)
                n = pool.value_load(S[f"turns{i}"][0:1, 0:1], min_val=1, max_val=NG_PAD // UNROLL)
                with pool.Fori(0, n) as t:
                    pool.wait_ge(s_idx, t + 1)
                    pool.nop(nofuse=True)
                    for k in range(UNROLL):
                        pool.indirect_dma_start(
                            out=got[:, k, :], out_offset=None, in_=of,
                            in_offset=bass.IndirectOffsetOnAxis(ap=quad_i[:, k:k + 1], axis=0)).then_inc(s_got, 16)

            @block.vector
            def _(dve):
                pre = Chain(dve, s_v)
                dve.wait_ge(s_iota, 2)
                pre(dve.memset(rec[:, :, :], 0))
                dve.nop().then_inc(s_rec, 1)
                n = dve.value_load(S[f"turns{i}"][0:1, 0:1], min_val=1, max_val=NG_PAD // UNROLL)
                with dve.Fori(0, n) as t:
                    step = Chain(dve, s_v, t * CH + PRE)
                    dve.wait_ge(s_bid, (t + 1) * 16)
                    dve.nop(nofuse=True)
                    bs = [dve.value_load(bids[0:1, k:k + 1], min_val=0, max_val=NB - 1) for k in range(UNROLL)]
                    for k in range(UNROLL):
                        step(dve.tensor_copy(cols[:, k, :], blk(S[f"lane_q{i}"], bs[k])))
                    step(dve.tensor_tensor(quad[:, :], place[:, :], cols[:, :, 0], ALU.add))
                    step(dve.tensor_scalar(quad_c[:, :], quad[:, :], float(NQ - 1), None, ALU.min))
                    step(dve.tensor_copy(quad_i[:, :], quad_c[:, :]))
                    dve.nop().then_inc(s_idx, 1)
                    step(dve.tensor_scalar(place[:, :], place[:, :], float(UNROLL), None, ALU.add))
                    step(dve.scalar_tensor_tensor(edge[:, :, :], bc(quad[:, :], 2, [P, UNROLL, QE]), float(QE),
                                                  slot[:, :, :], ALU.mult, ALU.add))
                    step(dve.tensor_tensor(valid[:, :, :], edge[:, :, :], bc(cols[:, :, 1], 2, [P, UNROLL, QE]), ALU.is_ge))
                    step(dve.tensor_tensor(below[:, :, :], edge[:, :, :], bc(cols[:, :, 2], 2, [P, UNROLL, QE]), ALU.is_lt))
                    step(dve.tensor_tensor(valid[:, :, :], valid[:, :, :], below[:, :, :], ALU.mult))
                    dve.wait_ge(s_st, t * 16)
                    step(dve.tensor_scalar(rec_f[:, :, R_MASK:R_MASK + QE], valid[:, :, :], BIG, -BIG, ALU.mult, ALU.add))
                    step(dve.tensor_copy(rec[:, :, R_QUAD], quad_i[:, :]))
                    step(dve.tensor_copy(rec[0:1, :, R_BLOCK], bids[0:1, :]))
                    dve.wait_ge(s_got, (t + 1) * 16 * UNROLL)
                    if i == 0:
                        step(dve.tensor_copy(rec_f[:, :, R_REL:R_REL + QE], got[:, :, QE:2 * QE]))
                    rows = got[:, :, 0:QE] if i == 0 else got[:, :, :].rearrange("p k (e f) -> p k e f", e=QE)[:, :, :, ED]
                    step(dve.tensor_copy(src_f[:, :, :], rows))
                    step(dve.scalar_tensor_tensor(src_f[:, :, :], src_f[:, :, :], float(-DUMMY), valid[:, :, :], ALU.add, ALU.mult))
                    step(dve.tensor_scalar(src_f[:, :, :], src_f[:, :, :], float(DUMMY), None, ALU.add))
                    step(dve.tensor_copy(rec[:, :, R_SRC:R_SRC + QE], src_f[:, :, :]))
                    while step.n < CH:
                        step(dve.nop())
                    assert step.n == CH, step.n
                    dve.nop().then_inc(s_rec, 1)
        ph.close()


def shared(nc, ctx):
    S = {}

    def sb(name, shape, dt=F32):
        S[name] = ctx.enter_context(nc.sbuf_tensor(name, shape, dt))

    def dram(name, shape, dt=F32):
        S[name] = nc.dram_tensor(name, shape, dt).ap()

    sb("state", [P, 6 * NB * D])
    part = lambda a, b: S["state"][:, a * NB * D:b * NB * D].rearrange("p (b f) -> p b f", b=NB)
    S["X"] = part(0, 1)
    S["H"] = part(1, 2)
    S["big"] = part(2, 4)
    S["big2"] = part(4, 6)
    sb("iota_c", [P, P])
    sb("iota_p", [P, 1])
    sb("ident", [P, P])
    sb("ones", [P, P])
    sb("tri", [P, P])
    sb("src_i", [EDGE_P, EDGE_C], I32)
    sb("dst_i", [EDGE_P, EDGE_C], I32)
    sb("place_i", [EDGE_P, EDGE_C], I32)
    sb("deg2", [P, NB])
    sb("start2", [P, NB])
    sb("lane_i", [P, NB, LANE], I32)
    sb("deg_l", [P, NB])
    for i in range(2):
        sb(f"lane_q{i}", [P, NB, 3])
        sb(f"turns{i}", [P, 1], I32)
    sb("adst", [P, NB])
    sb("m", [P, NB, 8])
    sb("l", [P, NB, 8])
    dram("lane_d", [NL, LANE], I32)
    dram("sorted_d", [NQ * QE, SROW])
    for i in range(2):
        dram(f"bid_d{i}", [NG_PAD], I32)
        dram(f"rec_d{i}", [NG_PAD, P, REC], I32)
    dram("tab0", [NL + 1, D2])
    dram("tab1", [NL + 1, D2])
    dram("tab2", [NL + 1, D2])
    dram("tab3", [NL + 1, XROW])
    return S


def hold(eng, sem, value):
    eng.wait_ge(sem, value)
    eng.nop(nofuse=True)


def rows_of(ap, n):
    return ap.rearrange("(a n) -> a n", a=1).broadcast_to([P, n])


def all_heads(ap, heads):
    return ap.rearrange("p b (h d) -> p b h d", h=heads)


def norm_begin(dve, step, src, dst, stat, wide):
    step(dve.tensor_reduce(stat[:, 0, :], src, AX.X, ALU.add))
    step(dve.tensor_scalar(stat[:, 0, :], stat[:, 0, :], 1.0 / D, None, ALU.mult))
    step(dve.tensor_tensor(dst, src, bc(stat[:, 0, :], 2, [P, NB, D]), ALU.subtract))
    step(dve.tensor_tensor(wide, dst, dst, ALU.mult))
    step(dve.tensor_reduce(stat[:, 1, :], wide, AX.X, ALU.add))
    step(dve.tensor_scalar(stat[:, 1, :], stat[:, 1, :], 1.0 / D, EPS, ALU.mult, ALU.add))


def norm_end(dve, step, dst, stat):
    step(dve.reciprocal(stat[:, 3, :], stat[:, 2, :]))
    step(dve.tensor_tensor(dst, dst, bc(stat[:, 3, :], 2, [P, NB, D]), ALU.mult))


def layer_input(dve, step, S, stat, wide, s_var, s_root, n):
    norm_begin(dve, step, S["X"][:, :, :], S["H"][:, :, :], stat, wide)
    dve.nop().then_inc(s_var, 1)
    dve.wait_ge(s_root, n)
    norm_end(dve, step, S["H"][:, :, :], stat)
    step(dve.tensor_scalar(S["H"][:, :, :], S["H"][:, :, :], 0.0, None, ALU.max))


def take_root(act, stat, s_var, s_root, n):
    act.wait_ge(s_var, n)
    act.activation(stat[:, 2, :], stat[:, 1, :], ACT.Sqrt).then_inc(s_root, 1)


def fetch_nodes(nc, S, A):
    with ExitStack() as ctx:
        ph = Phase(nc, ctx, "fetch")
        row = ph.sb("row", [P, NB], I32)
        row_f = ph.sb("row_f", [P, NB])
        s_row, s_x, s_v = (ph.sem(n) for n in ("rows_ready", "x_loaded", "dve_step"))
        with nc.Block() as block:
            @block.vector
            def _(dve):
                step = Chain(dve, s_v)
                step(dve.tensor_copy(row_f[:, :], S["lane_i"][:, :, 0]))
                step(dve.tensor_scalar(row_f[:, :], row_f[:, :], float(N_NODES - 1), None, ALU.min))
                dve.tensor_copy(row[:, :], row_f[:, :]).then_inc(s_row, 1)

            @block.gpsimd
            def _(pool):
                pool.wait_ge(s_row, 1)
                for b in range(NB):
                    pool.indirect_dma_start(out=S["X"][:, b, :], out_offset=None, in_=A["x"][:, :],
                                            in_offset=bass.IndirectOffsetOnAxis(ap=row[:, b:b + 1], axis=0)).then_inc(s_x, 16)
                pool.wait_ge(s_x, 16 * NB)
        ph.close()


def make_tables(nc, S, A, layer):
    heads = (1, 4, 8, 1)[layer]
    gat = layer == 3
    L = ("L0_gnn_", "L1_gnn_", "L2_gnn_", "L3_gnn_")[layer]
    NA = D if gat else D2
    NO = {0: D2, 1: D, 2: D, 3: 0}[layer]
    ROW = XROW if gat else D2
    tab = S[f"tab{layer}"]
    scale = {0: 1.0, 1: 64 ** -0.5, 2: 32 ** -0.5, 3: 1.0}[layer]
    with ExitStack() as ctx:
        ph = Phase(nc, ctx, f"make{layer}")
        stat = ph.sb("stat", [P, 4, NB])
        wide = S["big2"][:, :, 0:D]
        hst = ph.sb("hst", [P, D])
        hT = ph.sb("hT", [P, 2, P])
        w_row = ph.sb("w_row", [P, 2, NA])
        b_row = ph.sb("b_row", [P, NA])
        w_own = ph.sb("w_own", [P, 2, max(NO, 1)])
        b_own = ph.sb("b_own", [P, max(NO, 1)])
        row = ph.sb("row", [P, ROW])
        prod = ph.sb("prod", [P, D])
        idx = ph.sb("idx", [P, 1], I32)
        empty = ph.sb("empty", [P, NB])
        last_row = ph.sb("last_row", [1, ROW])
        qe = ph.sb("qe", [P, 2])
        att = ph.sb("att", [P, 2, D])
        term = ph.sb("term", [P, 3])
        w_nat = ph.sb("w_nat", [P, 2, D])
        psT = ph.ps("psT", [P, 512])
        psA = ph.ps("psA", [P, 512])
        psB = ph.ps("psB", [P, 512])
        psW = ph.ps("psW", [P, 512])
        s_w, s_v, s_var, s_root, s_wr, s_h, s_hst, s_T, s_hT, s_A, s_B, s_row, s_own, s_scat, s_dummy, s_wT, s_lr = (
            ph.sem(n) for n in ("weights_loaded", "dve_step", "var_ready", "root_ready", "weights_ready",
                                "h_ready", "h_staged", "h_turned", "hT_ready", "row_sums", "own_sums",
                                "row_ready", "own_ready", "row_stored", "dummy_stored", "w_turned", "dummy_ready"))
        n_loads = {0: 3, 1: 7, 2: 6, 3: 3}[layer]
        keeps = 3 * gat
        IN_LOOP = {0: 0, 1: 1, 2: 1, 3: 8}[layer]

        with nc.Block() as block:
            @block.sync
            def _(sp):
                def load(to, of):
                    sp.dma_start(to, of, allow_slow_non_contiguous=True).then_inc(s_w, 16)
                chunks = lambda ap: ap.rearrange("(c p) n -> p c n", p=P)
                if layer == 0:
                    w = chunks(A[L + "eW1"][0:2 * D, :])
                    load(w_row[:, :, :], w[:, 0:2, :])
                    load(w_own[:, :, :], w[:, 2:4, :])
                    load(b_own[:, :], rows_of(A[L + "eb1"], D2))
                elif not gat:
                    load(w_row[:, :, 0:D], chunks(A[L + "Wk"]))
                    load(w_row[:, :, D:D2], chunks(A[L + "Wv"]))
                    load(w_own[:, :, :], chunks(A[L + "Wq"]))
                    load(b_row[:, 0:D], rows_of(A[L + "bk"], D))
                    load(b_row[:, D:D2], rows_of(A[L + "bv"], D))
                    load(b_own[:, :], rows_of(A[L + "bq"], D))
                    if layer == 1:
                        load(qe[:, :], A[L + "query_emb"].rearrange("(c p) -> p c", p=P))
                    if layer == 2:
                        load(prod[:, :], rows_of(A[L + "be"], D))
                else:
                    load(w_nat[:, :, :], chunks(A[L + "W"]))
                    load(att[:, 0, :], rows_of(A[L + "att_src"], D))
                    load(att[:, 1, :], rows_of(A[L + "att_dst"], D))
                sp.wait_ge(s_lr, 1)
                sp.dma_start(tab[DUMMY:DUMMY + 1, :], last_row[:, :]).then_inc(s_dummy, 16)
                sp.wait_ge(s_dummy, 16)

            @block.gpsimd
            def _(pool):
                pool.memset(last_row[:, :], LOW if layer == 0 else 0.0).then_inc(s_lr, 1)
                with pool.Fori(0, NB) as b:
                    hold(pool, s_row, b + 2)
                    pool.indirect_dma_start(out=tab[:, :], out_offset=bass.IndirectOffsetOnAxis(ap=idx[:, 0:1], axis=0),
                                            in_=row[:, :], in_offset=None).then_inc(s_scat, 16)
                pool.wait_ge(s_scat, 16 * NB)

            @block.scalar
            def _(act):
                take_root(act, stat, s_var, s_root, 1)
                act.wait_ge(s_h, 1)
                if layer == 1:
                    act.wait_ge(s_wr, 1)
                with act.Fori(0, NB) as b:
                    act.activation(hst[:, :], blk(S["H"], b), ACT.Copy).then_inc(s_hst, 1)
                    act.wait_ge(s_T, b + 1)
                    act.wait_ge(s_own, b + 1)
                    if layer == 1:
                        act.activation(hT[:, 0, :], psT[:, 0:P], ACT.Identity, bias=qe[:, 0:1])
                        act.activation(hT[:, 1, :], psT[:, P:D], ACT.Identity, bias=qe[:, 1:2]).then_inc(s_hT, 1)
                    else:
                        act.activation(hT[:, :, :], psT[:, 0:D].rearrange("p (c n) -> p c n", c=2), ACT.Copy).then_inc(s_hT, 1)

            @block.tensor
            def _(pe):
                pe.wait_ge(s_wr, 1)
                if gat:
                    for c in range(2):
                        for k in range(2):
                            last = pe.transpose(psW[:, (2 * k + c) * P:(2 * k + c + 1) * P], w_nat[:, c, k * P:(k + 1) * P], S["ident"][:, :])
                    last.then_inc(s_wT, 1)
                    pe.wait_ge(s_h, 1)
                with pe.Fori(0, NB) as b:
                    pe.wait_ge(s_hst, b + 1)
                    pe.transpose(psT[:, 0:P], hst[:, 0:P], S["ident"][:, :])
                    pe.transpose(psT[:, P:D], hst[:, P:D], S["ident"][:, :]).then_inc(s_T, 1)
                    pe.wait_ge(s_hT, b + 1)
                    pe.wait_ge(s_row, b + 1)
                    pe.matmul(psA[:, 0:NA], hT[:, 0, :], w_row[:, 0, :], start=True, stop=False)
                    pe.matmul(psA[:, 0:NA], hT[:, 1, :], w_row[:, 1, :], start=False, stop=True).then_inc(s_A, 1)
                    if NO:
                        pe.wait_ge(s_own, b + 1)
                        pe.matmul(psB[:, 0:NO], hT[:, 0, :], w_own[:, 0, :], start=True, stop=False)
                        pe.matmul(psB[:, 0:NO], hT[:, 1, :], w_own[:, 1, :], start=False, stop=True).then_inc(s_B, 1)

            @block.vector
            def _(dve):
                step = Chain(dve, s_v)
                dve.wait_ge(s_w, 16 * n_loads + 16 * (layer == 2))
                if not gat and layer:
                    step(dve.tensor_scalar(w_own[:, :, :], w_own[:, :, :], scale, None, ALU.mult))
                    step(dve.tensor_scalar(b_own[:, :], b_own[:, :], scale, None, ALU.mult))
                if layer == 1:
                    step(dve.tensor_scalar(qe[:, :], qe[:, :], 0.1, None, ALU.mult))
                if layer == 2:
                    step(dve.tensor_tensor(b_row[:, 0:D], b_row[:, 0:D], prod[:, :], ALU.add))
                dve.nop().then_inc(s_wr, 1)
                if gat:
                    dve.wait_ge(s_wT, 1)
                    step(dve.tensor_copy(w_row[:, :, :], psW[:, :].rearrange("p (k n) -> p k n", k=2)))
                    step(dve.memset(row[:, :], 0.0))
                step(dve.tensor_scalar(empty[:, :], S["deg_l"][:, :], 0.0, None, ALU.is_equal))
                layer_input(dve, step, S, stat, wide, s_var, s_root, 1)
                if layer == 0:
                    step(dve.memset(S["big"][:, :, :], 0.0))
                if layer in (1, 2):
                    step(dve.memset(S["m"][:, :, :], LOW))
                    step(dve.memset(S["l"][:, :, :], 0.0))
                if layer == 2:
                    step(dve.memset(S["big"][:, :, D:D2], 0.0))
                if layer == 1:
                    step(dve.tensor_copy(S["l"][:, :, 0:heads], bc(empty[:, :], 2, [P, NB, heads])))
                if gat:
                    step(dve.memset(S["l"][:, :, :], 1.0))
                dve.nop().then_inc(s_h, 1)
                dve.nop().then_inc(s_row, 1)
                dve.nop().then_inc(s_own, 1)
                before = step.n
                with dve.Fori(0, NB) as b:
                    step = Chain(dve, s_v, b * IN_LOOP + before)
                    hold(dve, s_scat, b * 16)
                    dve.tensor_copy(idx[:, :], S["lane_i"][:, bass.ds(b, 1), 0])
                    dve.wait_ge(s_A, b + 1)
                    if layer == 0:
                        dve.tensor_copy(row[:, :], psA[:, :]).then_inc(s_row, 1)
                    elif not gat:
                        if layer == 1:
                            step(dve.tensor_tensor(row[:, :], psA[:, :], b_row[:, :], ALU.add))
                            dve.tensor_scalar(blk(S["big"], b)[:, D:D2], row[:, D:D2], empty[:, bass.ds(b, 1)], None, ALU.mult).then_inc(s_row, 1)
                        else:
                            dve.tensor_tensor(row[:, :], psA[:, :], b_row[:, :], ALU.add).then_inc(s_row, 1)
                            step(dve.nop())
                    else:
                        step(dve.tensor_copy(row[:, 0:D], psA[:, 0:D]))
                        step(dve.tensor_tensor(prod[:, :], row[:, 0:D], att[:, 0, :], ALU.mult))
                        step(dve.tensor_reduce(term[:, 0:1], prod[:, :], AX.X, ALU.add))
                        step(dve.tensor_tensor(prod[:, :], row[:, 0:D], att[:, 1, :], ALU.mult))
                        step(dve.tensor_reduce(term[:, 1:2], prod[:, :], AX.X, ALU.add))
                        step(dve.tensor_copy(S["adst"][:, bass.ds(b, 1)], term[:, 1:2]))
                        step(dve.tensor_tensor(term[:, 2:3], term[:, 0:1], term[:, 1:2], ALU.add))
                        step(dve.scalar_tensor_tensor(S["m"][:, bass.ds(b, 1), 0], term[:, 2:3], 0.2, term[:, 2:3], ALU.mult, ALU.max))
                        dve.tensor_copy(blk(S["big"], b)[:, D:D2], row[:, 0:D])
                        dve.tensor_copy(row[:, D:D + 1], term[:, 0:1]).then_inc(s_row, 1)
                        dve.wait_ge(s_row, b + 2)
                        dve.nop().then_inc(s_own, 1)
                    if NO:
                        hold(dve, s_B, b + 1)
                        own = blk(S["big2"], b)[:, 0:D2] if layer == 0 else blk(S["big"], b)[:, 0:D]
                        dve.tensor_tensor(own, psB[:, 0:NO], b_own[:, 0:NO], ALU.add).then_inc(s_own, 1)
                    assert step.n == IN_LOOP, step.n
        ph.close()


def edge_mlp(nc, S, A):
    with ExitStack() as ctx:
        ph = Phase(nc, ctx, "edge0")
        rec = ph.sb("rec", [P, UNROLL, REC], I32)
        feat = ph.sb("feat", [P, UNROLL, QE * ED])
        featT = ph.sb("featT", [P, 2, 2, P])
        ring = ph.sb("ring", [P, UNROLL, QE, D2])
        w_edge = ph.sb("w_edge", [P, D2])
        psT = [ph.ps(f"psT{i}", [P, 512]) for i in range(2)]
        psX = ph.ps("psX", [P, QE, D2])
        s_rec, s_done, s_feat = ([ph.sem(f"{n}{k}") for k in range(UNROLL)] for n in ("rec_loaded", "quad_done", "feat_loaded"))
        s_g = [[ph.sem(f"rows{k}_{h}") for h in range(2)] for k in range(UNROLL)]
        s_w, s_v, s_T, s_fT, s_x, s_xr = (ph.sem(n) for n in (
            "weights_loaded", "dve_step", "feat_turned", "featT_ready", "sums_ready", "sums_read"))
        turns = lambda eng: eng.value_load(S["turns0"][0:1, 0:1], min_val=1, max_val=NG_PAD // UNROLL)
        CH = UNROLL * QE

        with nc.Block() as block:
            @block.sync
            def _(sp):
                for h in range(2):
                    sp.dma_start(w_edge[h * ED:(h + 1) * ED, :], A["L0_gnn_eW1"][2 * D:2 * D + ED, :]).then_inc(s_w, 16)
                n = turns(sp)
                with sp.Fori(0, n) as t:
                    for k in range(UNROLL):
                        sp.wait_ge(s_done[k], t + 1)
                        sp.dma_start(rec[:, k, :], S["rec_d0"][bass.ds(t * UNROLL + k, 1), :, :].rearrange("a p f -> p (a f)")).then_inc(s_rec[k], 16)

            @block.gpsimd
            def _(pool):
                n = turns(pool)
                with pool.Fori(0, n) as t:
                    for k in range(UNROLL):
                        hold(pool, s_rec[k], (t + 1) * 16)
                        pool.indirect_dma_start(out=feat[:, k, :], out_offset=None, in_=A["feat_q"][:, :],
                                                in_offset=bass.IndirectOffsetOnAxis(ap=rec[:, k, R_QUAD:R_QUAD + 1], axis=0)).then_inc(s_feat[k], 16)
                        for s in range(QE):
                            pool.indirect_dma_start(out=ring[:, k, s, :], out_offset=None, in_=S["tab0"][:, :],
                                                    in_offset=bass.IndirectOffsetOnAxis(ap=rec[:, k, R_SRC + s:R_SRC + s + 1], axis=0)).then_inc(s_g[k][s // 2], 16)

            @block.scalar
            def _(act):
                act.nop().then_inc(s_fT, 1)
                n = turns(act)
                with act.Fori(0, n) as t:
                    for k in range(UNROLL):
                        act.wait_ge(s_T, t * UNROLL + (k + 1))
                        act.activation(featT[:, k % 2, :, :], psT[k % 2][:, 0:2 * P].rearrange("p (c n) -> p c n", c=2), ACT.Copy).then_inc(s_fT, 1)

            @block.tensor
            def _(pe):
                pe.wait_ge(s_w, 32)
                n = turns(pe)
                with pe.Fori(0, n) as t:
                    for k in range(UNROLL):
                        hold(pe, s_rec[k], (t + 1) * 16)
                        b = pe.value_load(rec[0:1, k, R_BLOCK:R_BLOCK + 1], min_val=0, max_val=NB - 1)
                        pe.wait_ge(s_feat[k], (t + 1) * 16)
                        pe.wait_ge(s_fT, t * UNROLL + (k + 1))
                        pe.transpose(psT[k % 2][:, 0:P], feat[:, k, 0:P], S["ident"][:, :])
                        pe.transpose(psT[k % 2][:, P:2 * P], feat[:, k, P:2 * P], S["ident"][:, :]).then_inc(s_T, 1)
                        pe.wait_ge(s_fT, t * UNROLL + (k + 2))
                        for s in range(QE):
                            if s % 2 == 0:
                                pe.wait_ge(s_xr, t * (2 * UNROLL) + (2 * k + s // 2 + 1))
                            lo = ED * (s % 2)
                            pe.matmul(psX[:, s, :], featT[lo:lo + ED, k % 2, s // 2, :], w_edge[lo:lo + ED, :], start=True, stop=False)
                            last = pe.matmul(psX[:, s, :], S["ident"][:, :], blk(S["big2"], b), start=False, stop=True)
                            if s % 2:
                                last.then_inc(s_x, 1)

            @block.vector
            def _(dve):
                dve.nop().then_inc(s_xr, 2)
                for k in range(UNROLL):
                    dve.nop().then_inc(s_done[k], 1)
                n = turns(dve)
                with dve.Fori(0, n) as t:
                    step = Chain(dve, s_v, t * CH)
                    for k in range(UNROLL):
                        hold(dve, s_rec[k], (t + 1) * 16)
                        b = dve.value_load(rec[0:1, k, R_BLOCK:R_BLOCK + 1], min_val=0, max_val=NB - 1)
                        for h in range(2):
                            dve.wait_ge(s_g[k][h], (t + 1) * 32)
                            dve.wait_ge(s_x, t * (2 * UNROLL) + (2 * k + h + 1))
                            both = ring[:, k, 2 * h:2 * h + 2, :]
                            dve.tensor_tensor(both, psX[:, 2 * h:2 * h + 2, :], both, ALU.add).then_inc(s_xr, 1)
                            dve.wait_ge(s_xr, t * (2 * UNROLL) + (2 * k + h + 3))
                            for s in (2 * h, 2 * h + 1):
                                step(dve.scalar_tensor_tensor(blk(S["big"], b), ring[:, k, s, :], 0.0, blk(S["big"], b), ALU.max, ALU.add))
                        dve.nop().then_inc(s_done[k], 1)
        ph.close()


def laid_out(inputs):
    a = {n: np.ascontiguousarray(v) for n, v in inputs.items()}
    pad = NQ * QE - N_EDGES
    src, rel, feat = a["src"], a.pop("edge_type_64"), a["edge_attr_64"]
    quads = lambda v: np.concatenate([v, np.zeros((pad,) + v.shape[1:], v.dtype)]).reshape(NQ, -1)
    a["edge_q"] = np.concatenate([quads(src), quads(rel)], axis=1)
    a["feat_q"] = quads(feat)
    return a


def update_nodes(nc, S, A):
    L = "L0_gnn_"
    with ExitStack() as ctx:
        ph = Phase(nc, ctx, "update")
        stat = ph.sb("stat", [P, 4, NB])
        wide = S["big2"][:, :, D:D2]
        Y = S["big2"][:, :, 0:D]
        sums = ph.sb("sums", [P, D2])
        hst = ph.sb("hst", [P, D])
        sumsT = ph.sb("sumsT", [P, 4, P])
        inT = ph.sb("inT", [P, 4, P])
        upT = ph.sb("upT", [P, 4, P])
        eW2 = ph.sb("eW2", [P, 4, D])
        nW1 = ph.sb("nW1", [P, 4, D2])
        nW2 = ph.sb("nW2", [P, 4, D])
        eb2 = ph.sb("eb2", [1, D])
        nb1 = ph.sb("nb1", [P, 4])
        rows = ph.sb("rows", [P, 3, D])
        deg_i = ph.sb("deg_i", [1, NL], I32)
        deg_row = S["big2"][0:1, :, D:D + P]
        psR, psH, psM, psU, psY = (ph.ps(n, [P, 512]) for n in ("psR", "psH", "psM", "psU", "psY"))
        s_w, s_v, s_var, s_root, s_deg, s_st, s_T, s_sT, s_M, s_mT, s_U, s_uT, s_Y, s_y = (
            ph.sem(n) for n in ("weights_loaded", "dve_step", "var_ready", "root_ready", "deg_ready",
                                "staged", "turned", "turned_copied", "agg_sums", "agg_copied", "up_sums",
                                "up_ready", "down_sums", "y_ready"))
        with nc.Block() as block:
            @block.sync
            def _(sp):
                chunks = lambda ap: ap.rearrange("(c p) n -> p c n", p=P)
                for to, of in ((eW2[:, :, :], chunks(A[L + "eW2"])), (nW1[:, :, :], chunks(A[L + "nW1"])),
                               (nW2[:, :, :], chunks(A[L + "nW2"])), (eb2[:, :], A[L + "eb2"].rearrange("(a n) -> a n", a=1)),
                               (nb1[:, :], A[L + "nb1"].rearrange("(c p) -> p c", p=P)),
                               (rows[:, 0, :], rows_of(A[L + "nb2"], D)), (rows[:, 1, :], rows_of(A[L + "ln_gamma"], D)),
                               (rows[:, 2, :], rows_of(A[L + "ln_beta"], D)),
                               (deg_i[:, :], S["lane_d"][:, 2].rearrange("(a n) -> a n", a=1))):
                    sp.dma_start(to, of, allow_slow_non_contiguous=True).then_inc(s_w, 16)

            @block.scalar
            def _(act):
                act.wait_ge(s_w, 16 * 9)
                with act.Fori(0, NB) as b:
                    act.activation(sums[:, :], blk(S["big"], b), ACT.Copy)
                    act.activation(hst[:, :], blk(S["H"], b), ACT.Copy).then_inc(s_st, 1)
                    act.wait_ge(s_T, b + 1)
                    act.activation(sumsT[:, :, :], psR[:, :].rearrange("p (c n) -> p c n", c=4), ACT.Copy)
                    act.activation(inT[:, 0:2, :], psH[:, 0:D].rearrange("p (c n) -> p c n", c=2), ACT.Copy).then_inc(s_sT, 1)
                    act.wait_ge(s_M, b + 1)
                    act.activation(inT[:, 2:4, :], psM[:, 0:D].rearrange("p (c n) -> p c n", c=2), ACT.Copy).then_inc(s_mT, 1)
                    act.wait_ge(s_U, b + 1)
                    for c in range(4):
                        last = act.activation(upT[:, c, :], psU[:, c * P:(c + 1) * P], ACT.Relu, bias=nb1[:, c:c + 1])
                    last.then_inc(s_uT, 1)
                take_root(act, stat, s_var, s_root, 1)

            @block.tensor
            def _(pe):
                pe.wait_ge(s_w, 16 * 9)
                pe.wait_ge(s_deg, 1)
                with pe.Fori(0, NB) as b:
                    pe.wait_ge(s_st, b + 1)
                    for c in range(4):
                        pe.transpose(psR[:, c * P:(c + 1) * P], sums[:, c * P:(c + 1) * P], S["ident"][:, :])
                    for c in range(2):
                        last = pe.transpose(psH[:, c * P:(c + 1) * P], hst[:, c * P:(c + 1) * P], S["ident"][:, :])
                    last.then_inc(s_T, 1)
                    pe.wait_ge(s_sT, b + 1)
                    for f in range(2):
                        to = psM[:, f * P:(f + 1) * P]
                        for c in range(4):
                            pe.matmul(to, eW2[:, c, f * P:(f + 1) * P], sumsT[:, c, :], start=(c == 0), stop=False)
                        last = pe.matmul(to, eb2[0:1, f * P:(f + 1) * P], blk(deg_row, b), start=False, stop=True)
                    last.then_inc(s_M, 1)
                    pe.wait_ge(s_mT, b + 1)
                    for f in range(4):
                        for c in range(4):
                            last = pe.matmul(psU[:, f * P:(f + 1) * P], nW1[:, c, f * P:(f + 1) * P], inT[:, c, :], start=(c == 0), stop=(c == 3))
                    last.then_inc(s_U, 1)
                    pe.wait_ge(s_uT, b + 1)
                    pe.wait_ge(s_y, b + 1)
                    for c in range(4):
                        last = pe.matmul(psY[:, 0:D], upT[:, c, :], nW2[:, c, :], start=(c == 0), stop=(c == 3))
                    last.then_inc(s_Y, 1)

            @block.vector
            def _(dve):
                step = Chain(dve, s_v)
                dve.wait_ge(s_w, 16 * 9)
                step(dve.tensor_copy(deg_row, deg_i[:, :].rearrange("a (b n) -> a b n", n=P)))
                dve.nop().then_inc(s_deg, 1)
                dve.nop().then_inc(s_y, 1)
                with dve.Fori(0, NB) as b:
                    dve.wait_ge(s_Y, b + 1)
                    dve.tensor_tensor(blk(Y, b), psY[:, 0:D], blk(S["H"], b), ALU.add).then_inc(s_y, 1)
                dve.wait_ge(s_y, NB + 1)
                row = lambda i: bc(rows[:, i, :], 1, [P, NB, D])
                step(dve.tensor_tensor(Y, Y, row(0), ALU.add))
                finish_layer(dve, step, S, Y, wide, stat, s_var, s_root, row(1), row(2))
        ph.close()


def finish_layer(dve, step, S, Y, wide, stat, s_var, s_root, gamma, beta):
    norm_begin(dve, step, Y, Y, stat, wide)
    dve.nop().then_inc(s_var, 1)
    dve.wait_ge(s_root, 1)
    norm_end(dve, step, Y, stat)
    step(dve.tensor_tensor(Y, Y, gamma, ALU.mult))
    step(dve.tensor_tensor(S["X"][:, :, :], S["X"][:, :, :], beta, ALU.add))
    step(dve.tensor_tensor(S["X"][:, :, :], S["X"][:, :, :], Y, ALU.add))


def attend(nc, S, A, layer):
    heads = (None, 4, 8)[layer]
    hd = D // heads
    ROWS = QE + 1
    with ExitStack() as ctx:
        ph = Phase(nc, ctx, f"edge{layer}")
        rec = ph.sb("rec", [P, UNROLL, REC], I32)
        FW = (None, ED, SROW)[layer]
        feat = ph.sb("feat", [P, UNROLL, QE, FW])
        PAIR = (None, 2, 1)[layer]
        TP = PAIR * ED
        featT = ph.sb("featT", [TP, 2, QE // PAIR, P])
        ring = ph.sb("ring", [P, UNROLL, QE, D2])
        w_edge = ph.sb("w_edge", [P, D])
        prod = ph.sb("prod", [P, QE, D])
        cat = ph.sb("cat", [P, ROWS, heads])
        wgt = ph.sb("wgt", [P, ROWS, heads])
        tot = ph.sb("tot", [P, heads])
        psT = [ph.ps(f"psT{i}", [P, 512]) for i in range(2)]
        psX = ph.ps("psX", [P, QE, D2])
        psV = ph.ps("psV", [P, 512])
        s_rec, s_done, s_feat, s_g = ([ph.sem(f"{n}{k}") for k in range(UNROLL)] for n in (
            "rec_loaded", "quad_done", "feat_ready", "rows_loaded"))
        s_w, s_v, s_T, s_fT, s_x, s_xr, s_cat, s_exp, s_wv, s_pv, s_wr, s_iota = (ph.sem(n) for n in (
            "weights_loaded", "dve_step", "feat_turned", "featT_ready", "keys_ready", "keys_read",
            "scores_ready", "weights_ready", "values_weighted", "values_summed", "w_edge_ready", "ring_cleared"))
        turns = lambda eng: eng.value_load(S[f"turns{layer - 1}"][0:1, 0:1], min_val=1, max_val=NG_PAD // UNROLL)
        CH = 12 * UNROLL
        FEAT_INC = 1 if layer == 1 else 16
        PRE = 3 + (layer == 1)

        with nc.Block() as block:
            @block.sync
            def _(sp):
                for h in range(2):
                    if layer == 2:
                        sp.dma_start(w_edge[h * ED:(h + 1) * ED, :], A["L2_gnn_We"][:, :]).then_inc(s_w, 16)
                    else:
                        for i in range(heads):
                            sp.dma_start(w_edge[h * ED:(h + 1) * ED, i * hd:(i + 1) * hd], A["L1_gnn_rel_w"][:, :]).then_inc(s_w, 16)
                n = turns(sp)
                with sp.Fori(0, n) as t:
                    for k in range(UNROLL):
                        sp.wait_ge(s_done[k], t + 1)
                        sp.dma_start(rec[:, k, :], S[f"rec_d{layer - 1}"][bass.ds(t * UNROLL + k, 1), :, :].rearrange("a p f -> p (a f)")).then_inc(s_rec[k], 16)

            @block.gpsimd
            def _(pool):
                n = turns(pool)
                with pool.Fori(0, n) as t:
                    for k in range(UNROLL):
                        hold(pool, s_rec[k], (t + 1) * 16)
                        if layer == 2:
                            pool.indirect_dma_start(out=feat[:, k, :, :].rearrange("p s f -> p (s f)"), out_offset=None,
                                                    in_=S["sorted_d"].rearrange("(q e) f -> q (e f)", e=QE),
                                                    in_offset=bass.IndirectOffsetOnAxis(ap=rec[:, k, R_QUAD:R_QUAD + 1], axis=0)).then_inc(s_feat[k], 16)
                        else:
                            for s in range(QE):
                                last = pool.tensor_scalar(feat[:, k, s, :], S["iota_c"][:, 0:ED], rec[:, k, R_REL + s:R_REL + s + 1].bitcast(F32), None, ALU.is_equal)
                            last.then_inc(s_feat[k], 1)
                        for s in range(QE):
                            pool.indirect_dma_start(out=ring[:, k, s, :], out_offset=None, in_=S[f"tab{layer}"][:, :],
                                                    in_offset=bass.IndirectOffsetOnAxis(ap=rec[:, k, R_SRC + s:R_SRC + s + 1], axis=0)).then_inc(s_g[k], 16)

            @block.scalar
            def _(act):
                act.nop().then_inc(s_fT, 1)
                n = turns(act)
                with act.Fori(0, n) as t:
                    for k in range(UNROLL):
                        act.wait_ge(s_T, t * UNROLL + (k + 1))
                        act.activation(featT[:, k % 2, :, :], psT[k % 2][0:TP, 0:QE // PAIR * P].rearrange("p (c n) -> p c n", n=P), ACT.Copy).then_inc(s_fT, 1)
                        act.wait_ge(s_cat, t * UNROLL + (k + 1))
                        act.activation(wgt[:, :, :], cat[:, :, :], ACT.Exp).then_inc(s_exp, 1)

            @block.tensor
            def _(pe):
                def sum_values(k, t, prev):
                    pe.wait_ge(s_wv, t * UNROLL + (k + 1))
                    before = (prev - 1) % UNROLL
                    pe.wait_ge(s_done[before], t + (2 if k >= 2 else 1))
                    for s in range(QE):
                        last = pe.matmul(psV[:, 0:D], S["ident"][:, :], ring[:, prev, s, D:D2], start=(s == 0), stop=(s == QE - 1))
                    last.then_inc(s_pv, 1)

                pe.wait_ge(s_wr, 1)
                n = turns(pe)
                with pe.Fori(0, n) as t:
                    for k in range(UNROLL):
                        pe.wait_ge(s_feat[k], (t + 1) * FEAT_INC)
                        hold(pe, s_fT, t * UNROLL + (k + 1))
                        for c in range(QE // PAIR):
                            slots = feat[:, k, 2 * c:2 * c + 2, :] if PAIR == 2 else feat[:, k, c, 0:ED]
                            last = pe.transpose(psT[k % 2][0:TP, c * P:(c + 1) * P], slots, S["ident"][:, :])
                        last.then_inc(s_T, 1)
                        pe.wait_ge(s_g[k], (t + 1) * 16 * QE)
                        pe.wait_ge(s_fT, t * UNROLL + (k + 2))
                        pe.wait_ge(s_xr, t * UNROLL + (k + 1))
                        for s in range(QE):
                            lo = ED * (s % PAIR)
                            pe.matmul(psX[:, s, 0:D], featT[lo:lo + ED, k % 2, s // PAIR, :], w_edge[lo:lo + ED, :], start=True, stop=False)
                            last = pe.matmul(psX[:, s, 0:D], S["ident"][:, :], ring[:, k, s, 0:D], start=False, stop=True)
                        last.then_inc(s_x, 1)
                        sum_values(k, t, (k - 1) % UNROLL)
                sum_values(0, n, UNROLL - 1)

            @block.vector
            def _(dve):
                def block_of(k):
                    return dve.value_load(rec[0:1, k, R_BLOCK:R_BLOCK + 1], min_val=0, max_val=NB - 1)

                def add_values(step, k, t, prev):
                    hold(dve, s_pv, t * UNROLL + (k + 1))
                    acc = blk(S["big"], block_of(prev))[:, D:D2]
                    dve.tensor_tensor(acc, psV[:, 0:D], acc, ALU.add).then_inc(s_done[prev], 1)

                pre = Chain(dve, s_v)
                dve.wait_ge(s_w, 32 if layer == 2 else 32 * heads)
                pre(dve.memset(rec[:, UNROLL - 1, :], 0))
                pre(dve.memset(ring[:, UNROLL - 1, :, D:D2], 0.0))
                pre(dve.nop())
                if layer == 1:
                    pre(dve.tensor_scalar(w_edge[:, :], w_edge[:, :], 0.2, None, ALU.mult))
                dve.nop().then_inc(s_wr, 1)
                dve.nop().then_inc(s_wv, 1)
                dve.nop().then_inc(s_xr, 1)
                for k in range(UNROLL - 1):
                    dve.nop().then_inc(s_done[k], 1)
                n = turns(dve)
                with dve.Fori(0, n) as t:
                    step = Chain(dve, s_v, t * CH + PRE)
                    for k in range(UNROLL):
                        hold(dve, s_rec[k], (t + 1) * 16)
                        b = block_of(k)
                        mask = rec[:, k, R_MASK:R_MASK + QE].bitcast(F32)
                        dve.wait_ge(s_x, t * UNROLL + (k + 1))
                        dve.tensor_tensor(prod[:, :, :], psX[:, :, 0:D], bc(blk(S["big"], b)[:, 0:D], 1, [P, QE, D]), ALU.mult).then_inc(s_xr, 1)
                        dve.wait_ge(s_xr, t * UNROLL + (k + 2))
                        step(dve.tensor_reduce(cat[:, 0:QE, :].rearrange("p s h -> p (s h)"),
                                               prod[:, :, :].rearrange("p s (h d) -> p (s h) d", d=hd), AX.X, ALU.add))
                        step(dve.tensor_tensor(cat[:, 0:QE, :], cat[:, 0:QE, :], bc(mask, 2, [P, QE, heads]), ALU.add))
                        m = blk(S["m"], b)[:, 0:heads]
                        l = blk(S["l"], b)[:, 0:heads]
                        step(dve.tensor_scalar(cat[:, QE, :], m, 0.0, None, ALU.add))
                        dve.nop(nofuse=True)
                        step(dve.tensor_reduce(m, cat[:, :, :].rearrange("p r h -> p h r"), AX.X, ALU.max))
                        step(dve.tensor_tensor(cat[:, :, :], cat[:, :, :], bc(m, 1, [P, ROWS, heads]), ALU.subtract))
                        dve.nop().then_inc(s_cat, 1)
                        add_values(step, k, t, (k - 1) % UNROLL)
                        dve.wait_ge(s_exp, t * UNROLL + (k + 1))
                        vals = ring[:, k, :, D:D2].rearrange("p s (h d) -> p s h d", h=heads)
                        dve.tensor_tensor(vals, vals, bc(wgt[:, 0:QE, :], 3, [P, QE, heads, hd]), ALU.mult).then_inc(s_wv, 1)
                        step(dve.tensor_reduce(tot[:, :], wgt[:, 0:QE, :].rearrange("p r h -> p h r"), AX.X, ALU.add))
                        step(dve.tensor_tensor(l, l, wgt[:, QE, :], ALU.mult))
                        step(dve.tensor_tensor(l, l, tot[:, :], ALU.add))
                        prev = (k - 1) % UNROLL
                        dve.wait_ge(s_done[prev], t + (2 if prev < k else 1))
                        acc = blk(S["big"], b)[:, D:D2].rearrange("p (h d) -> p h d", h=heads)
                        step(dve.tensor_tensor(acc, acc, bc(wgt[:, QE, :], 2, [P, heads, hd]), ALU.mult))
                    while step.n < CH:
                        step(dve.nop())
                    assert step.n == CH, step.n
                add_values(None, 0, n, UNROLL - 1)
        ph.close()


def project_out(nc, S, A):
    L, heads = "L1_gnn_", 4
    with ExitStack() as ctx:
        ph = Phase(nc, ctx, "project")
        stat = ph.sb("stat", [P, 4, NB])
        Y, wide = S["big2"][:, :, 0:D], S["big2"][:, :, D:D2]
        msg = ph.sb("msg", [P, D])
        msgT = ph.sb("msgT", [P, 2, P])
        Wo = ph.sb("Wo", [P, 2, D])
        rows = ph.sb("rows", [P, 3, D])
        rl = ph.sb("rl", [P, NB, heads])
        psT, psY = ph.ps("psT", [P, 512]), ph.ps("psY", [P, 512])
        s_w, s_v, s_var, s_root, s_n, s_st, s_T, s_mT, s_Y, s_y = (ph.sem(n) for n in (
            "weights_loaded", "dve_step", "var_ready", "root_ready", "normalised", "staged", "turned",
            "turned_copied", "out_sums", "y_ready"))
        with nc.Block() as block:
            @block.sync
            def _(sp):
                sp.dma_start(Wo[:, :, :], A[L + "Wo"].rearrange("(c p) n -> p c n", p=P)).then_inc(s_w, 16)
                for i, n in enumerate(("bo", "gamma", "beta")):
                    sp.dma_start(rows[:, i, :], rows_of(A[L + n], D)).then_inc(s_w, 16)

            @block.scalar
            def _(act):
                act.wait_ge(s_n, 1)
                with act.Fori(0, NB) as b:
                    act.activation(msg[:, :], blk(S["big"], b)[:, D:D2], ACT.Copy).then_inc(s_st, 1)
                    act.wait_ge(s_T, b + 1)
                    act.activation(msgT[:, :, :], psT[:, 0:D].rearrange("p (c n) -> p c n", c=2), ACT.Copy).then_inc(s_mT, 1)
                take_root(act, stat, s_var, s_root, 1)

            @block.tensor
            def _(pe):
                pe.wait_ge(s_w, 64)
                with pe.Fori(0, NB) as b:
                    pe.wait_ge(s_st, b + 1)
                    for c in range(2):
                        last = pe.transpose(psT[:, c * P:(c + 1) * P], msg[:, c * P:(c + 1) * P], S["ident"][:, :])
                    last.then_inc(s_T, 1)
                    pe.wait_ge(s_mT, b + 1)
                    pe.wait_ge(s_y, b + 1)
                    for c in range(2):
                        last = pe.matmul(psY[:, 0:D], msgT[:, c, :], Wo[:, c, :], start=(c == 0), stop=(c == 1))
                    last.then_inc(s_Y, 1)

            @block.vector
            def _(dve):
                step = Chain(dve, s_v)
                step(dve.reciprocal(rl[:, :, :], S["l"][:, :, 0:heads]))
                acc = all_heads(S["big"][:, :, D:D2], heads)
                step(dve.tensor_tensor(acc, acc, bc(rl[:, :, :], 3, [P, NB, heads, D // heads]), ALU.mult))
                dve.nop().then_inc(s_n, 1)
                dve.nop().then_inc(s_y, 1)
                with dve.Fori(0, NB) as b:
                    dve.wait_ge(s_Y, b + 1)
                    dve.tensor_tensor(blk(Y, b), psY[:, 0:D], blk(S["H"], b), ALU.add).then_inc(s_y, 1)
                dve.wait_ge(s_y, NB + 1)
                dve.wait_ge(s_w, 64)
                row = lambda i: bc(rows[:, i, :], 1, [P, NB, D])
                step(dve.tensor_tensor(Y, Y, row(0), ALU.add))
                finish_layer(dve, step, S, Y, wide, stat, s_var, s_root, row(1), row(2))
        ph.close()


def share_softmax(nc, S, A):
    heads = 8
    with ExitStack() as ctx:
        ph = Phase(nc, ctx, "share")
        mx = ph.sb("mx", [P, heads])
        mcol = ph.sb("mcol", [heads, 1])
        mcols = ph.sb("mcols", [heads, P])
        mall = ph.sb("mall", [P, heads])
        sc = ph.sb("sc", [P, NB, heads])
        ls = ph.sb("ls", [P, NB, heads])
        lsum = ph.sb("lsum", [P, heads])
        rz = ph.sb("rz", [P, heads])
        bias = ph.sb("bias", [P, D])
        ps1, ps2, ps3 = (ph.ps(f"ps{i}", [P, 512]) for i in range(3))
        s_w, s_v, s_mx, s_mt, s_col, s_all, s_d, s_e, s_l, s_z = (ph.sem(n) for n in (
            "bias_loaded", "dve_step", "max_ready", "max_turned", "col_ready", "max_spread", "diff_ready",
            "exp_ready", "sum_ready", "sum_spread"))
        with nc.Block() as block:
            @block.sync
            def _(sp):
                sp.dma_start(bias[:, :], rows_of(A["L2_gnn_bias"], D)).then_inc(s_w, 16)

            @block.scalar
            def _(act):
                act.wait_ge(s_d, 1)
                act.activation(sc[:, :, :], sc[:, :, :], ACT.Exp).then_inc(s_e, 1)

            @block.tensor
            def _(pe):
                pe.wait_ge(s_mx, 1)
                pe.transpose(ps1[0:heads, 0:P], mx[:, :], S["ident"][:, :]).then_inc(s_mt, 1)
                pe.wait_ge(s_col, 1)
                pe.matmul(ps2[:, 0:heads], mcols[:, :], S["ident"][0:heads, 0:heads], start=True, stop=True).then_inc(s_all, 1)
                pe.wait_ge(s_l, 1)
                pe.matmul(ps3[:, 0:heads], S["ones"][:, :], lsum[:, :], start=True, stop=True).then_inc(s_z, 1)

            @block.vector
            def _(dve):
                step = Chain(dve, s_v)
                step(dve.tensor_reduce(mx[:, :], S["m"][:, :, 0:heads].rearrange("p b h -> p h b"), AX.X, ALU.max))
                dve.nop().then_inc(s_mx, 1)
                dve.wait_ge(s_mt, 1)
                step(dve.tensor_reduce(mcol[:, :], ps1[0:heads, 0:P], AX.X, ALU.max))
                step(dve.tensor_scalar(mcols[:, :], S["ones"][0:heads, :], mcol[:, 0:1], None, ALU.mult))
                dve.nop().then_inc(s_col, 1)
                dve.wait_ge(s_all, 1)
                step(dve.tensor_copy(mall[:, :], ps2[:, 0:heads]))
                step(dve.tensor_tensor(sc[:, :, :], S["m"][:, :, 0:heads], bc(mall[:, :], 1, [P, NB, heads]), ALU.subtract))
                dve.nop().then_inc(s_d, 1)
                dve.wait_ge(s_e, 1)
                step(dve.tensor_tensor(ls[:, :, :], S["l"][:, :, 0:heads], sc[:, :, :], ALU.mult))
                step(dve.tensor_reduce(lsum[:, :], ls[:, :, :].rearrange("p b h -> p h b"), AX.X, ALU.add))
                dve.nop().then_inc(s_l, 1)
                dve.wait_ge(s_z, 1)
                step(dve.reciprocal(rz[:, :], ps3[:, 0:heads]))
                step(dve.tensor_tensor(sc[:, :, :], sc[:, :, :], bc(rz[:, :], 1, [P, NB, heads]), ALU.mult))
                acc = all_heads(S["big"][:, :, D:D2], heads)
                step(dve.tensor_tensor(acc, acc, bc(sc[:, :, :], 3, [P, NB, heads, D // heads]), ALU.mult))
                X = S["X"][:, :, :]
                step(dve.tensor_tensor(X, X, S["big"][:, :, D:D2], ALU.add))
                dve.wait_ge(s_w, 16)
                step(dve.tensor_tensor(X, X, bc(bias[:, :], 1, [P, NB, D]), ALU.add))
        ph.close()


def gat_edges(nc, S, A):
    ROWS = QE + 1
    with ExitStack() as ctx:
        ph = Phase(nc, ctx, "edge3")
        rec = ph.sb("rec", [P, UNROLL, REC], I32)
        ring = ph.sb("ring", [P, UNROLL, QE, XROW])
        cat = ph.sb("cat", [P, ROWS])
        wgt = ph.sb("wgt", [P, ROWS])
        tot = ph.sb("tot", [P, 1])
        s_rec, s_done, s_g = ([ph.sem(f"{n}{k}") for k in range(UNROLL)] for n in ("rec_loaded", "quad_done", "rows_loaded"))
        s_v, s_cat, s_exp = (ph.sem(n) for n in ("dve_step", "scores_ready", "weights_ready"))
        turns = lambda eng: eng.value_load(S["turns0"][0:1, 0:1], min_val=1, max_val=NG_PAD // UNROLL)
        CH = 13 * UNROLL

        with nc.Block() as block:
            @block.sync
            def _(sp):
                n = turns(sp)
                with sp.Fori(0, n) as t:
                    for k in range(UNROLL):
                        sp.wait_ge(s_done[k], t + 1)
                        sp.dma_start(rec[:, k, :], S["rec_d0"][bass.ds(t * UNROLL + k, 1), :, :].rearrange("a p f -> p (a f)")).then_inc(s_rec[k], 16)

            @block.gpsimd
            def _(pool):
                n = turns(pool)
                with pool.Fori(0, n) as t:
                    for k in range(UNROLL):
                        hold(pool, s_rec[k], (t + 1) * 16)
                        for s in range(QE):
                            pool.indirect_dma_start(out=ring[:, k, s, :], out_offset=None, in_=S["tab3"][:, :],
                                                    in_offset=bass.IndirectOffsetOnAxis(ap=rec[:, k, R_SRC + s:R_SRC + s + 1], axis=0)).then_inc(s_g[k], 16)

            @block.scalar
            def _(act):
                n = turns(act)
                with act.Fori(0, n) as t:
                    for k in range(UNROLL):
                        act.wait_ge(s_cat, t * UNROLL + (k + 1))
                        act.activation(wgt[:, :], cat[:, :], ACT.Exp).then_inc(s_exp, 1)

            @block.vector
            def _(dve):
                for k in range(UNROLL):
                    dve.nop().then_inc(s_done[k], 1)
                n = turns(dve)
                with dve.Fori(0, n) as t:
                    step = Chain(dve, s_v, t * CH)
                    for k in range(UNROLL):
                        hold(dve, s_rec[k], (t + 1) * 16)
                        b = dve.value_load(rec[0:1, k, R_BLOCK:R_BLOCK + 1], min_val=0, max_val=NB - 1)
                        mask = rec[:, k, R_MASK:R_MASK + QE].bitcast(F32)
                        m, l = S["m"][:, bass.ds(b, 1), 0], S["l"][:, bass.ds(b, 1), 0]
                        acc = blk(S["big"], b)[:, D:D2]
                        dve.wait_ge(s_g[k], (t + 1) * 16 * QE)
                        step(dve.tensor_scalar(cat[:, 0:QE], ring[:, k, :, D], S["adst"][:, bass.ds(b, 1)], None, ALU.add))
                        step(dve.scalar_tensor_tensor(cat[:, 0:QE], cat[:, 0:QE], 0.2, cat[:, 0:QE], ALU.mult, ALU.max))
                        step(dve.tensor_tensor(cat[:, 0:QE], cat[:, 0:QE], mask, ALU.add))
                        step(dve.tensor_scalar(cat[:, QE:ROWS], m, 0.0, None, ALU.add))
                        dve.nop(nofuse=True)
                        step(dve.tensor_reduce(m, cat[:, :], AX.X, ALU.max))
                        step(dve.tensor_scalar(cat[:, :], cat[:, :], m, None, ALU.subtract))
                        dve.nop().then_inc(s_cat, 1)
                        dve.wait_ge(s_exp, t * UNROLL + (k + 1))
                        step(dve.tensor_reduce(tot[:, :], wgt[:, 0:QE], AX.X, ALU.add))
                        step(dve.scalar_tensor_tensor(l, l, wgt[:, QE:ROWS], tot[:, :], ALU.mult, ALU.add))
                        step(dve.tensor_scalar(acc, acc, wgt[:, QE:ROWS], None, ALU.mult))
                        for s in range(QE):
                            step(dve.scalar_tensor_tensor(acc, ring[:, k, s, 0:D], wgt[:, s:s + 1], acc, ALU.mult, ALU.add))
                        dve.nop().then_inc(s_done[k], 1)
                    assert step.n == CH, step.n
        ph.close()


def gate_nodes(nc, S, A, out):
    L = "L3_gnn_"
    GATES = (0, 2, 3)
    with ExitStack() as ctx:
        ph = Phase(nc, ctx, "gate")
        bias = ph.sb("bias", [P, D])
        w_nat = ph.sb("w_nat", [P, 6, D])
        wT = ph.sb("wT", [P, 2, 3 * D])
        rl = ph.sb("rl", [P, NB])
        hb = ph.sb("hb", [P, D])
        hbT = ph.sb("hbT", [P, 2, P])
        gi, gc, go, cell = (ph.sb(n, [P, D]) for n in ("gi", "gc", "go", "cell"))
        res = ph.sb("res", [P, D])
        idx = ph.sb("idx", [P, 1], I32)
        psW = [ph.ps(f"psW{i}", [P, 512]) for i in range(3)]
        psT, psA, psB = (ph.ps(n, [P, 512]) for n in ("psT", "psA", "psB"))
        s_w, s_v, s_wT, s_wc, s_n, s_st, s_T, s_hT, s_A, s_g, s_c, s_t, s_res, s_out = (ph.sem(n) for n in (
            "weights_loaded", "dve_step", "w_turned", "w_copied", "normalised", "staged", "turned",
            "turned_copied", "gate_sums", "gates_ready", "cell_ready", "cell_tanh", "result_ready", "rows_stored"))
        IN_LOOP = 3
        with nc.Block() as block:
            @block.sync
            def _(sp):
                sp.dma_start(bias[:, :], rows_of(A[L + "bias"], D)).then_inc(s_w, 16)
                for i, g in enumerate(GATES):
                    sp.dma_start(w_nat[:, 2 * i:2 * i + 2, :], A[L + "W_ih"][g * D:(g + 1) * D, :].rearrange("(c p) n -> p c n", p=P)).then_inc(s_w, 16)

            @block.gpsimd
            def _(pool):
                with pool.Fori(0, NB) as b:
                    hold(pool, s_res, b + 1)
                    pool.indirect_dma_start(out=out[:, :], out_offset=bass.IndirectOffsetOnAxis(ap=idx[:, 0:1], axis=0),
                                            in_=res[:, :], in_offset=None, bounds_check=N_NODES - 1, oob_is_err=False).then_inc(s_out, 16)
                pool.wait_ge(s_out, 16 * NB)

            @block.scalar
            def _(act):
                act.wait_ge(s_n, 1)
                with act.Fori(0, NB) as b:
                    act.activation(hb[:, :], blk(S["big"], b)[:, D:D2], ACT.Tanh).then_inc(s_st, 1)
                    act.wait_ge(s_T, b + 1)
                    act.activation(hbT[:, :, :], psT[:, 0:D].rearrange("p (c n) -> p c n", c=2), ACT.Copy).then_inc(s_hT, 1)
                    act.wait_ge(s_A, b + 1)
                    act.wait_ge(s_res, b)
                    act.activation(gi[:, :], psA[:, 0:D], ACT.Sigmoid)
                    act.activation(gc[:, :], psA[:, D:D2], ACT.Tanh)
                    act.activation(go[:, :], psB[:, 0:D], ACT.Sigmoid).then_inc(s_g, 1)
                    act.wait_ge(s_c, b + 1)
                    act.activation(cell[:, :], gc[:, :], ACT.Tanh).then_inc(s_t, 1)

            @block.tensor
            def _(pe):
                pe.wait_ge(s_w, 64)
                for i in range(6):
                    for k in range(2):
                        last = pe.transpose(psW[i // 2][:, ((i % 2) * 2 + k) * P:((i % 2) * 2 + k + 1) * P], w_nat[:, i, k * P:(k + 1) * P], S["ident"][:, :])
                last.then_inc(s_wT, 1)
                pe.wait_ge(s_wc, 1)
                with pe.Fori(0, NB) as b:
                    pe.wait_ge(s_st, b + 1)
                    for c in range(2):
                        last = pe.transpose(psT[:, c * P:(c + 1) * P], hb[:, c * P:(c + 1) * P], S["ident"][:, :])
                    last.then_inc(s_T, 1)
                    pe.wait_ge(s_hT, b + 1)
                    for c in range(2):
                        pe.matmul(psA[:, :], hbT[:, c, :], wT[:, c, 0:D2], start=(c == 0), stop=(c == 1))
                    for c in range(2):
                        last = pe.matmul(psB[:, 0:D], hbT[:, c, :], wT[:, c, D2:3 * D], start=(c == 0), stop=(c == 1))
                    last.then_inc(s_A, 1)

            @block.vector
            def _(dve):
                step = Chain(dve, s_v)
                dve.wait_ge(s_w, 64)
                dve.wait_ge(s_wT, 1)
                for i in range(6):
                    step(dve.tensor_copy(wT[:, :, i * P:(i + 1) * P], psW[i // 2][:, (i % 2) * D:(i % 2 + 1) * D].rearrange("p (k n) -> p k n", k=2)))
                dve.nop().then_inc(s_wc, 1)
                step(dve.reciprocal(rl[:, :], S["l"][:, :, 0]))
                acc = S["big"][:, :, D:D2]
                step(dve.tensor_tensor(acc, acc, bc(rl[:, :], 2, [P, NB, D]), ALU.mult))
                step(dve.tensor_tensor(acc, acc, bc(bias[:, :], 1, [P, NB, D]), ALU.add))
                dve.nop().then_inc(s_n, 1)
                before = step.n
                with dve.Fori(0, NB) as b:
                    step = Chain(dve, s_v, b * IN_LOOP + before)
                    dve.wait_ge(s_g, b + 1)
                    step(dve.tensor_tensor(gc[:, :], gi[:, :], gc[:, :], ALU.mult))
                    dve.nop().then_inc(s_c, 1)
                    dve.wait_ge(s_t, b + 1)
                    step(dve.tensor_tensor(cell[:, :], cell[:, :], go[:, :], ALU.mult))
                    hold(dve, s_out, b * 16)
                    step(dve.tensor_copy(idx[:, :], S["lane_i"][:, bass.ds(b, 1), 0]))
                    dve.tensor_tensor(res[:, :], cell[:, :], blk(S["X"], b), ALU.add).then_inc(s_res, 1)
                    assert step.n == IN_LOOP
        ph.close()


def graph_network(nc, A, out):
    with ExitStack() as ctx:
        S = shared(nc, ctx)
        first_steps(nc, S, A)
        rank_edges(nc, S, A)
        sort_edges(nc, S, A)
        order_nodes(nc, S, A)
        build_records(nc, S, A, 0)
        build_records(nc, S, A, 1)
        fetch_nodes(nc, S, A)
        make_tables(nc, S, A, 0)
        edge_mlp(nc, S, A)
        update_nodes(nc, S, A)
        make_tables(nc, S, A, 1)
        attend(nc, S, A, 1)
        project_out(nc, S, A)
        make_tables(nc, S, A, 2)
        attend(nc, S, A, 2)
        share_softmax(nc, S, A)
        make_tables(nc, S, A, 3)
        gat_edges(nc, S, A)
        gate_nodes(nc, S, A, out)


def kernel(**inputs):
    import concourse.bacc as _bacc
    from concourse.bass_utils import run_bass_kernel_spmd as _run

    nc = _bacc.Bacc("TRN2", target_bir_lowering=False, num_devices=1)
    arrays, args = {}, {}
    for name, a in laid_out(inputs).items():
        if name == "L3_gnn_W_hh":
            continue
        arrays[f"in_{name}"] = a
        args[name] = nc.dram_tensor(f"in_{name}", list(a.shape), mybir.dt.from_np(a.dtype), kind="ExternalInput").ap()
    out = nc.dram_tensor("out_0", [N_NODES, D], F32, kind="ExternalOutput").ap()
    graph_network(nc, args, out)
    r = _run(nc, [arrays], core_ids=[0])
    return r.results[0]["out_0"]
```

```python
import concourse.bass as bass
from concourse import mybir
from contextlib import ExitStack
import numpy as np

F32 = mybir.dt.float32
BF16 = mybir.dt.bfloat16
I32 = mybir.dt.int32
ALU = mybir.AluOpType
ACT = mybir.ActivationFunctionType
AX = mybir.AxisListType

P = 128
N_NODES = 3125
N_EDGES = 53125
D = 256
D2 = 2 * D
ED = 64
NB = -(-N_NODES // P)
NL = NB * P
QE = 4
NQ = -(-N_EDGES // QE)
EDGE_P = 125
EDGE_C = N_EDGES // EDGE_P
SPAN = 85
COLS = 17
HERE = 5
KEY_MAIN = 2.0
QUADS_MAX = NQ + NL + NB
UNROLL = 4
AQ = 8
HALF = 16
NG_PAD = -(-(QUADS_MAX + UNROLL) // P) * P
DUMMY = NL
KEY_STEP = 4096
KEY_CAP = 1023
BIG = 3.0e38
LOW = -1.0e30
EPS = 1e-5
REC = 16
R_SRC, R_REL, R_MASK, R_QUAD, R_BLOCK = 0, 4, 8, 12, 13
LANE = 9
SROW = ED + 4
XROW = D + 4


class Phase:

    def __init__(self, nc, ctx, name):
        self.nc, self.ctx, self.sems, self.name = nc, ctx, [], name

    def sb(self, name, shape, dt=F32):
        return self.ctx.enter_context(self.nc.sbuf_tensor(f"{self.name}_{name}", shape, dt))

    def ps(self, name, shape, dt=F32):
        return self.ctx.enter_context(self.nc.psum_tensor(f"{self.name}_{name}", shape, dt))

    def sem(self, name):
        s = self.nc.alloc_semaphore(f"{self.name}_{name}")
        self.sems.append(s)
        return s

    def close(self):
        self.nc.clear_and_free_semaphores(self.sems)
        self.nc.all_engine_barrier()


class Chain:

    def __init__(self, eng, sem, base=0):
        self.eng, self.sem, self.base, self.n = eng, sem, base, 0

    def __call__(self, ins):
        self.n += 1
        ins.then_inc(self.sem, 1)
        self.eng.wait_ge(self.sem, self.base + self.n)


def bc(ap, axis, shape):
    return ap.unsqueeze(axis).broadcast_to(shape)


def blk(ap, b):
    v = ap[:, bass.ds(b, 1)]
    return v.rearrange("p a f -> p (a f)") if len(v.shape) == 3 else v


def first_steps(nc, S, A):
    with ExitStack() as ctx:
        ph = Phase(nc, ctx, "first")
        rows = ph.sb("rows", [SPAN, 2, EDGE_C // SPAN, EDGE_P], I32)
        rows_f = ph.sb("rows_f", [SPAN, 2, EDGE_C // SPAN, EDGE_P])
        ps = [ph.ps(f"ps{i}", [P, 512]) for i in range(2)]
        s_ld, s_iota, s_v, s_f, s_t = (ph.sem(n) for n in ("list_loaded", "iota_done", "dve_step", "rows_ready", "turned"))
        parts = EDGE_C // SPAN
        with nc.Block() as block:
            @block.sync
            def _(sp):
                for i, n in enumerate(("src", "dst")):
                    sp.dma_start(rows[:, i, :, :], A[n].rearrange("(c t p) -> t c p", t=SPAN, p=EDGE_P)).then_inc(s_ld, 16)

            @block.gpsimd
            def _(pool):
                kw = dict(allow_small_or_imprecise_dtypes=True)
                pool.iota(S["iota_c"][:, :], [[1, P]], base=0, channel_multiplier=0, **kw).then_inc(s_iota, 1)
                pool.iota(S["iota_p"][:, :], [[0, 1]], base=0, channel_multiplier=1, **kw).then_inc(s_iota, 1)

            @block.tensor
            def _(pe):
                pe.wait_ge(s_f, 1)
                for i in range(2):
                    for c in range(parts):
                        last = pe.transpose(ps[i][0:EDGE_P, c * SPAN:(c + 1) * SPAN], rows_f[:, i, c, :], S["ident"][0:SPAN, 0:SPAN])
                last.then_inc(s_t, 1)

            @block.vector
            def _(dve):
                step = Chain(dve, s_v)
                dve.wait_ge(s_iota, 2)
                step(dve.tensor_scalar(S["ident"][:, :], S["iota_c"][:, :], S["iota_p"][:, 0:1], None, ALU.is_equal))
                step(dve.tensor_scalar(S["tri"][:, :], S["iota_c"][:, :], S["iota_p"][:, 0:1], None, ALU.is_gt))
                step(dve.memset(S["ones"][:, :], 1.0))
                dve.wait_ge(s_ld, 32)
                step(dve.tensor_copy(rows_f[:, :, :, :], rows[:, :, :, :]))
                dve.nop().then_inc(s_f, 1)
                dve.wait_ge(s_t, 1)
                step(dve.tensor_copy(S["src_i"][:, :], ps[0][0:EDGE_P, 0:EDGE_C]))
                step(dve.tensor_copy(S["dst_i"][:, :], ps[1][0:EDGE_P, 0:EDGE_C]))
                step(dve.tensor_copy(S["dst_f"][:, :], ps[1][0:EDGE_P, 0:EDGE_C]))
        ph.close()


def rank_edges(nc, S, A):
    TURNS = EDGE_C // COLS
    with ExitStack() as ctx:
        ph = Phase(nc, ctx, "rank")
        part_i = ph.sb("part_i", [EDGE_P, EDGE_C], I32)
        src_f = ph.sb("src_f", [EDGE_P, EDGE_C])
        slo = ph.sb("slo", [EDGE_P, EDGE_C], BF16)
        shi = ph.sb("shi", [EDGE_P, EDGE_C], BF16)
        iota_b = ph.sb("iota_b", [P, P], BF16)
        tri_b = ph.sb("tri_b", [P, P], BF16)
        row_i = ph.sb("row_i", [P, 2, COLS, EDGE_P], I32)
        same = ph.sb("same", [EDGE_P, COLS, EDGE_P], BF16)
        oh_lo = ph.sb("oh_lo", [EDGE_P, COLS, P], BF16)
        oh_hi = ph.sb("oh_hi", [EDGE_P, COLS, NB], BF16)
        above = ph.sb("above", [EDGE_P, EDGE_C])
        place = ph.sb("place", [EDGE_P, EDGE_C])
        zeros = ph.sb("zeros", [P, EDGE_C])
        scan = ph.sb("scan", [P, 2, EDGE_C])
        tot = ph.sb("tot", [P, NB])
        cum = ph.sb("cum", [P, NB])
        look = ph.sb("look", [EDGE_P, COLS, NB])
        W = EDGE_C * EDGE_P // 2
        flat = S["state"]
        oh_loT = flat[:, 0:W + 1].bitcast(BF16)[:, 0:2 * W + 1]
        HW = (EDGE_C * NB + 1) // 2
        before = [flat[:, W + 1 + h * HW:W + 1 + (h + 1) * HW].bitcast(BF16)[:, 0:EDGE_C * NB].rearrange("p (t n) -> p t n", n=NB)
                  for h in range(2)]
        hist = before[0]
        psH = [ph.ps(f"psH{i}", [P, 512]) for i in range(2)]
        psS = ph.ps("psS", [P, 512])
        psL = [ph.ps(f"psL{i}", [P, 512]) for i in range(2)]
        s_v, s_row, s_rused, s_oh, s_H, s_hist, s_deg, s_pre, s_L, s_lk, s_bf, s_a = (ph.sem(n) for n in (
            "dve_step", "row_loaded", "row_used", "onehot_ready", "hist_summed", "hist_copied", "deg_ready",
            "prefix_done", "lookup_done", "lookup_used", "before_ready", "constants_ready"))
        s_row = [s_row, ph.sem("row_loaded_b")]
        IN_A, IN_B = 7, 4

        with nc.Block() as block:
            @block.sync
            def _(sp):
                def load(t, h):
                    sp.dma_start(row_i[:, h, :, :].rearrange("p c n -> p (c n)"),
                                 A["src"][bass.ds(t * (COLS * EDGE_P), COLS * EDGE_P)].rearrange("(a n) -> a n", a=1).broadcast_to([P, COLS * EDGE_P])).then_inc(s_row[h], 16)
                with sp.Fori(0, TURNS // 2) as u:
                    for h in range(2):
                        sp.wait_ge(s_rused, u * 2 + h)
                        load(u * 2 + h, h)
                sp.wait_ge(s_rused, TURNS - 1)
                load(TURNS - 1, 0)

            @block.tensor
            def _(pe):
                def histograms(t, h):
                    pe.wait_ge(s_oh, t + 1)
                    for j in range(COLS):
                        last = pe.matmul(psH[h][:, j * NB:(j + 1) * NB], oh_lo[:, j, :],
                                         oh_hi[:, j, :], start=True, stop=True)
                    last.then_inc(s_H, 1)
                with pe.Fori(0, TURNS // 2) as u:
                    for h in range(2):
                        pe.wait_ge(s_hist, u * 2 + h)
                        histograms(u * 2 + h, h)
                histograms(TURNS - 1, 0)
                pe.wait_ge(s_deg, 1)
                pe.matmul(psS[:, 0:NB], S["tri"][:, :], S["deg2"][:, :], start=True, stop=True)
                pe.matmul(psS[:, 64:64 + NB], S["ones"][:, :], S["deg2"][:, :], start=True, stop=True).then_inc(s_pre, 1)
                pe.wait_ge(s_bf, 1)

                def lookup(g, h):
                    for j in range(COLS):
                        for i in range(2):
                            last = pe.matmul(psL[h][0:EDGE_P, j * NB:(j + 1) * NB],
                                             oh_loT[:, bass.ds((g * COLS + j) * EDGE_P, EDGE_P)],
                                             before[i][:, bass.ds(g * COLS + j, 1), :].rearrange("p a n -> p (a n)"), start=(i == 0), stop=(i == 1))
                    last.then_inc(s_L, 1)
                lookup(0, 0)
                with pe.Fori(0, TURNS // 2) as u:
                    for h in range(2):
                        pe.wait_ge(s_lk, u * 2 + h)
                        lookup(u * 2 + (h + 1), 1 - h)

            @block.scalar
            def _(act):
                def copy(t, h):
                    hold(act, s_H, t + 1)
                    act.activation(hist[:, bass.ds(t * COLS, COLS), :], psH[h][:, 0:COLS * NB].rearrange("p (c n) -> p c n", n=NB), ACT.Copy).then_inc(s_hist, 1)
                with act.Fori(0, TURNS // 2) as u:
                    for h in range(2):
                        copy(u * 2 + h, h)
                copy(TURNS - 1, 0)

            @block.vector
            def _(dve):
                step = Chain(dve, s_v)
                step(dve.tensor_copy(iota_b[:, :], S["iota_c"][:, :]))
                step(dve.tensor_scalar(tri_b[:, :], S["iota_c"][:, :], S["iota_p"][:, 0:1], None, ALU.is_lt))
                step(dve.tensor_copy(src_f[:, :], S["src_i"][:, :]))
                step(dve.tensor_scalar(part_i[:, :], S["src_i"][:, :], P - 1, None, ALU.bitwise_and))
                step(dve.tensor_copy(slo[:, :], part_i[:, :]))
                step(dve.tensor_scalar(part_i[:, :], S["src_i"][:, :], 7, None, ALU.logical_shift_right))
                step(dve.tensor_copy(shi[:, :], part_i[:, :]))
                step(dve.memset(zeros[:, :], 0.0))
                n0 = step.n

                def one_hot_hi(t):
                    return dve.tensor_tensor(oh_hi[:, :, :], bc(iota_b[0:EDGE_P, 0:NB], 1, [EDGE_P, COLS, NB]),
                                             bc(shi[:, bass.ds(t * COLS, COLS)], 2, [EDGE_P, COLS, NB]), ALU.is_equal)

                def turn(t, h, half_turns):
                    step = Chain(dve, s_v, t * IN_A + n0)
                    cols = lambda ap: ap[:, bass.ds(t * COLS, COLS)]
                    hold(dve, s_H, t)
                    step(one_hot_hi(t))
                    dve.tensor_tensor(oh_lo[:, :, :], bc(iota_b[0:EDGE_P, :], 1, [EDGE_P, COLS, P]),
                                      bc(cols(slo), 2, [EDGE_P, COLS, P]), ALU.is_equal).then_inc(s_oh, 1)
                    hold(dve, s_row[h], half_turns * 16 + 16)
                    step(dve.tensor_tensor(same[:, :, :], row_i[0:EDGE_P, h, :, :], bc(cols(src_f), 2, [EDGE_P, COLS, EDGE_P]), ALU.is_equal))
                    step(dve.tensor_tensor(same[:, :, :], same[:, :, :], bc(tri_b[0:EDGE_P, 0:EDGE_P], 1, [EDGE_P, COLS, EDGE_P]), ALU.mult))
                    dve.nop(nofuse=True)
                    step(dve.tensor_reduce(cols(above), same[:, :, :], AX.X, ALU.add))
                    rows = row_i[:, h, :, :].rearrange("p c n -> p (c n)")
                    step(dve.tensor_scalar(rows, rows, P - 1, None, ALU.bitwise_and))
                    dve.nop(nofuse=True)
                    step(dve.tensor_scalar(oh_loT[:, bass.ds(t * (COLS * EDGE_P), COLS * EDGE_P)], rows, S["iota_p"][:, 0:1], None, ALU.is_equal))
                    step(dve.nop())
                    dve.nop().then_inc(s_rused, 1)
                    assert step.n == IN_A

                with dve.Fori(0, TURNS // 2) as u:
                    for h in range(2):
                        turn(u * 2 + h, h, u)
                turn(TURNS - 1, 0, TURNS // 2)
                step = Chain(dve, s_v, n0 + TURNS * IN_A)
                dve.wait_ge(s_hist, TURNS)
                step(dve.tensor_reduce(S["deg2"][:, :], hist[:, :, :].rearrange("p t n -> p n t"), AX.X, ALU.add))
                dve.nop().then_inc(s_deg, 1)
                dve.wait_ge(s_pre, 1)
                starts(dve, step, S["start2"], tot, cum, zeros, psS[:, 0:NB], psS[:, 64:64 + NB])
                base = step.base + step.n
                with dve.Fori(0, NB) as b:
                    step = Chain(dve, s_v, b * IN_B + base)
                    one = hist[:, :, bass.ds(b, 1)].rearrange("p t a -> p (t a)")
                    to = lambda h: before[h][:, :, bass.ds(b, 1)].rearrange("p t a -> p (t a)")
                    step(dve.tensor_tensor_scan(scan[:, 0, :], one, zeros[:, :], S["start2"][:, bass.ds(b, 1)], ALU.add, ALU.add))
                    step(dve.tensor_tensor(scan[:, 1, :], scan[:, 0, :], one, ALU.subtract))
                    step(dve.tensor_scalar(to(0), scan[:, 1, :], 0.0, None, ALU.add))
                    step(dve.tensor_tensor(to(1), scan[:, 1, :], to(0), ALU.subtract))
                    assert step.n == IN_B
                dve.nop().then_inc(s_bf, 1)
                base = base + IN_B * NB

                def found(g, h):
                    step = Chain(dve, s_v, g * 3 + base)
                    step(one_hot_hi(g))
                    hold(dve, s_L, g + 1)
                    step(dve.tensor_tensor(look[:, :, :], psL[h][0:EDGE_P, 0:COLS * NB].rearrange("p (j n) -> p j n", n=NB),
                                           oh_hi[:, :, :], ALU.mult))
                    dve.nop().then_inc(s_lk, 1)
                    dve.nop(nofuse=True)
                    step(dve.tensor_reduce(place[:, bass.ds(g * COLS, COLS)], look[:, :, :], AX.X, ALU.add))
                with dve.Fori(0, TURNS // 2) as u:
                    for h in range(2):
                        found(u * 2 + h, h)
                found(TURNS - 1, 0)
                step = Chain(dve, s_v, base + 3 * TURNS)
                step(dve.tensor_tensor(place[:, :], place[:, :], above[:, :], ALU.add))
                step(dve.tensor_copy(S["place_i"][:, :], place[:, :]))
        ph.close()


def starts(dve, step, start, tot, cum, zeros, ps_within, ps_tot):
    step(dve.tensor_copy(tot[:, :], ps_tot))
    step(dve.tensor_tensor_scan(cum[:, :], tot[:, :], zeros[:, 0:NB], 0.0, ALU.add, ALU.add))
    step(dve.tensor_tensor(cum[:, :], cum[:, :], tot[:, :], ALU.subtract))
    step(dve.tensor_tensor(start[:, :], cum[:, :], ps_within, ALU.add))


def order_nodes(nc, S, A):
    RING = 5
    TURNS = EDGE_C // (HERE * RING)
    EARLY = 8
    with ExitStack() as ctx:
        ph = Phase(nc, ctx, "order")
        part_i = ph.sb("part_i", [EDGE_P, EDGE_C], I32)
        dlo = ph.sb("dlo", [EDGE_P, EDGE_C], BF16)
        dhi = ph.sb("dhi", [EDGE_P, EDGE_C], BF16)
        iota_b = ph.sb("iota_b", [P, P], BF16)
        node_of = ph.sb("node_of", [P, NB])
        PARTS = 5
        PC = EDGE_C // PARTS
        onehot_hi = ph.sb("onehot_hi", [EDGE_P, EDGE_C, NB], BF16)
        row = ph.sb("row", [EDGE_P, RING, HERE, SROW])
        idx = ph.sb("idx", [EDGE_P, RING, HERE], I32)
        pad = ph.sb("pad", [NQ * QE - N_EDGES, SROW])
        s_ld = [ph.sem(f"row_loaded{k}") for k in range(RING)]
        s_st = [ph.sem(f"row_stored{k}") for k in range(RING)]
        s_clear, s_pd = (ph.sem(n) for n in ("rows_cleared", "pad_stored"))
        of = A["edge_attr_64"].rearrange("(t p) f -> p t f", p=EDGE_P)
        flat = S["state"]
        W = PC * P
        onehot_lo = flat[0:EDGE_P, 0:W].bitcast(BF16).rearrange("p (a c n) -> p a c n", a=2, n=P)
        diag = flat[:, W:W + NL].rearrange("p (b n) -> p b n", n=P)
        keyrow = flat[:, W + NL:W + 2 * NL]
        above = flat[:, W + 2 * NL:W + 3 * NL]
        zeros = ph.sb("zeros_b", [EDGE_P, P], BF16)
        deg = ph.sb("deg", [P, NB])
        tot = ph.sb("tot", [P, NB])
        cum = ph.sb("cum", [P, NB])
        zrow = ph.sb("zrow", [P, NB])
        start = ph.sb("start", [P, NB])
        w0 = ph.sb("w0", [P, NB])
        w1 = ph.sb("w1", [P, NB])
        i0 = ph.sb("i0", [P, NB], I32)
        i1 = ph.sb("i1", [P, NB], I32)
        q0 = ph.sb("q0", [P, 2, NB])
        nq = ph.sb("nq", [P, 2, NB])
        key = ph.sb("key", [P, NB])
        pos = ph.sb("pos", [P, NB])
        pos_i = ph.sb("pos_i", [P, NB], I32)
        lane_w = ph.sb("lane_w", [P, NB, LANE], I32)
        lane_f = ph.sb("lane_f", [P, NB, LANE])
        wide = ph.sb("wide", [P, 64])
        mcol = ph.sb("mcol", [64, 1])
        mcols = ph.sb("mcols", [64, P])
        mrow = ph.sb("mrow", [P, 64])
        mend = ph.sb("mend", [P, 2, NB])
        lane_q = ph.sb("lane_q", [P, 3, NB])
        pk = ph.ps("pk", [P, 7 * 512])
        ph_ = ph.ps("phist", [P, 512])

        s_iota, s_v, s_part, s_used = (ph.sem(n) for n in ("iota_done", "dve_step", "part_ready", "part_used"))
        s_deg, s_pre, s_diag, s_key, s_keyrow = (ph.sem(n) for n in (
            "deg_ready", "prefix_done", "diag_ready", "key_spread", "keyrow_ready"))
        s_lane, s_scat, s_back, s_m, s_mt, s_mr, s_md = (ph.sem(n) for n in (
            "lanes_ready", "lanes_scattered", "lanes_loaded", "quads_ready", "quads_turned",
            "mcol_ready", "mrow_done"))

        with nc.Block() as block:
            @block.sync
            def _(sp):
                def load_rows(t):
                    for k in range(RING):
                        at = bass.ds((t * RING + k) * HERE, HERE)
                        hold(sp, s_st[k], t * (16 * HERE))
                        sp.dma_start(row[:, k, :, 0:ED], of[:, at, :]).then_inc(s_ld[k], 16)
                        sp.dma_start(row[:, k, :, ED], S["dst_f"][:, at], allow_slow_non_contiguous=True).then_inc(s_ld[k], 16)
                        sp.dma_start(idx[:, k, :], S["place_i"][:, at]).then_inc(s_ld[k], 16)

                sp.wait_ge(s_clear, 1)
                sp.dma_start(S["sorted_d"][N_EDGES:NQ * QE, :], pad[:, :]).then_inc(s_pd, 16)
                with sp.Fori(0, EARLY) as t:
                    load_rows(t)
                sp.wait_ge(s_scat, 16 * NB)
                sp.dma_start(S["lane_i"][:, :, :], S["lane_d"].rearrange("(b p) f -> p b f", p=P)).then_inc(s_back, 16)
                with sp.Fori(0, TURNS - EARLY) as t:
                    load_rows(t + EARLY)
                sp.wait_ge(s_pd, 16)

            @block.gpsimd
            def _(pool):
                kw = dict(allow_small_or_imprecise_dtypes=True)
                pool.iota(iota_b[:, :], [[1, P]], base=0, channel_multiplier=0, **kw).then_inc(s_iota, 1)
                pool.iota(node_of[:, :], [[P, NB]], base=0, channel_multiplier=1, **kw).then_inc(s_iota, 1)
                def scatter_rows(t):
                    for k in range(RING):
                        hold(pool, s_ld[k], (t + 1) * 48)
                        for j in range(HERE):
                            pool.indirect_dma_start(
                                out=S["sorted_d"][:, :], out_offset=bass.IndirectOffsetOnAxis(ap=idx[:, k, j:j + 1], axis=0),
                                in_=row[:, k, j, :], in_offset=None).then_inc(s_st[k], 16)

                with pool.Fori(0, EARLY) as t:
                    scatter_rows(t)
                pool.wait_ge(s_lane, 1)
                for b in range(NB):
                    pool.indirect_dma_start(
                        out=S["lane_d"][:, :], out_offset=bass.IndirectOffsetOnAxis(ap=pos_i[:, b:b + 1], axis=0),
                        in_=lane_w[:, b, :], in_offset=None).then_inc(s_scat, 16)
                with pool.Fori(0, TURNS - EARLY) as t:
                    scatter_rows(t + EARLY)
                for k in range(RING):
                    pool.wait_ge(s_st[k], TURNS * HERE * 16)

            @block.vector
            def _(dve):
                step = Chain(dve, s_v)
                step(dve.memset(pad[:, :], 0.0))
                step(dve.memset(row[:, :, :, :], 0.0))
                dve.nop().then_inc(s_clear, 1)
                dve.wait_ge(s_iota, 2)
                step(dve.memset(zrow[:, :], 0.0))
                step(dve.memset(zeros[:, :], 0.0))
                step(dve.tensor_scalar(part_i[:, :], S["dst_i"][:, :], P - 1, None, ALU.bitwise_and))
                step(dve.tensor_copy(dlo[:, :], part_i[:, :]))
                step(dve.tensor_scalar(part_i[:, :], S["dst_i"][:, :], 7, None, ALU.logical_shift_right))
                step(dve.tensor_copy(dhi[:, :], part_i[:, :]))
                step(dve.tensor_tensor(onehot_hi[:, :, :], bc(iota_b[0:EDGE_P, 0:NB], 1, [EDGE_P, EDGE_C, NB]),
                                       bc(dhi[:, :], 2, [EDGE_P, EDGE_C, NB]), ALU.is_equal))
                for c in range(PARTS):
                    if c >= 2:
                        dve.wait_ge(s_used, c - 1)
                    dve.tensor_tensor(onehot_lo[:, c % 2, :, :], bc(iota_b[0:EDGE_P, :], 1, [EDGE_P, PC, P]),
                                      bc(dlo[:, c * PC:(c + 1) * PC], 2, [EDGE_P, PC, P]),
                                      ALU.is_equal).then_inc(s_part, 1)
                dve.wait_ge(s_used, PARTS)
                step(dve.tensor_copy(deg[:, :], ph_[:, 0:NB]))
                dve.nop().then_inc(s_deg, 1)
                dve.wait_ge(s_pre, 1)
                starts(dve, step, start, tot, cum, zrow, ph_[:, 64:64 + NB], ph_[:, 128:128 + NB])
                for i, (st, dg) in enumerate(((start, deg), (S["start2"], S["deg2"]))):
                    step(dve.tensor_copy(i0[:, :], st[:, :]))
                    step(dve.tensor_scalar(i1[:, :], i0[:, :], 2, None, ALU.logical_shift_right))
                    step(dve.tensor_copy(q0[:, i, :], i1[:, :]))
                    step(dve.tensor_tensor(w0[:, :], st[:, :], dg[:, :], ALU.add))
                    step(dve.tensor_scalar(w0[:, :], w0[:, :], -1.0, 0.0, ALU.add, ALU.max))
                    step(dve.tensor_copy(i0[:, :], w0[:, :]))
                    step(dve.tensor_scalar(i1[:, :], i0[:, :], 2, None, ALU.logical_shift_right))
                    step(dve.tensor_copy(w1[:, :], i1[:, :]))
                    step(dve.tensor_tensor(nq[:, i, :], w1[:, :], q0[:, i, :], ALU.subtract))
                    step(dve.tensor_scalar(w0[:, :], dg[:, :], 0.0, None, ALU.is_gt))
                    step(dve.scalar_tensor_tensor(nq[:, i, :], nq[:, i, :], 1.0, w0[:, :], ALU.add, ALU.mult))
                step(dve.scalar_tensor_tensor(key[:, :], nq[:, 0, :], KEY_MAIN, nq[:, 1, :], ALU.mult, ALU.add))
                step(dve.tensor_scalar(key[:, :], key[:, :], float(KEY_CAP), float(KEY_STEP), ALU.min, ALU.mult))
                step(dve.tensor_tensor(key[:, :], key[:, :], node_of[:, :], ALU.subtract))
                step(dve.tensor_scalar(key[:, :], key[:, :], float(KEY_STEP - 1), None, ALU.add))
                dve.tensor_tensor(diag, bc(S["ident"][:, :], 1, [P, NB, P]),
                                  bc(key[:, :], 2, [P, NB, P]), ALU.mult).then_inc(s_diag, 1)
                dve.wait_ge(s_keyrow, 1)
                for b in range(NB):
                    step(dve.tensor_scalar(above, keyrow, key[:, b:b + 1], 0.0, ALU.is_gt, ALU.add,
                                           accum_out=pos[:, b:b + 1]))
                step(dve.tensor_copy(pos_i[:, :], pos[:, :]))
                for c, v in enumerate((node_of[:, :], start[:, :], deg[:, :], q0[:, 0, :], nq[:, 0, :],
                                       S["start2"][:, :], S["deg2"][:, :], q0[:, 1, :], nq[:, 1, :])):
                    step(dve.tensor_copy(lane_w[:, :, c], v))
                dve.nop().then_inc(s_lane, 1)
                dve.wait_ge(s_back, 16)
                step(dve.tensor_copy(lane_f[:, :, :], S["lane_i"][:, :, :]))
                step(dve.tensor_copy(S["deg_l"][:, :], lane_f[:, :, 2]))
                step(dve.memset(wide[:, :], 0.0))
                for i in range(2):
                    step(dve.tensor_copy(wide[:, 32 * i:32 * i + NB], lane_f[:, :, 4 + 4 * i]))
                dve.nop().then_inc(s_m, 1)
                dve.wait_ge(s_mt, 1)
                step(dve.tensor_reduce(mcol[:, :], ph_[0:64, 192:192 + P], AX.X, ALU.max))
                step(dve.tensor_scalar(mcol[:, :], mcol[:, :], 1.0, None, ALU.max))
                step(dve.tensor_scalar(mcols[:, :], S["ones"][0:64, :], mcol[:, 0:1], None, ALU.mult))
                dve.nop().then_inc(s_mr, 1)
                dve.wait_ge(s_md, 1)
                step(dve.tensor_copy(mrow[:, :], ph_[:, 384:448]))
                for i in range(2):
                    m, me, lq = mrow[:, 32 * i:32 * i + NB], mend[:, i, :], lane_q
                    step(dve.tensor_tensor_scan(me, m, zrow[:, :], 0.0, ALU.add, ALU.add))
                    step(dve.tensor_tensor(w0[:, :], me, m, ALU.subtract))
                    first, begin, count = (lane_f[:, :, 4 * i + j] for j in (3, 1, 2))
                    step(dve.tensor_tensor(lq[:, 0, :], first, w0[:, :], ALU.subtract))
                    step(dve.tensor_copy(lq[:, 1, :], begin))
                    step(dve.tensor_tensor(lq[:, 2, :], begin, count, ALU.add))
                    step(dve.tensor_copy(S[f"block_at{i}"][:, :], w0[:, :]))
                    step(dve.tensor_copy(S[f"lane_dq{i}"][:, :, 0], lq[:, :, 0]))
                    step(dve.tensor_tensor(S[f"lane_dq{i}"][:, :, 1:NB], lq[:, :, 1:NB], lq[:, :, 0:NB - 1], ALU.subtract))
                    step(dve.tensor_scalar(w1[:, 0:1], mend[:, i, NB - 1:NB], float(UNROLL - 1), None, ALU.add))
                    step(dve.tensor_copy(i0[:, 0:1], w1[:, 0:1]))
                    step(dve.tensor_scalar(S[f"turns{i}"][:, :], i0[:, 0:1], 2, None, ALU.logical_shift_right))
                    step(dve.tensor_scalar(w1[:, 0:1], mend[:, i, NB - 1:NB], float(AQ - 1), None, ALU.add))
                    step(dve.tensor_copy(i0[:, 0:1], w1[:, 0:1]))
                    step(dve.tensor_scalar(S[f"attend_turns{i}"][:, :], i0[:, 0:1], 3, None, ALU.logical_shift_right))
                    step(dve.tensor_scalar(w1[:, 0:1], mend[:, i, NB - 1:NB], float(2 * HALF - 1), None, ALU.add))
                    step(dve.tensor_copy(i0[:, 0:1], w1[:, 0:1]))
                    step(dve.tensor_scalar(S[f"rec_turns{i}"][:, :], i0[:, 0:1], 5, None, ALU.logical_shift_right))
            @block.tensor
            def _(pe):
                pe.wait_ge(s_part, 1)
                pe.matmul(ph_[:, 0:NB], zeros[:, :], onehot_hi[:, 0, :], start=True, stop=False)
                for c in range(PARTS):
                    pe.wait_ge(s_part, c + 1)
                    with pe.Fori(0, PC // HERE) as t:
                        for u in range(HERE):
                            pe.matmul(ph_[:, 0:NB],
                                      onehot_lo[:, c % 2, bass.ds(t * HERE + u, 1), :].rearrange("p a f -> p (a f)"),
                                      onehot_hi[:, bass.ds(t * HERE + (c * PC + u), 1), :].rearrange("p a f -> p (a f)"),
                                      start=False, stop=False)
                    pe.matmul(ph_[:, 0:NB], zeros[:, :], onehot_hi[:, 0, :], start=False,
                              stop=(c == PARTS - 1)).then_inc(s_used, 1)
                pe.wait_ge(s_deg, 1)
                pe.matmul(ph_[:, 64:64 + NB], S["tri"][:, :], deg[:, :], start=True, stop=True)
                pe.matmul(ph_[:, 128:128 + NB], S["ones"][:, :], deg[:, :], start=True, stop=True).then_inc(s_pre, 1)
                pe.wait_ge(s_diag, 1)
                for b in range(NB):
                    last = pe.matmul(pk[:, b * P:(b + 1) * P], S["ones"][:, :], diag[:, b, :], start=True, stop=True)
                last.then_inc(s_key, 1)
                pe.wait_ge(s_m, 1)
                pe.transpose(ph_[0:64, 192:192 + P], wide[:, :], S["ident"][:, :]).then_inc(s_mt, 1)
                pe.wait_ge(s_mr, 1)
                pe.matmul(ph_[:, 384:448], mcols[:, :], S["ident"][0:64, 0:64], start=True, stop=True).then_inc(s_md, 1)

            @block.scalar
            def _(act):
                act.wait_ge(s_key, 1)
                act.activation(keyrow, pk[:, 0:NB * P], ACT.Copy).then_inc(s_keyrow, 1)
        ph.close()


def build_records(nc, S, A, i):
    with ExitStack() as ctx:
        ph = Phase(nc, ctx, f"rec{i}")
        GOT = (2 * QE, QE * SROW)[i]
        of = (A["edge_q"], S["sorted_d"].rearrange("(q e) f -> q (e f)", e=QE).bitcast(I32))[i]
        got = S["state"][:, 0:2 * HALF * GOT].bitcast(I32).rearrange("p (h k f) -> p h k f", h=2, f=GOT)
        place = ph.sb("place", [P, 2, HALF])
        slot = ph.sb("slot", [P, HALF, QE])
        begun = ph.sb("begun", [P, HALF, NB])
        terms = ph.sb("terms", [P, 3, HALF, NB])
        cols = ph.sb("cols", [P, 2, 3, HALF])
        block_f = ph.sb("block_f", [P, 2, HALF])
        quad = ph.sb("quad", [P, 2, HALF])
        quad_c = ph.sb("quad_c", [P, HALF])
        quad_i = ph.sb("quad_i", [P, 2, HALF], I32)
        edge = ph.sb("edge", [P, HALF, QE])
        valid = ph.sb("valid", [P, HALF, QE])
        below = ph.sb("below", [P, HALF, QE])
        src_f = ph.sb("src_f", [P, HALF, QE])
        rec = ph.sb("rec_w", [P, 2, HALF, REC], I32)
        rec_f = rec[:, :, :, :].bitcast(F32)
        s_iota, s_v, s_idx, s_rec = (ph.sem(n) for n in ("iota_done", "dve_step", "index_ready", "record_ready"))
        s_got, s_st = ([ph.sem(f"{n}{h}") for h in range(2)] for n in ("edges_gathered", "records_stored"))
        turns = lambda eng: eng.value_load(S[f"rec_turns{i}"][0:1, 0:1], min_val=1, max_val=NG_PAD // (2 * HALF))
        FIND, MAKE = 8, 12 + (i == 0)
        CH = 2 * (FIND + MAKE)

        with nc.Block() as block:
            @block.sync
            def _(sp):
                n = turns(sp)
                with sp.Fori(0, n) as t:
                    for h in range(2):
                        sp.wait_ge(s_rec, t * 2 + (h + 1))
                        sp.dma_start(S[f"rec_d{i}"][bass.ds((t * 2 + h) * HALF, HALF), :, :].rearrange("k p f -> p k f"),
                                     rec[:, h, :, :]).then_inc(s_st[h], 16)
                for h in range(2):
                    hold(sp, s_st[h], n * 16)

            @block.gpsimd
            def _(pool):
                kw = dict(allow_small_or_imprecise_dtypes=True)
                pool.iota(place[:, :, :], [[HALF, 2], [1, HALF]], base=0, channel_multiplier=0, **kw).then_inc(s_iota, 1)
                pool.iota(slot[:, :, :], [[0, HALF], [1, QE]], base=0, channel_multiplier=0, **kw).then_inc(s_iota, 1)
                n = turns(pool)
                with pool.Fori(0, n) as t:
                    for h in range(2):
                        hold(pool, s_idx, t * 2 + (h + 1))
                        for k in range(HALF):
                            pool.indirect_dma_start(
                                out=got[:, h, k, :], out_offset=None, in_=of,
                                in_offset=bass.IndirectOffsetOnAxis(ap=quad_i[:, h, k:k + 1], axis=0)).then_inc(s_got[h], 16)

            @block.vector
            def _(dve):
                def find(step, h):
                    where = place[:, h, :]
                    step(dve.tensor_tensor(begun[:, :, :], bc(where, 2, [P, HALF, NB]), bc(S[f"block_at{i}"][:, :], 1, [P, HALF, NB]), ALU.is_ge))
                    for c in range(3):
                        last = dve.tensor_tensor(terms[:, c, :, :], begun[:, :, :], bc(S[f"lane_dq{i}"][:, c, :], 1, [P, HALF, NB]), ALU.mult)
                    step(last)
                    dve.tensor_reduce(block_f[:, h, :], begun[:, :, :], AX.X, ALU.add)
                    step(dve.tensor_reduce(cols[:, h, :, :], terms[:, :, :, :], AX.X, ALU.add))
                    step(dve.tensor_tensor(quad[:, h, :], where, cols[:, h, 0, :], ALU.add))
                    step(dve.tensor_scalar(quad_c[:, :], quad[:, h, :], float(NQ - 1), None, ALU.min))
                    step(dve.tensor_copy(quad_i[:, h, :], quad_c[:, :]))
                    dve.nop().then_inc(s_idx, 1)
                    step(dve.tensor_scalar(where, where, float(2 * HALF), None, ALU.add))
                    step(dve.tensor_scalar(block_f[:, h, :], block_f[:, h, :], -1.0, None, ALU.add))

                def make(step, t, h):
                    wide = [P, HALF, QE]
                    dve.wait_ge(s_st[h], t * 16)
                    step(dve.tensor_copy(rec[:, h, :, R_QUAD], quad_i[:, h, :]))
                    step(dve.tensor_copy(rec[:, h, :, R_BLOCK], block_f[:, h, :]))
                    step(dve.scalar_tensor_tensor(edge[:, :, :], bc(quad[:, h, :], 2, wide), float(QE), slot[:, :, :], ALU.mult, ALU.add))
                    step(dve.tensor_tensor(valid[:, :, :], edge[:, :, :], bc(cols[:, h, 1, :], 2, wide), ALU.is_ge))
                    step(dve.tensor_tensor(below[:, :, :], edge[:, :, :], bc(cols[:, h, 2, :], 2, wide), ALU.is_lt))
                    step(dve.tensor_tensor(valid[:, :, :], valid[:, :, :], below[:, :, :], ALU.mult))
                    step(dve.tensor_scalar(rec_f[:, h, :, R_MASK:R_MASK + QE], valid[:, :, :], BIG, -BIG, ALU.mult, ALU.add))
                    dve.wait_ge(s_got[h], (t + 1) * (16 * HALF))
                    if i == 0:
                        step(dve.tensor_copy(rec_f[:, h, :, R_REL:R_REL + QE], got[:, h, :, QE:2 * QE]))
                    rows = got[:, h, :, 0:QE] if i == 0 else got[:, h, :, :].rearrange("p k (e f) -> p k e f", e=QE)[:, :, :, ED].bitcast(F32)
                    step(dve.tensor_copy(src_f[:, :, :], rows))
                    step(dve.scalar_tensor_tensor(src_f[:, :, :], src_f[:, :, :], float(-DUMMY), valid[:, :, :], ALU.add, ALU.mult))
                    step(dve.tensor_scalar(src_f[:, :, :], src_f[:, :, :], float(DUMMY), None, ALU.add))
                    step(dve.tensor_copy(rec[:, h, :, R_SRC:R_SRC + QE], src_f[:, :, :]))
                    step(dve.nop())
                    dve.nop().then_inc(s_rec, 1)

                pre = Chain(dve, s_v)
                dve.wait_ge(s_iota, 2)
                pre(dve.memset(rec[:, :, :, :], 0))
                n = turns(dve)
                find(pre, 0)
                with dve.Fori(0, n) as t:
                    step = Chain(dve, s_v, t * CH + (1 + FIND))
                    find(step, 1)
                    make(step, t, 0)
                    find(step, 0)
                    make(step, t, 1)
                    assert step.n == CH, (step.n, CH)
        ph.close()


def shared(nc, ctx):
    S = {}

    def sb(name, shape, dt=F32):
        S[name] = ctx.enter_context(nc.sbuf_tensor(name, shape, dt))

    def dram(name, shape, dt=F32):
        S[name] = nc.dram_tensor(name, shape, dt).ap()

    sb("state", [P, 6 * NB * D])
    part = lambda a, b: S["state"][:, a * NB * D:b * NB * D].rearrange("p (b f) -> p b f", b=NB)
    S["X"] = part(0, 1)
    S["H"] = part(1, 2)
    S["big"] = part(2, 4)
    S["big2"] = part(4, 6)
    sb("iota_c", [P, P])
    sb("iota_p", [P, 1])
    sb("ident", [P, P])
    sb("ones", [P, P])
    sb("tri", [P, P])
    sb("lane_i", [P, NB, LANE], I32)
    sb("deg_l", [P, NB])
    for i in range(2):
        sb(f"block_at{i}", [P, NB])
        sb(f"lane_dq{i}", [P, 3, NB])
        sb(f"turns{i}", [P, 1], I32)
        sb(f"attend_turns{i}", [P, 1], I32)
        sb(f"rec_turns{i}", [P, 1], I32)
    sb("adst", [P, NB])
    sb("m", [P, NB, 8])
    sb("l", [P, NB, 8])
    dram("lane_d", [NL, LANE], I32)
    dram("sorted_d", [NQ * QE, SROW])
    for i in range(2):
        dram(f"rec_d{i}", [NG_PAD, P, REC], I32)
    dram("tab0", [NL + 1, D2])
    dram("tab1", [NL + 1, D2])
    dram("tab2", [NL + 1, D2])
    dram("tab3", [NL + 1, XROW])
    return S


def shared_by_lists(nc, ctx, S):
    def sb(name, shape, dt=F32):
        S[name] = ctx.enter_context(nc.sbuf_tensor(name, shape, dt))

    sb("src_i", [EDGE_P, EDGE_C], I32)
    sb("dst_i", [EDGE_P, EDGE_C], I32)
    sb("dst_f", [EDGE_P, EDGE_C])
    sb("place_i", [EDGE_P, EDGE_C], I32)
    sb("deg2", [P, NB])
    sb("start2", [P, NB])


def hold(eng, sem, value):
    eng.wait_ge(sem, value)
    eng.nop(nofuse=True)


def rows_of(ap, n):
    return ap.rearrange("(a n) -> a n", a=1).broadcast_to([P, n])


def all_heads(ap, heads):
    return ap.rearrange("p b (h d) -> p b h d", h=heads)


def norm_begin(dve, step, src, dst, stat, wide):
    step(dve.tensor_reduce(stat[:, 0, :], src, AX.X, ALU.add))
    step(dve.tensor_scalar(stat[:, 0, :], stat[:, 0, :], 1.0 / D, None, ALU.mult))
    step(dve.tensor_tensor(dst, src, bc(stat[:, 0, :], 2, [P, NB, D]), ALU.subtract))
    step(dve.tensor_tensor(wide, dst, dst, ALU.mult))
    step(dve.tensor_reduce(stat[:, 1, :], wide, AX.X, ALU.add))
    step(dve.tensor_scalar(stat[:, 1, :], stat[:, 1, :], 1.0 / D, EPS, ALU.mult, ALU.add))


def norm_end(dve, step, dst, stat):
    step(dve.reciprocal(stat[:, 3, :], stat[:, 2, :]))
    step(dve.tensor_tensor(dst, dst, bc(stat[:, 3, :], 2, [P, NB, D]), ALU.mult))


def layer_input(dve, step, S, stat, wide, s_var, s_root, n):
    norm_begin(dve, step, S["X"][:, :, :], S["H"][:, :, :], stat, wide)
    dve.nop().then_inc(s_var, 1)
    dve.wait_ge(s_root, n)
    norm_end(dve, step, S["H"][:, :, :], stat)
    step(dve.tensor_scalar(S["H"][:, :, :], S["H"][:, :, :], 0.0, None, ALU.max))


def take_root(act, stat, s_var, s_root, n):
    act.wait_ge(s_var, n)
    act.activation(stat[:, 2, :], stat[:, 1, :], ACT.Sqrt).then_inc(s_root, 1)


def fetch_nodes(nc, S, A):
    with ExitStack() as ctx:
        ph = Phase(nc, ctx, "fetch")
        row = ph.sb("row", [P, NB], I32)
        row_f = ph.sb("row_f", [P, NB])
        s_row, s_x, s_v = (ph.sem(n) for n in ("rows_ready", "x_loaded", "dve_step"))
        with nc.Block() as block:
            @block.vector
            def _(dve):
                step = Chain(dve, s_v)
                step(dve.tensor_copy(row_f[:, :], S["lane_i"][:, :, 0]))
                step(dve.tensor_scalar(row_f[:, :], row_f[:, :], float(N_NODES - 1), None, ALU.min))
                dve.tensor_copy(row[:, :], row_f[:, :]).then_inc(s_row, 1)

            @block.gpsimd
            def _(pool):
                pool.wait_ge(s_row, 1)
                for b in range(NB):
                    pool.indirect_dma_start(out=S["X"][:, b, :], out_offset=None, in_=A["x"][:, :],
                                            in_offset=bass.IndirectOffsetOnAxis(ap=row[:, b:b + 1], axis=0)).then_inc(s_x, 16)
                pool.wait_ge(s_x, 16 * NB)
        ph.close()


def make_tables(nc, S, A, layer):
    heads = (1, 4, 8, 1)[layer]
    gat = layer == 3
    L = ("L0_gnn_", "L1_gnn_", "L2_gnn_", "L3_gnn_")[layer]
    NA = D if gat else D2
    NO = {0: D2, 1: D, 2: D, 3: 0}[layer]
    ROW = XROW if gat else D2
    tab = S[f"tab{layer}"]
    scale = {0: 1.0, 1: 64 ** -0.5, 2: 32 ** -0.5, 3: 1.0}[layer]
    with ExitStack() as ctx:
        ph = Phase(nc, ctx, f"make{layer}")
        stat = ph.sb("stat", [P, 4, NB])
        wide = S["big2"][:, :, 0:D]
        hst = ph.sb("hst", [P, D])
        hT = ph.sb("hT", [P, 2, P])
        w_row = ph.sb("w_row", [P, 2, NA])
        b_row = ph.sb("b_row", [P, NA])
        w_own = ph.sb("w_own", [P, 2, max(NO, 1)])
        b_own = ph.sb("b_own", [P, max(NO, 1)])
        row = ph.sb("row", [P, ROW])
        prod = ph.sb("prod", [P, D])
        idx = ph.sb("idx", [P, 1], I32)
        empty = ph.sb("empty", [P, NB])
        last_row = ph.sb("last_row", [1, ROW])
        qe = ph.sb("qe", [P, 2])
        att = ph.sb("att", [P, 2, D])
        term = ph.sb("term", [P, 3])
        w_nat = ph.sb("w_nat", [P, 2, D])
        psT = ph.ps("psT", [P, 512])
        psA = ph.ps("psA", [P, 512])
        psB = ph.ps("psB", [P, 512])
        psW = ph.ps("psW", [P, 512])
        s_w, s_v, s_var, s_root, s_wr, s_h, s_hst, s_T, s_hT, s_A, s_B, s_row, s_own, s_scat, s_dummy, s_wT, s_lr = (
            ph.sem(n) for n in ("weights_loaded", "dve_step", "var_ready", "root_ready", "weights_ready",
                                "h_ready", "h_staged", "h_turned", "hT_ready", "row_sums", "own_sums",
                                "row_ready", "own_ready", "row_stored", "dummy_stored", "w_turned", "dummy_ready"))
        n_loads = {0: 3, 1: 7, 2: 6, 3: 3}[layer]
        keeps = 3 * gat
        IN_LOOP = {0: 0, 1: 1, 2: 1, 3: 8}[layer]

        with nc.Block() as block:
            @block.sync
            def _(sp):
                def load(to, of):
                    sp.dma_start(to, of, allow_slow_non_contiguous=True).then_inc(s_w, 16)
                chunks = lambda ap: ap.rearrange("(c p) n -> p c n", p=P)
                if layer == 0:
                    w = chunks(A[L + "eW1"][0:2 * D, :])
                    load(w_row[:, :, :], w[:, 0:2, :])
                    load(w_own[:, :, :], w[:, 2:4, :])
                    load(b_own[:, :], rows_of(A[L + "eb1"], D2))
                elif not gat:
                    load(w_row[:, :, 0:D], chunks(A[L + "Wk"]))
                    load(w_row[:, :, D:D2], chunks(A[L + "Wv"]))
                    load(w_own[:, :, :], chunks(A[L + "Wq"]))
                    load(b_row[:, 0:D], rows_of(A[L + "bk"], D))
                    load(b_row[:, D:D2], rows_of(A[L + "bv"], D))
                    load(b_own[:, :], rows_of(A[L + "bq"], D))
                    if layer == 1:
                        load(qe[:, :], A[L + "query_emb"].rearrange("(c p) -> p c", p=P))
                    if layer == 2:
                        load(prod[:, :], rows_of(A[L + "be"], D))
                else:
                    load(w_nat[:, :, :], chunks(A[L + "W"]))
                    load(att[:, 0, :], rows_of(A[L + "att_src"], D))
                    load(att[:, 1, :], rows_of(A[L + "att_dst"], D))
                sp.wait_ge(s_lr, 1)
                sp.dma_start(tab[DUMMY:DUMMY + 1, :], last_row[:, :]).then_inc(s_dummy, 16)
                sp.wait_ge(s_dummy, 16)

            @block.gpsimd
            def _(pool):
                pool.memset(last_row[:, :], LOW if layer == 0 else 0.0).then_inc(s_lr, 1)
                with pool.Fori(0, NB) as b:
                    hold(pool, s_row, b + 2)
                    pool.indirect_dma_start(out=tab[:, :], out_offset=bass.IndirectOffsetOnAxis(ap=idx[:, 0:1], axis=0),
                                            in_=row[:, :], in_offset=None).then_inc(s_scat, 16)
                pool.wait_ge(s_scat, 16 * NB)

            @block.scalar
            def _(act):
                take_root(act, stat, s_var, s_root, 1)
                act.wait_ge(s_h, 1)
                if layer == 1:
                    act.wait_ge(s_wr, 1)
                with act.Fori(0, NB) as b:
                    act.activation(hst[:, :], blk(S["H"], b), ACT.Copy).then_inc(s_hst, 1)
                    act.wait_ge(s_T, b + 1)
                    act.wait_ge(s_own, b + 1)
                    if layer == 1:
                        act.activation(hT[:, 0, :], psT[:, 0:P], ACT.Identity, bias=qe[:, 0:1])
                        act.activation(hT[:, 1, :], psT[:, P:D], ACT.Identity, bias=qe[:, 1:2]).then_inc(s_hT, 1)
                    else:
                        act.activation(hT[:, :, :], psT[:, 0:D].rearrange("p (c n) -> p c n", c=2), ACT.Copy).then_inc(s_hT, 1)

            @block.tensor
            def _(pe):
                pe.wait_ge(s_wr, 1)
                if gat:
                    for c in range(2):
                        for k in range(2):
                            last = pe.transpose(psW[:, (2 * k + c) * P:(2 * k + c + 1) * P], w_nat[:, c, k * P:(k + 1) * P], S["ident"][:, :])
                    last.then_inc(s_wT, 1)
                    pe.wait_ge(s_h, 1)
                with pe.Fori(0, NB) as b:
                    pe.wait_ge(s_hst, b + 1)
                    pe.transpose(psT[:, 0:P], hst[:, 0:P], S["ident"][:, :])
                    pe.transpose(psT[:, P:D], hst[:, P:D], S["ident"][:, :]).then_inc(s_T, 1)
                    pe.wait_ge(s_hT, b + 1)
                    pe.wait_ge(s_row, b + 1)
                    pe.matmul(psA[:, 0:NA], hT[:, 0, :], w_row[:, 0, :], start=True, stop=False)
                    pe.matmul(psA[:, 0:NA], hT[:, 1, :], w_row[:, 1, :], start=False, stop=True).then_inc(s_A, 1)
                    if NO:
                        pe.wait_ge(s_own, b + 1)
                        pe.matmul(psB[:, 0:NO], hT[:, 0, :], w_own[:, 0, :], start=True, stop=False)
                        pe.matmul(psB[:, 0:NO], hT[:, 1, :], w_own[:, 1, :], start=False, stop=True).then_inc(s_B, 1)

            @block.vector
            def _(dve):
                step = Chain(dve, s_v)
                dve.wait_ge(s_w, 16 * n_loads + 16 * (layer == 2))
                if not gat and layer:
                    step(dve.tensor_scalar(w_own[:, :, :], w_own[:, :, :], scale, None, ALU.mult))
                    step(dve.tensor_scalar(b_own[:, :], b_own[:, :], scale, None, ALU.mult))
                if layer == 1:
                    step(dve.tensor_scalar(qe[:, :], qe[:, :], 0.1, None, ALU.mult))
                if layer == 2:
                    step(dve.tensor_tensor(b_row[:, 0:D], b_row[:, 0:D], prod[:, :], ALU.add))
                dve.nop().then_inc(s_wr, 1)
                if gat:
                    dve.wait_ge(s_wT, 1)
                    step(dve.tensor_copy(w_row[:, :, :], psW[:, :].rearrange("p (k n) -> p k n", k=2)))
                    step(dve.memset(row[:, :], 0.0))
                step(dve.tensor_scalar(empty[:, :], S["deg_l"][:, :], 0.0, None, ALU.is_equal))
                layer_input(dve, step, S, stat, wide, s_var, s_root, 1)
                if layer == 0:
                    step(dve.memset(S["big"][:, :, :], 0.0))
                if layer in (1, 2):
                    step(dve.memset(S["m"][:, :, :], LOW))
                    step(dve.memset(S["l"][:, :, :], 0.0))
                if layer == 2:
                    step(dve.memset(S["big"][:, :, D:D2], 0.0))
                if layer == 1:
                    step(dve.tensor_copy(S["l"][:, :, 0:heads], bc(empty[:, :], 2, [P, NB, heads])))
                if gat:
                    step(dve.memset(S["l"][:, :, :], 1.0))
                dve.nop().then_inc(s_h, 1)
                dve.nop().then_inc(s_row, 1)
                dve.nop().then_inc(s_own, 1)
                before = step.n
                with dve.Fori(0, NB) as b:
                    step = Chain(dve, s_v, b * IN_LOOP + before)
                    hold(dve, s_scat, b * 16)
                    dve.tensor_copy(idx[:, :], S["lane_i"][:, bass.ds(b, 1), 0])
                    dve.wait_ge(s_A, b + 1)
                    if layer == 0:
                        dve.tensor_copy(row[:, :], psA[:, :]).then_inc(s_row, 1)
                    elif not gat:
                        if layer == 1:
                            step(dve.tensor_tensor(row[:, :], psA[:, :], b_row[:, :], ALU.add))
                            dve.tensor_scalar(blk(S["big"], b)[:, D:D2], row[:, D:D2], empty[:, bass.ds(b, 1)], None, ALU.mult).then_inc(s_row, 1)
                        else:
                            dve.tensor_tensor(row[:, :], psA[:, :], b_row[:, :], ALU.add).then_inc(s_row, 1)
                            step(dve.nop())
                    else:
                        step(dve.tensor_copy(row[:, 0:D], psA[:, 0:D]))
                        step(dve.tensor_tensor(prod[:, :], row[:, 0:D], att[:, 0, :], ALU.mult))
                        step(dve.tensor_reduce(term[:, 0:1], prod[:, :], AX.X, ALU.add))
                        step(dve.tensor_tensor(prod[:, :], row[:, 0:D], att[:, 1, :], ALU.mult))
                        step(dve.tensor_reduce(term[:, 1:2], prod[:, :], AX.X, ALU.add))
                        step(dve.tensor_copy(S["adst"][:, bass.ds(b, 1)], term[:, 1:2]))
                        step(dve.tensor_tensor(term[:, 2:3], term[:, 0:1], term[:, 1:2], ALU.add))
                        step(dve.scalar_tensor_tensor(S["m"][:, bass.ds(b, 1), 0], term[:, 2:3], 0.2, term[:, 2:3], ALU.mult, ALU.max))
                        dve.tensor_copy(blk(S["big"], b)[:, D:D2], row[:, 0:D])
                        dve.tensor_copy(row[:, D:D + 1], term[:, 0:1]).then_inc(s_row, 1)
                        dve.wait_ge(s_row, b + 2)
                        dve.nop().then_inc(s_own, 1)
                    if NO:
                        hold(dve, s_B, b + 1)
                        own = blk(S["big2"], b)[:, 0:D2] if layer == 0 else blk(S["big"], b)[:, 0:D]
                        dve.tensor_tensor(own, psB[:, 0:NO], b_own[:, 0:NO], ALU.add).then_inc(s_own, 1)
                    assert step.n == IN_LOOP, step.n
        ph.close()


def edge_mlp(nc, S, A):
    with ExitStack() as ctx:
        ph = Phase(nc, ctx, "edge0")
        rec = ph.sb("rec", [P, UNROLL, REC], I32)
        feat = ph.sb("feat", [P, UNROLL, QE * ED])
        featT = ph.sb("featT", [P, 2, 2, P])
        ring = ph.sb("ring", [P, UNROLL, QE, D2])
        w_edge = ph.sb("w_edge", [P, D2])
        psT = [ph.ps(f"psT{i}", [P, 512]) for i in range(2)]
        psX = ph.ps("psX", [P, QE, D2])
        s_rec, s_done, s_feat = ([ph.sem(f"{n}{k}") for k in range(UNROLL)] for n in ("rec_loaded", "quad_done", "feat_loaded"))
        s_g = [[ph.sem(f"rows{k}_{h}") for h in range(2)] for k in range(UNROLL)]
        s_w, s_v, s_T, s_fT, s_x, s_xr = (ph.sem(n) for n in (
            "weights_loaded", "dve_step", "feat_turned", "featT_ready", "sums_ready", "sums_read"))
        turns = lambda eng: eng.value_load(S["turns0"][0:1, 0:1], min_val=1, max_val=NG_PAD // UNROLL)
        CH = UNROLL * QE

        with nc.Block() as block:
            @block.sync
            def _(sp):
                for h in range(2):
                    sp.dma_start(w_edge[h * ED:(h + 1) * ED, :], A["L0_gnn_eW1"][2 * D:2 * D + ED, :]).then_inc(s_w, 16)
                n = turns(sp)
                with sp.Fori(0, n) as t:
                    for k in range(UNROLL):
                        sp.wait_ge(s_done[k], t + 1)
                        sp.dma_start(rec[:, k, :], S["rec_d0"][bass.ds(t * UNROLL + k, 1), :, :].rearrange("a p f -> p (a f)")).then_inc(s_rec[k], 16)

            @block.gpsimd
            def _(pool):
                n = turns(pool)
                with pool.Fori(0, n) as t:
                    for k in range(UNROLL):
                        hold(pool, s_rec[k], (t + 1) * 16)
                        pool.indirect_dma_start(out=feat[:, k, :], out_offset=None, in_=A["feat_q"][:, :],
                                                in_offset=bass.IndirectOffsetOnAxis(ap=rec[:, k, R_QUAD:R_QUAD + 1], axis=0)).then_inc(s_feat[k], 16)
                        for s in range(QE):
                            pool.indirect_dma_start(out=ring[:, k, s, :], out_offset=None, in_=S["tab0"][:, :],
                                                    in_offset=bass.IndirectOffsetOnAxis(ap=rec[:, k, R_SRC + s:R_SRC + s + 1], axis=0)).then_inc(s_g[k][s // 2], 16)

            @block.scalar
            def _(act):
                act.nop().then_inc(s_fT, 1)
                n = turns(act)
                with act.Fori(0, n) as t:
                    for k in range(UNROLL):
                        act.wait_ge(s_T, t * UNROLL + (k + 1))
                        act.activation(featT[:, k % 2, :, :], psT[k % 2][:, 0:2 * P].rearrange("p (c n) -> p c n", c=2), ACT.Copy).then_inc(s_fT, 1)

            @block.tensor
            def _(pe):
                pe.wait_ge(s_w, 32)
                n = turns(pe)
                with pe.Fori(0, n) as t:
                    for k in range(UNROLL):
                        hold(pe, s_rec[k], (t + 1) * 16)
                        b = pe.value_load(rec[0:1, k, R_BLOCK:R_BLOCK + 1], min_val=0, max_val=NB - 1)
                        pe.wait_ge(s_feat[k], (t + 1) * 16)
                        pe.wait_ge(s_fT, t * UNROLL + (k + 1))
                        pe.transpose(psT[k % 2][:, 0:P], feat[:, k, 0:P], S["ident"][:, :])
                        pe.transpose(psT[k % 2][:, P:2 * P], feat[:, k, P:2 * P], S["ident"][:, :]).then_inc(s_T, 1)
                        pe.wait_ge(s_fT, t * UNROLL + (k + 2))
                        for s in range(QE):
                            if s % 2 == 0:
                                pe.wait_ge(s_xr, t * (2 * UNROLL) + (2 * k + s // 2 + 1))
                            lo = ED * (s % 2)
                            pe.matmul(psX[:, s, :], featT[lo:lo + ED, k % 2, s // 2, :], w_edge[lo:lo + ED, :], start=True, stop=False)
                            last = pe.matmul(psX[:, s, :], S["ident"][:, :], blk(S["big2"], b), start=False, stop=True)
                            if s % 2:
                                last.then_inc(s_x, 1)

            @block.vector
            def _(dve):
                dve.nop().then_inc(s_xr, 2)
                for k in range(UNROLL):
                    dve.nop().then_inc(s_done[k], 1)
                n = turns(dve)
                with dve.Fori(0, n) as t:
                    step = Chain(dve, s_v, t * CH)
                    for k in range(UNROLL):
                        hold(dve, s_rec[k], (t + 1) * 16)
                        b = dve.value_load(rec[0:1, k, R_BLOCK:R_BLOCK + 1], min_val=0, max_val=NB - 1)
                        for h in range(2):
                            dve.wait_ge(s_g[k][h], (t + 1) * 32)
                            dve.wait_ge(s_x, t * (2 * UNROLL) + (2 * k + h + 1))
                            both = ring[:, k, 2 * h:2 * h + 2, :]
                            dve.tensor_tensor(both, psX[:, 2 * h:2 * h + 2, :], both, ALU.add).then_inc(s_xr, 1)
                            dve.wait_ge(s_xr, t * (2 * UNROLL) + (2 * k + h + 3))
                            for s in (2 * h, 2 * h + 1):
                                step(dve.scalar_tensor_tensor(blk(S["big"], b), ring[:, k, s, :], 0.0, blk(S["big"], b), ALU.max, ALU.add))
                        dve.nop().then_inc(s_done[k], 1)
        ph.close()


def laid_out(inputs):
    a = {n: np.ascontiguousarray(v) for n, v in inputs.items()}
    pad = NQ * QE - N_EDGES
    src, rel, feat = a["src"], a.pop("edge_type_64"), a["edge_attr_64"]
    quads = lambda v: np.concatenate([v, np.zeros((pad,) + v.shape[1:], v.dtype)]).reshape(NQ, -1)
    a["edge_q"] = np.concatenate([quads(src), quads(rel)], axis=1)
    a["feat_q"] = quads(feat)
    return a


def update_nodes(nc, S, A):
    L = "L0_gnn_"
    with ExitStack() as ctx:
        ph = Phase(nc, ctx, "update")
        stat = ph.sb("stat", [P, 4, NB])
        wide = S["big2"][:, :, D:D2]
        Y = S["big2"][:, :, 0:D]
        sums = ph.sb("sums", [P, D2])
        hst = ph.sb("hst", [P, D])
        sumsT = ph.sb("sumsT", [P, 4, P])
        inT = ph.sb("inT", [P, 4, P])
        upT = ph.sb("upT", [P, 4, P])
        eW2 = ph.sb("eW2", [P, 4, D])
        nW1 = ph.sb("nW1", [P, 4, D2])
        nW2 = ph.sb("nW2", [P, 4, D])
        eb2 = ph.sb("eb2", [1, D])
        nb1 = ph.sb("nb1", [P, 4])
        rows = ph.sb("rows", [P, 3, D])
        deg_i = ph.sb("deg_i", [1, NL], I32)
        deg_row = S["big2"][0:1, :, D:D + P]
        psR, psH, psM, psU, psY = (ph.ps(n, [P, 512]) for n in ("psR", "psH", "psM", "psU", "psY"))
        s_w, s_v, s_var, s_root, s_deg, s_st, s_T, s_sT, s_M, s_mT, s_U, s_uT, s_Y, s_y = (
            ph.sem(n) for n in ("weights_loaded", "dve_step", "var_ready", "root_ready", "deg_ready",
                                "staged", "turned", "turned_copied", "agg_sums", "agg_copied", "up_sums",
                                "up_ready", "down_sums", "y_ready"))
        with nc.Block() as block:
            @block.sync
            def _(sp):
                chunks = lambda ap: ap.rearrange("(c p) n -> p c n", p=P)
                for to, of in ((eW2[:, :, :], chunks(A[L + "eW2"])), (nW1[:, :, :], chunks(A[L + "nW1"])),
                               (nW2[:, :, :], chunks(A[L + "nW2"])), (eb2[:, :], A[L + "eb2"].rearrange("(a n) -> a n", a=1)),
                               (nb1[:, :], A[L + "nb1"].rearrange("(c p) -> p c", p=P)),
                               (rows[:, 0, :], rows_of(A[L + "nb2"], D)), (rows[:, 1, :], rows_of(A[L + "ln_gamma"], D)),
                               (rows[:, 2, :], rows_of(A[L + "ln_beta"], D)),
                               (deg_i[:, :], S["lane_d"][:, 2].rearrange("(a n) -> a n", a=1))):
                    sp.dma_start(to, of, allow_slow_non_contiguous=True).then_inc(s_w, 16)

            @block.scalar
            def _(act):
                act.wait_ge(s_w, 16 * 9)
                with act.Fori(0, NB) as b:
                    act.activation(sums[:, :], blk(S["big"], b), ACT.Copy)
                    act.activation(hst[:, :], blk(S["H"], b), ACT.Copy).then_inc(s_st, 1)
                    act.wait_ge(s_T, b + 1)
                    act.activation(sumsT[:, :, :], psR[:, :].rearrange("p (c n) -> p c n", c=4), ACT.Copy)
                    act.activation(inT[:, 0:2, :], psH[:, 0:D].rearrange("p (c n) -> p c n", c=2), ACT.Copy).then_inc(s_sT, 1)
                    act.wait_ge(s_M, b + 1)
                    act.activation(inT[:, 2:4, :], psM[:, 0:D].rearrange("p (c n) -> p c n", c=2), ACT.Copy).then_inc(s_mT, 1)
                    act.wait_ge(s_U, b + 1)
                    for c in range(4):
                        last = act.activation(upT[:, c, :], psU[:, c * P:(c + 1) * P], ACT.Relu, bias=nb1[:, c:c + 1])
                    last.then_inc(s_uT, 1)
                take_root(act, stat, s_var, s_root, 1)

            @block.tensor
            def _(pe):
                pe.wait_ge(s_w, 16 * 9)
                pe.wait_ge(s_deg, 1)
                with pe.Fori(0, NB) as b:
                    pe.wait_ge(s_st, b + 1)
                    for c in range(4):
                        pe.transpose(psR[:, c * P:(c + 1) * P], sums[:, c * P:(c + 1) * P], S["ident"][:, :])
                    for c in range(2):
                        last = pe.transpose(psH[:, c * P:(c + 1) * P], hst[:, c * P:(c + 1) * P], S["ident"][:, :])
                    last.then_inc(s_T, 1)
                    pe.wait_ge(s_sT, b + 1)
                    for f in range(2):
                        to = psM[:, f * P:(f + 1) * P]
                        for c in range(4):
                            pe.matmul(to, eW2[:, c, f * P:(f + 1) * P], sumsT[:, c, :], start=(c == 0), stop=False)
                        last = pe.matmul(to, eb2[0:1, f * P:(f + 1) * P], blk(deg_row, b), start=False, stop=True)
                    last.then_inc(s_M, 1)
                    pe.wait_ge(s_mT, b + 1)
                    for f in range(4):
                        for c in range(4):
                            last = pe.matmul(psU[:, f * P:(f + 1) * P], nW1[:, c, f * P:(f + 1) * P], inT[:, c, :], start=(c == 0), stop=(c == 3))
                    last.then_inc(s_U, 1)
                    pe.wait_ge(s_uT, b + 1)
                    pe.wait_ge(s_y, b + 1)
                    for c in range(4):
                        last = pe.matmul(psY[:, 0:D], upT[:, c, :], nW2[:, c, :], start=(c == 0), stop=(c == 3))
                    last.then_inc(s_Y, 1)

            @block.vector
            def _(dve):
                step = Chain(dve, s_v)
                dve.wait_ge(s_w, 16 * 9)
                step(dve.tensor_copy(deg_row, deg_i[:, :].rearrange("a (b n) -> a b n", n=P)))
                dve.nop().then_inc(s_deg, 1)
                dve.nop().then_inc(s_y, 1)
                with dve.Fori(0, NB) as b:
                    dve.wait_ge(s_Y, b + 1)
                    dve.tensor_tensor(blk(Y, b), psY[:, 0:D], blk(S["H"], b), ALU.add).then_inc(s_y, 1)
                dve.wait_ge(s_y, NB + 1)
                row = lambda i: bc(rows[:, i, :], 1, [P, NB, D])
                step(dve.tensor_tensor(Y, Y, row(0), ALU.add))
                finish_layer(dve, step, S, Y, wide, stat, s_var, s_root, row(1), row(2))
        ph.close()


def finish_layer(dve, step, S, Y, wide, stat, s_var, s_root, gamma, beta):
    norm_begin(dve, step, Y, Y, stat, wide)
    dve.nop().then_inc(s_var, 1)
    dve.wait_ge(s_root, 1)
    norm_end(dve, step, Y, stat)
    step(dve.tensor_tensor(Y, Y, gamma, ALU.mult))
    step(dve.tensor_tensor(S["X"][:, :, :], S["X"][:, :, :], beta, ALU.add))
    step(dve.tensor_tensor(S["X"][:, :, :], S["X"][:, :, :], Y, ALU.add))


def attend(nc, S, A, layer):
    heads = (None, 4, 8)[layer]
    hd = D // heads
    ROWS = QE + 1
    with ExitStack() as ctx:
        ph = Phase(nc, ctx, f"edge{layer}")
        rec = ph.sb("rec", [P, AQ, REC], I32)
        FW = (None, ED, SROW)[layer]
        feat = ph.sb("feat", [P, AQ, QE, FW])
        PAIR = (None, 2, 1)[layer]
        TP = PAIR * ED
        featT = ph.sb("featT", [TP, 2, QE // PAIR, P])
        IN_BIG2 = NB * D2 // (QE * D2)
        rest = ph.sb("ring", [P, AQ - IN_BIG2, QE, D2])
        ring = [S["big2"].rearrange("p b f -> p (b f)")[:, k * QE * D2:(k + 1) * QE * D2].rearrange("p (s f) -> p s f", f=D2)
                for k in range(IN_BIG2)] + [rest[:, k, :, :] for k in range(AQ - IN_BIG2)]
        w_edge = ph.sb("w_edge", [P, D])
        prod = ph.sb("prod", [P, QE, D])
        cat = ph.sb("cat", [P, 2, ROWS, heads])
        wgt = ph.sb("wgt", [P, 2, ROWS, heads])
        tot = ph.sb("tot", [P, heads])
        psT = [ph.ps(f"psT{i}", [P, 512]) for i in range(2)]
        psX = [ph.ps(f"psX{i}", [P, 2, QE // 2, D]) for i in range(2)]
        s_rec, s_done, s_feat, s_g = ([ph.sem(f"{n}{k}") for k in range(AQ)] for n in (
            "rec_loaded", "quad_done", "feat_ready", "rows_loaded"))
        s_w, s_v, s_T, s_fT, s_x, s_xr, s_cat, s_exp, s_wr = (ph.sem(n) for n in (
            "weights_loaded", "dve_step", "feat_turned", "featT_ready", "keys_ready", "keys_read",
            "scores_ready", "weights_ready", "w_edge_ready"))
        turns = lambda eng: eng.value_load(S[f"attend_turns{layer - 1}"][0:1, 0:1], min_val=1, max_val=NG_PAD // AQ)
        CH = 11 * AQ
        FEAT_INC = 1 if layer == 1 else 16
        PRE = 4 + (layer == 1)

        with nc.Block() as block:
            @block.sync
            def _(sp):
                for h in range(2):
                    if layer == 2:
                        sp.dma_start(w_edge[h * ED:(h + 1) * ED, :], A["L2_gnn_We"][:, :]).then_inc(s_w, 16)
                    else:
                        for i in range(heads):
                            sp.dma_start(w_edge[h * ED:(h + 1) * ED, i * hd:(i + 1) * hd], A["L1_gnn_rel_w"][:, :]).then_inc(s_w, 16)
                n = turns(sp)
                with sp.Fori(0, n) as t:
                    for k in range(AQ):
                        sp.wait_ge(s_done[k], t + 1)
                        sp.dma_start(rec[:, k, :], S[f"rec_d{layer - 1}"][bass.ds(t * AQ + k, 1), :, :].rearrange("a p f -> p (a f)")).then_inc(s_rec[k], 16)

            @block.gpsimd
            def _(pool):
                def features(k):
                    if layer == 2:
                        pool.indirect_dma_start(out=feat[:, k, :, :].rearrange("p s f -> p (s f)"), out_offset=None,
                                                in_=S["sorted_d"].rearrange("(q e) f -> q (e f)", e=QE),
                                                in_offset=bass.IndirectOffsetOnAxis(ap=rec[:, k, R_QUAD:R_QUAD + 1], axis=0)).then_inc(s_feat[k], 16)
                    else:
                        for s in range(QE):
                            last = pool.tensor_scalar(feat[:, k, s, :], S["iota_c"][:, 0:ED], rec[:, k, R_REL + s:R_REL + s + 1].bitcast(F32), None, ALU.is_equal)
                        last.then_inc(s_feat[k], 1)

                n = turns(pool)
                with pool.Fori(0, n) as t:
                    for k in range(AQ):
                        hold(pool, s_rec[k], (t + 1) * 16)
                        features(k)
                        for s in range(QE):
                            pool.indirect_dma_start(out=ring[k][:, s, :], out_offset=None, in_=S[f"tab{layer}"][:, :],
                                                    in_offset=bass.IndirectOffsetOnAxis(ap=rec[:, k, R_SRC + s:R_SRC + s + 1], axis=0)).then_inc(s_g[k], 16)
                hold(pool, s_done[0], n + 1)
                features(0)

            @block.scalar
            def _(act):
                def copy_features(t, k, buf):
                    act.wait_ge(s_T, t * AQ + (k + 1))
                    act.activation(featT[:, buf, :, :], psT[buf][0:TP, 0:QE // PAIR * P].rearrange("p (c n) -> p c n", n=P), ACT.Copy).then_inc(s_fT, 1)

                act.nop().then_inc(s_fT, 1)
                act.nop().then_inc(s_exp, 1)
                n = turns(act)
                copy_features(0, 0, 0)
                with act.Fori(0, n) as t:
                    for k in range(AQ):
                        copy_features(t, k + 1, (k + 1) % 2)
                        act.wait_ge(s_cat, t * AQ + (k + 1))
                        act.activation(wgt[:, k % 2, :, :], cat[:, k % 2, :, :], ACT.Exp).then_inc(s_exp, 1)

            @block.tensor
            def _(pe):
                def turn_features(turn, t, k, buf, at):
                    pe.wait_ge(s_feat[at], turn * FEAT_INC)
                    hold(pe, s_fT, t * AQ + (k if k else 1))
                    for c in range(QE // PAIR):
                        slots = feat[:, at, 2 * c:2 * c + 2, :] if PAIR == 2 else feat[:, at, c, 0:ED]
                        last = pe.transpose(psT[buf][0:TP, c * P:(c + 1) * P], slots, S["ident"][:, :])
                    last.then_inc(s_T, 1)

                pe.wait_ge(s_wr, 1)
                n = turns(pe)
                turn_features(1, 0, 0, 0, 0)
                with pe.Fori(0, n) as t:
                    for k in range(AQ):
                        nxt = (k + 1) % AQ
                        pe.wait_ge(s_g[k], (t + 1) * 16 * QE)
                        pe.wait_ge(s_fT, t * AQ + (k + 2))
                        pe.wait_ge(s_xr, t * AQ + (k + 1))
                        for s in range(QE):
                            lo = ED * (s % PAIR)
                            if s == QE - 1:
                                turn_features(t + (1 if nxt else 2), t, k + 1, (k + 1) % 2, nxt)
                            pe.matmul(psX[k % 2][:, s % 2, s // 2, :], featT[lo:lo + ED, k % 2, s // PAIR, :], w_edge[lo:lo + ED, :], start=True, stop=False)
                            last = pe.matmul(psX[k % 2][:, s % 2, s // 2, :], S["ident"][:, :], ring[k][:, s, 0:D], start=False, stop=True)
                        last.then_inc(s_x, 1)

            @block.vector
            def _(dve):
                def block_of(k, t=None):
                    if t is not None:
                        hold(dve, s_rec[k], (t + 1) * 16)
                    return dve.value_load(rec[0:1, k, R_BLOCK:R_BLOCK + 1], min_val=0, max_val=NB - 1)

                def values(step, t, k, at, b, step_in_loop=True):
                    dve.wait_ge(s_exp, t * AQ + (k + 1))
                    w = wgt[:, at % 2, :, :]
                    v = ring[at][:, :, D:D2]
                    acc = blk(S["big"], b)[:, D:D2]
                    acc_h = acc.rearrange("p (h d) -> p h d", h=heads)
                    l = blk(S["l"], b)[:, 0:heads]
                    vals = v.rearrange("p s (h d) -> p s h d", h=heads)
                    dve.nop(nofuse=True)
                    dve.tensor_tensor(l, l, w[:, QE, :], ALU.mult)
                    dve.tensor_tensor(vals, vals, bc(w[:, 0:QE, :], 3, [P, QE, heads, hd]), ALU.mult)
                    nxt = None
                    if at < AQ - 2 or at == AQ - 1 and k == 0 and step_in_loop:
                        nxt = block_of((at + 2) % AQ, t)
                    step(dve.tensor_reduce(tot[:, :], w[:, 0:QE, :].rearrange("p r h -> p h r"), AX.X, ALU.add))
                    step(dve.tensor_tensor(v[:, 0:2, :], v[:, 0:2, :], v[:, 2:4, :], ALU.add))
                    dve.tensor_tensor(acc_h, acc_h, bc(w[:, QE, :], 2, [P, heads, hd]), ALU.mult)
                    dve.tensor_tensor(l, l, tot[:, :], ALU.add)
                    step(dve.tensor_tensor(v[:, 0, :], v[:, 0, :], v[:, 1, :], ALU.add))
                    step(dve.tensor_tensor(acc, acc, v[:, 0, :], ALU.add))
                    dve.nop().then_inc(s_done[at], 1)
                    return nxt

                pre = Chain(dve, s_v)
                dve.wait_ge(s_w, 32 if layer == 2 else 32 * heads)
                pre(dve.memset(rec[:, AQ - 1, :], 0))
                pre(dve.memset(ring[AQ - 1][:, :, D:D2], 0.0))
                pre(dve.memset(wgt[:, 1, 0:QE, :], 0.0))
                pre(dve.memset(wgt[:, 1, QE, :], 1.0))
                if layer == 1:
                    pre(dve.tensor_scalar(w_edge[:, :], w_edge[:, :], 0.2, None, ALU.mult))
                dve.nop().then_inc(s_wr, 1)
                dve.nop().then_inc(s_xr, 1)
                for k in range(AQ - 1):
                    dve.nop().then_inc(s_done[k], 1)
                n = turns(dve)
                with dve.Fori(0, n) as t:
                    step = Chain(dve, s_v, t * CH + PRE)
                    b_prev, b = block_of(AQ - 1), block_of(0, t)
                    for k in range(AQ):
                        mask = rec[:, k, R_MASK:R_MASK + QE].bitcast(F32)
                        dve.wait_ge(s_x, t * AQ + (k + 1))
                        score, m = cat[:, k % 2, :, :], blk(S["m"], b)[:, 0:heads]
                        dve.tensor_scalar(score[:, QE, :], m, 0.0, None, ALU.add)
                        dve.tensor_tensor(prod[:, :, :].rearrange("p (c a) d -> p a c d", a=2), psX[k % 2][:, :, :, :],
                                          blk(S["big"], b)[:, 0:D].unsqueeze(1).unsqueeze(1).broadcast_to([P, 2, QE // 2, D]), ALU.mult).then_inc(s_xr, 1)
                        dve.wait_ge(s_xr, t * AQ + (k + 2))
                        step(dve.tensor_reduce(score[:, 0:QE, :].rearrange("p s h -> p (s h)"),
                                               prod[:, :, :].rearrange("p s (h d) -> p (s h) d", d=hd), AX.X, ALU.add))
                        step(dve.tensor_tensor(score[:, 0:QE, :], score[:, 0:QE, :], bc(mask, 2, [P, QE, heads]), ALU.add))
                        dve.nop(nofuse=True)
                        step(dve.tensor_reduce(m, score.rearrange("p r h -> p h r"), AX.X, ALU.max))
                        step(dve.tensor_tensor(score, score, bc(m, 1, [P, ROWS, heads]), ALU.subtract))
                        dve.nop().then_inc(s_cat, 1)
                        b_prev, b = b, values(step, t, k, (k - 1) % AQ, b_prev)
                    while step.n < CH:
                        step(dve.nop())
                    assert step.n == CH, step.n
                step = Chain(dve, s_v, n * CH + PRE)
                values(step, n, 0, AQ - 1, block_of(AQ - 1), step_in_loop=False)
        ph.close()


def project_out(nc, S, A):
    L, heads = "L1_gnn_", 4
    with ExitStack() as ctx:
        ph = Phase(nc, ctx, "project")
        stat = ph.sb("stat", [P, 4, NB])
        Y, wide = S["big2"][:, :, 0:D], S["big2"][:, :, D:D2]
        msg = ph.sb("msg", [P, D])
        msgT = ph.sb("msgT", [P, 2, P])
        Wo = ph.sb("Wo", [P, 2, D])
        rows = ph.sb("rows", [P, 3, D])
        rl = ph.sb("rl", [P, NB, heads])
        psT, psY = ph.ps("psT", [P, 512]), ph.ps("psY", [P, 512])
        s_w, s_v, s_var, s_root, s_n, s_st, s_T, s_mT, s_Y, s_y = (ph.sem(n) for n in (
            "weights_loaded", "dve_step", "var_ready", "root_ready", "normalised", "staged", "turned",
            "turned_copied", "out_sums", "y_ready"))
        with nc.Block() as block:
            @block.sync
            def _(sp):
                sp.dma_start(Wo[:, :, :], A[L + "Wo"].rearrange("(c p) n -> p c n", p=P)).then_inc(s_w, 16)
                for i, n in enumerate(("bo", "gamma", "beta")):
                    sp.dma_start(rows[:, i, :], rows_of(A[L + n], D)).then_inc(s_w, 16)

            @block.scalar
            def _(act):
                act.wait_ge(s_n, 1)
                with act.Fori(0, NB) as b:
                    act.activation(msg[:, :], blk(S["big"], b)[:, D:D2], ACT.Copy).then_inc(s_st, 1)
                    act.wait_ge(s_T, b + 1)
                    act.activation(msgT[:, :, :], psT[:, 0:D].rearrange("p (c n) -> p c n", c=2), ACT.Copy).then_inc(s_mT, 1)
                take_root(act, stat, s_var, s_root, 1)

            @block.tensor
            def _(pe):
                pe.wait_ge(s_w, 64)
                with pe.Fori(0, NB) as b:
                    pe.wait_ge(s_st, b + 1)
                    for c in range(2):
                        last = pe.transpose(psT[:, c * P:(c + 1) * P], msg[:, c * P:(c + 1) * P], S["ident"][:, :])
                    last.then_inc(s_T, 1)
                    pe.wait_ge(s_mT, b + 1)
                    pe.wait_ge(s_y, b + 1)
                    for c in range(2):
                        last = pe.matmul(psY[:, 0:D], msgT[:, c, :], Wo[:, c, :], start=(c == 0), stop=(c == 1))
                    last.then_inc(s_Y, 1)

            @block.vector
            def _(dve):
                step = Chain(dve, s_v)
                step(dve.reciprocal(rl[:, :, :], S["l"][:, :, 0:heads]))
                acc = all_heads(S["big"][:, :, D:D2], heads)
                step(dve.tensor_tensor(acc, acc, bc(rl[:, :, :], 3, [P, NB, heads, D // heads]), ALU.mult))
                dve.nop().then_inc(s_n, 1)
                dve.nop().then_inc(s_y, 1)
                with dve.Fori(0, NB) as b:
                    dve.wait_ge(s_Y, b + 1)
                    dve.tensor_tensor(blk(Y, b), psY[:, 0:D], blk(S["H"], b), ALU.add).then_inc(s_y, 1)
                dve.wait_ge(s_y, NB + 1)
                dve.wait_ge(s_w, 64)
                row = lambda i: bc(rows[:, i, :], 1, [P, NB, D])
                step(dve.tensor_tensor(Y, Y, row(0), ALU.add))
                finish_layer(dve, step, S, Y, wide, stat, s_var, s_root, row(1), row(2))
        ph.close()


def share_softmax(nc, S, A):
    heads = 8
    with ExitStack() as ctx:
        ph = Phase(nc, ctx, "share")
        mx = ph.sb("mx", [P, heads])
        mcol = ph.sb("mcol", [heads, 1])
        mcols = ph.sb("mcols", [heads, P])
        mall = ph.sb("mall", [P, heads])
        sc = ph.sb("sc", [P, NB, heads])
        ls = ph.sb("ls", [P, NB, heads])
        lsum = ph.sb("lsum", [P, heads])
        rz = ph.sb("rz", [P, heads])
        bias = ph.sb("bias", [P, D])
        ps1, ps2, ps3 = (ph.ps(f"ps{i}", [P, 512]) for i in range(3))
        s_w, s_v, s_mx, s_mt, s_col, s_all, s_d, s_e, s_l, s_z = (ph.sem(n) for n in (
            "bias_loaded", "dve_step", "max_ready", "max_turned", "col_ready", "max_spread", "diff_ready",
            "exp_ready", "sum_ready", "sum_spread"))
        with nc.Block() as block:
            @block.sync
            def _(sp):
                sp.dma_start(bias[:, :], rows_of(A["L2_gnn_bias"], D)).then_inc(s_w, 16)

            @block.scalar
            def _(act):
                act.wait_ge(s_d, 1)
                act.activation(sc[:, :, :], sc[:, :, :], ACT.Exp).then_inc(s_e, 1)

            @block.tensor
            def _(pe):
                pe.wait_ge(s_mx, 1)
                pe.transpose(ps1[0:heads, 0:P], mx[:, :], S["ident"][:, :]).then_inc(s_mt, 1)
                pe.wait_ge(s_col, 1)
                pe.matmul(ps2[:, 0:heads], mcols[:, :], S["ident"][0:heads, 0:heads], start=True, stop=True).then_inc(s_all, 1)
                pe.wait_ge(s_l, 1)
                pe.matmul(ps3[:, 0:heads], S["ones"][:, :], lsum[:, :], start=True, stop=True).then_inc(s_z, 1)

            @block.vector
            def _(dve):
                step = Chain(dve, s_v)
                step(dve.tensor_reduce(mx[:, :], S["m"][:, :, 0:heads].rearrange("p b h -> p h b"), AX.X, ALU.max))
                dve.nop().then_inc(s_mx, 1)
                dve.wait_ge(s_mt, 1)
                step(dve.tensor_reduce(mcol[:, :], ps1[0:heads, 0:P], AX.X, ALU.max))
                step(dve.tensor_scalar(mcols[:, :], S["ones"][0:heads, :], mcol[:, 0:1], None, ALU.mult))
                dve.nop().then_inc(s_col, 1)
                dve.wait_ge(s_all, 1)
                step(dve.tensor_copy(mall[:, :], ps2[:, 0:heads]))
                step(dve.tensor_tensor(sc[:, :, :], S["m"][:, :, 0:heads], bc(mall[:, :], 1, [P, NB, heads]), ALU.subtract))
                dve.nop().then_inc(s_d, 1)
                dve.wait_ge(s_e, 1)
                step(dve.tensor_tensor(ls[:, :, :], S["l"][:, :, 0:heads], sc[:, :, :], ALU.mult))
                step(dve.tensor_reduce(lsum[:, :], ls[:, :, :].rearrange("p b h -> p h b"), AX.X, ALU.add))
                dve.nop().then_inc(s_l, 1)
                dve.wait_ge(s_z, 1)
                step(dve.reciprocal(rz[:, :], ps3[:, 0:heads]))
                step(dve.tensor_tensor(sc[:, :, :], sc[:, :, :], bc(rz[:, :], 1, [P, NB, heads]), ALU.mult))
                acc = all_heads(S["big"][:, :, D:D2], heads)
                step(dve.tensor_tensor(acc, acc, bc(sc[:, :, :], 3, [P, NB, heads, D // heads]), ALU.mult))
                X = S["X"][:, :, :]
                step(dve.tensor_tensor(X, X, S["big"][:, :, D:D2], ALU.add))
                dve.wait_ge(s_w, 16)
                step(dve.tensor_tensor(X, X, bc(bias[:, :], 1, [P, NB, D]), ALU.add))
        ph.close()


def gat_edges(nc, S, A):
    ROWS = QE + 1
    with ExitStack() as ctx:
        ph = Phase(nc, ctx, "edge3")
        rec = ph.sb("rec", [P, UNROLL, REC], I32)
        ring = ph.sb("ring", [P, UNROLL, QE, XROW])
        cat = ph.sb("cat", [P, ROWS])
        wgt = ph.sb("wgt", [P, ROWS])
        tot = ph.sb("tot", [P, 1])
        s_rec, s_done, s_g = ([ph.sem(f"{n}{k}") for k in range(UNROLL)] for n in ("rec_loaded", "quad_done", "rows_loaded"))
        s_v, s_cat, s_exp = (ph.sem(n) for n in ("dve_step", "scores_ready", "weights_ready"))
        turns = lambda eng: eng.value_load(S["turns0"][0:1, 0:1], min_val=1, max_val=NG_PAD // UNROLL)
        CH = 13 * UNROLL

        with nc.Block() as block:
            @block.sync
            def _(sp):
                n = turns(sp)
                with sp.Fori(0, n) as t:
                    for k in range(UNROLL):
                        sp.wait_ge(s_done[k], t + 1)
                        sp.dma_start(rec[:, k, :], S["rec_d0"][bass.ds(t * UNROLL + k, 1), :, :].rearrange("a p f -> p (a f)")).then_inc(s_rec[k], 16)

            @block.gpsimd
            def _(pool):
                n = turns(pool)
                with pool.Fori(0, n) as t:
                    for k in range(UNROLL):
                        hold(pool, s_rec[k], (t + 1) * 16)
                        for s in range(QE):
                            pool.indirect_dma_start(out=ring[:, k, s, :], out_offset=None, in_=S["tab3"][:, :],
                                                    in_offset=bass.IndirectOffsetOnAxis(ap=rec[:, k, R_SRC + s:R_SRC + s + 1], axis=0)).then_inc(s_g[k], 16)

            @block.scalar
            def _(act):
                n = turns(act)
                with act.Fori(0, n) as t:
                    for k in range(UNROLL):
                        act.wait_ge(s_cat, t * UNROLL + (k + 1))
                        act.activation(wgt[:, :], cat[:, :], ACT.Exp).then_inc(s_exp, 1)

            @block.vector
            def _(dve):
                for k in range(UNROLL):
                    dve.nop().then_inc(s_done[k], 1)
                n = turns(dve)
                with dve.Fori(0, n) as t:
                    step = Chain(dve, s_v, t * CH)
                    for k in range(UNROLL):
                        hold(dve, s_rec[k], (t + 1) * 16)
                        b = dve.value_load(rec[0:1, k, R_BLOCK:R_BLOCK + 1], min_val=0, max_val=NB - 1)
                        mask = rec[:, k, R_MASK:R_MASK + QE].bitcast(F32)
                        m, l = S["m"][:, bass.ds(b, 1), 0], S["l"][:, bass.ds(b, 1), 0]
                        acc = blk(S["big"], b)[:, D:D2]
                        dve.wait_ge(s_g[k], (t + 1) * 16 * QE)
                        step(dve.tensor_scalar(cat[:, 0:QE], ring[:, k, :, D], S["adst"][:, bass.ds(b, 1)], None, ALU.add))
                        step(dve.scalar_tensor_tensor(cat[:, 0:QE], cat[:, 0:QE], 0.2, cat[:, 0:QE], ALU.mult, ALU.max))
                        step(dve.tensor_tensor(cat[:, 0:QE], cat[:, 0:QE], mask, ALU.add))
                        step(dve.tensor_scalar(cat[:, QE:ROWS], m, 0.0, None, ALU.add))
                        dve.nop(nofuse=True)
                        step(dve.tensor_reduce(m, cat[:, :], AX.X, ALU.max))
                        step(dve.tensor_scalar(cat[:, :], cat[:, :], m, None, ALU.subtract))
                        dve.nop().then_inc(s_cat, 1)
                        dve.wait_ge(s_exp, t * UNROLL + (k + 1))
                        step(dve.tensor_reduce(tot[:, :], wgt[:, 0:QE], AX.X, ALU.add))
                        step(dve.scalar_tensor_tensor(l, l, wgt[:, QE:ROWS], tot[:, :], ALU.mult, ALU.add))
                        step(dve.tensor_scalar(acc, acc, wgt[:, QE:ROWS], None, ALU.mult))
                        for s in range(QE):
                            step(dve.scalar_tensor_tensor(acc, ring[:, k, s, 0:D], wgt[:, s:s + 1], acc, ALU.mult, ALU.add))
                        dve.nop().then_inc(s_done[k], 1)
                    assert step.n == CH, step.n
        ph.close()


def gate_nodes(nc, S, A, out):
    L = "L3_gnn_"
    GATES = (0, 2, 3)
    with ExitStack() as ctx:
        ph = Phase(nc, ctx, "gate")
        bias = ph.sb("bias", [P, D])
        w_nat = ph.sb("w_nat", [P, 6, D])
        wT = ph.sb("wT", [P, 2, 3 * D])
        rl = ph.sb("rl", [P, NB])
        hb = ph.sb("hb", [P, D])
        hbT = ph.sb("hbT", [P, 2, P])
        gi, gc, go, cell = (ph.sb(n, [P, D]) for n in ("gi", "gc", "go", "cell"))
        res = ph.sb("res", [P, D])
        idx = ph.sb("idx", [P, 1], I32)
        psW = [ph.ps(f"psW{i}", [P, 512]) for i in range(3)]
        psT, psA, psB = (ph.ps(n, [P, 512]) for n in ("psT", "psA", "psB"))
        s_w, s_v, s_wT, s_wc, s_n, s_st, s_T, s_hT, s_A, s_g, s_c, s_t, s_res, s_out = (ph.sem(n) for n in (
            "weights_loaded", "dve_step", "w_turned", "w_copied", "normalised", "staged", "turned",
            "turned_copied", "gate_sums", "gates_ready", "cell_ready", "cell_tanh", "result_ready", "rows_stored"))
        IN_LOOP = 3
        with nc.Block() as block:
            @block.sync
            def _(sp):
                sp.dma_start(bias[:, :], rows_of(A[L + "bias"], D)).then_inc(s_w, 16)
                for i, g in enumerate(GATES):
                    sp.dma_start(w_nat[:, 2 * i:2 * i + 2, :], A[L + "W_ih"][g * D:(g + 1) * D, :].rearrange("(c p) n -> p c n", p=P)).then_inc(s_w, 16)

            @block.gpsimd
            def _(pool):
                with pool.Fori(0, NB) as b:
                    hold(pool, s_res, b + 1)
                    pool.indirect_dma_start(out=out[:, :], out_offset=bass.IndirectOffsetOnAxis(ap=idx[:, 0:1], axis=0),
                                            in_=res[:, :], in_offset=None, bounds_check=N_NODES - 1, oob_is_err=False).then_inc(s_out, 16)
                pool.wait_ge(s_out, 16 * NB)

            @block.scalar
            def _(act):
                act.wait_ge(s_n, 1)
                with act.Fori(0, NB) as b:
                    act.activation(hb[:, :], blk(S["big"], b)[:, D:D2], ACT.Tanh).then_inc(s_st, 1)
                    act.wait_ge(s_T, b + 1)
                    act.activation(hbT[:, :, :], psT[:, 0:D].rearrange("p (c n) -> p c n", c=2), ACT.Copy).then_inc(s_hT, 1)
                    act.wait_ge(s_A, b + 1)
                    act.wait_ge(s_res, b)
                    act.activation(gi[:, :], psA[:, 0:D], ACT.Sigmoid)
                    act.activation(gc[:, :], psA[:, D:D2], ACT.Tanh)
                    act.activation(go[:, :], psB[:, 0:D], ACT.Sigmoid).then_inc(s_g, 1)
                    act.wait_ge(s_c, b + 1)
                    act.activation(cell[:, :], gc[:, :], ACT.Tanh).then_inc(s_t, 1)

            @block.tensor
            def _(pe):
                pe.wait_ge(s_w, 64)
                for i in range(6):
                    for k in range(2):
                        last = pe.transpose(psW[i // 2][:, ((i % 2) * 2 + k) * P:((i % 2) * 2 + k + 1) * P], w_nat[:, i, k * P:(k + 1) * P], S["ident"][:, :])
                last.then_inc(s_wT, 1)
                pe.wait_ge(s_wc, 1)
                with pe.Fori(0, NB) as b:
                    pe.wait_ge(s_st, b + 1)
                    for c in range(2):
                        last = pe.transpose(psT[:, c * P:(c + 1) * P], hb[:, c * P:(c + 1) * P], S["ident"][:, :])
                    last.then_inc(s_T, 1)
                    pe.wait_ge(s_hT, b + 1)
                    for c in range(2):
                        pe.matmul(psA[:, :], hbT[:, c, :], wT[:, c, 0:D2], start=(c == 0), stop=(c == 1))
                    for c in range(2):
                        last = pe.matmul(psB[:, 0:D], hbT[:, c, :], wT[:, c, D2:3 * D], start=(c == 0), stop=(c == 1))
                    last.then_inc(s_A, 1)

            @block.vector
            def _(dve):
                step = Chain(dve, s_v)
                dve.wait_ge(s_w, 64)
                dve.wait_ge(s_wT, 1)
                for i in range(6):
                    step(dve.tensor_copy(wT[:, :, i * P:(i + 1) * P], psW[i // 2][:, (i % 2) * D:(i % 2 + 1) * D].rearrange("p (k n) -> p k n", k=2)))
                dve.nop().then_inc(s_wc, 1)
                step(dve.reciprocal(rl[:, :], S["l"][:, :, 0]))
                acc = S["big"][:, :, D:D2]
                step(dve.tensor_tensor(acc, acc, bc(rl[:, :], 2, [P, NB, D]), ALU.mult))
                step(dve.tensor_tensor(acc, acc, bc(bias[:, :], 1, [P, NB, D]), ALU.add))
                dve.nop().then_inc(s_n, 1)
                before = step.n
                with dve.Fori(0, NB) as b:
                    step = Chain(dve, s_v, b * IN_LOOP + before)
                    dve.wait_ge(s_g, b + 1)
                    step(dve.tensor_tensor(gc[:, :], gi[:, :], gc[:, :], ALU.mult))
                    dve.nop().then_inc(s_c, 1)
                    dve.wait_ge(s_t, b + 1)
                    step(dve.tensor_tensor(cell[:, :], cell[:, :], go[:, :], ALU.mult))
                    hold(dve, s_out, b * 16)
                    step(dve.tensor_copy(idx[:, :], S["lane_i"][:, bass.ds(b, 1), 0]))
                    dve.tensor_tensor(res[:, :], cell[:, :], blk(S["X"], b), ALU.add).then_inc(s_res, 1)
                    assert step.n == IN_LOOP
        ph.close()


def graph_network(nc, A, out):
    with ExitStack() as ctx:
        S = shared(nc, ctx)
        with ExitStack() as lists:
            shared_by_lists(nc, lists, S)
            first_steps(nc, S, A)
            rank_edges(nc, S, A)
            order_nodes(nc, S, A)
        build_records(nc, S, A, 0)
        build_records(nc, S, A, 1)
        fetch_nodes(nc, S, A)
        make_tables(nc, S, A, 0)
        edge_mlp(nc, S, A)
        update_nodes(nc, S, A)
        make_tables(nc, S, A, 1)
        attend(nc, S, A, 1)
        project_out(nc, S, A)
        make_tables(nc, S, A, 2)
        attend(nc, S, A, 2)
        share_softmax(nc, S, A)
        make_tables(nc, S, A, 3)
        gat_edges(nc, S, A)
        gate_nodes(nc, S, A, out)


def kernel(**inputs):
    import concourse.bacc as _bacc
    from concourse.bass_utils import run_bass_kernel_spmd as _run

    nc = _bacc.Bacc("TRN2", target_bir_lowering=False, num_devices=1)
    arrays, args = {}, {}
    for name, a in laid_out(inputs).items():
        if name == "L3_gnn_W_hh":
            continue
        arrays[f"in_{name}"] = a
        args[name] = nc.dram_tensor(f"in_{name}", list(a.shape), mybir.dt.from_np(a.dtype), kind="ExternalInput").ap()
    out = nc.dram_tensor("out_0", [N_NODES, D], F32, kind="ExternalOutput").ap()
    graph_network(nc, args, out)
    r = _run(nc, [arrays], core_ids=[0])
    return r.results[0]["out_0"]
```

```python
import concourse.bass as bass
from concourse import mybir
from contextlib import ExitStack
import numpy as np

F32 = mybir.dt.float32
BF16 = mybir.dt.bfloat16
I32 = mybir.dt.int32
ALU = mybir.AluOpType
ACT = mybir.ActivationFunctionType
AX = mybir.AxisListType

P = 128
N_NODES = 3125
N_EDGES = 53125
D = 256
D2 = 2 * D
ED = 64
NB = -(-N_NODES // P)
NL = NB * P
QE = 4
NQ = -(-N_EDGES // QE)
EDGE_P = 125
EDGE_C = N_EDGES // EDGE_P
SPAN = 85
COLS = 17
HERE = 5
KEY_MAIN = 2.0
QUADS_MAX = NQ + NL + NB
RING_0 = 4
AQ = 16
RING = 8
ROW_RING = 5
ROW_TURNS = EDGE_C // (HERE * ROW_RING)
ROW_EARLY = 7
HALF = 16
NG_PAD = -(-(QUADS_MAX + AQ) // P) * P
DUMMY = NL
KEY_STEP = 4096
KEY_CAP = 1023
BIG = 3.0e38
LOW = -1.0e30
EPS = 1e-5
REC = 16
R_SRC, R_REL, R_MASK, R_QUAD, R_BLOCK = 0, 4, 8, 12, 13
LANE = 9
SROW = ED + 4
XROW = D + 4


class Phase:

    def __init__(self, nc, ctx, name):
        self.nc, self.ctx, self.sems, self.name = nc, ctx, [], name

    def sb(self, name, shape, dt=F32):
        return self.ctx.enter_context(self.nc.sbuf_tensor(f"{self.name}_{name}", shape, dt))

    def ps(self, name, shape, dt=F32):
        return self.ctx.enter_context(self.nc.psum_tensor(f"{self.name}_{name}", shape, dt))

    def sem(self, name):
        s = self.nc.alloc_semaphore(f"{self.name}_{name}")
        self.sems.append(s)
        return s

    def close(self):
        self.nc.clear_and_free_semaphores(self.sems)
        self.nc.all_engine_barrier()


class Chain:

    def __init__(self, eng, sem, base=0):
        self.eng, self.sem, self.base, self.n = eng, sem, base, 0

    def __call__(self, ins):
        self.n += 1
        ins.then_inc(self.sem, 1)
        self.eng.wait_ge(self.sem, self.base + self.n)

    def put(self, ins):
        self.n += 1
        ins.then_inc(self.sem, 1)
        return self.n

    def until(self, n):
        self.eng.wait_ge(self.sem, self.base + n)


def bc(ap, axis, shape):
    return ap.unsqueeze(axis).broadcast_to(shape)


def blk(ap, b):
    v = ap[:, bass.ds(b, 1)]
    return v.rearrange("p a f -> p (a f)") if len(v.shape) == 3 else v


def first_steps(nc, S, A):
    with ExitStack() as ctx:
        ph = Phase(nc, ctx, "first")
        rows = ph.sb("rows", [SPAN, 2, EDGE_C // SPAN, EDGE_P], I32)
        rows_f = ph.sb("rows_f", [SPAN, 2, EDGE_C // SPAN, EDGE_P])
        ps = [ph.ps(f"ps{i}", [P, 512]) for i in range(2)]
        s_ld, s_iota, s_v, s_f, s_t = (ph.sem(n) for n in ("list_loaded", "iota_done", "dve_step", "rows_ready", "turned"))
        parts = EDGE_C // SPAN
        with nc.Block() as block:
            @block.sync
            def _(sp):
                for i, n in enumerate(("src", "dst")):
                    sp.dma_start(rows[:, i, :, :], A[n].rearrange("(c t p) -> t c p", t=SPAN, p=EDGE_P)).then_inc(s_ld, 16)

            @block.gpsimd
            def _(pool):
                kw = dict(allow_small_or_imprecise_dtypes=True)
                pool.iota(S["iota_c"][:, :], [[1, P]], base=0, channel_multiplier=0, **kw).then_inc(s_iota, 1)
                pool.iota(S["iota_p"][:, :], [[0, 1]], base=0, channel_multiplier=1, **kw).then_inc(s_iota, 1)

            @block.tensor
            def _(pe):
                pe.wait_ge(s_f, 1)
                for i in range(2):
                    for c in range(parts):
                        last = pe.transpose(ps[i][0:EDGE_P, c * SPAN:(c + 1) * SPAN], rows_f[:, i, c, :], S["ident"][0:SPAN, 0:SPAN])
                last.then_inc(s_t, 1)

            @block.vector
            def _(dve):
                step = Chain(dve, s_v)
                dve.wait_ge(s_iota, 2)
                step(dve.tensor_scalar(S["ident"][:, :], S["iota_c"][:, :], S["iota_p"][:, 0:1], None, ALU.is_equal))
                step(dve.tensor_scalar(S["tri"][:, :], S["iota_c"][:, :], S["iota_p"][:, 0:1], None, ALU.is_gt))
                step(dve.memset(S["ones"][:, :], 1.0))
                dve.wait_ge(s_ld, 32)
                step(dve.tensor_copy(rows_f[:, :, :, :], rows[:, :, :, :]))
                dve.nop().then_inc(s_f, 1)
                dve.wait_ge(s_t, 1)
                step(dve.tensor_copy(S["src_i"][:, :], ps[0][0:EDGE_P, 0:EDGE_C]))
                step(dve.tensor_copy(S["dst_i"][:, :], ps[1][0:EDGE_P, 0:EDGE_C]))
                step(dve.tensor_copy(S["dst_f"][:, :], ps[1][0:EDGE_P, 0:EDGE_C]))
        ph.close()


def rank_edges(nc, S, A):
    TURNS = EDGE_C // COLS
    with ExitStack() as ctx:
        ph = Phase(nc, ctx, "rank")
        part_i = ph.sb("part_i", [EDGE_P, EDGE_C], I32)
        src_f = ph.sb("src_f", [EDGE_P, EDGE_C])
        slo = ph.sb("slo", [EDGE_P, EDGE_C], BF16)
        shi = ph.sb("shi", [EDGE_P, EDGE_C], BF16)
        iota_b = ph.sb("iota_b", [P, P], BF16)
        tri_b = ph.sb("tri_b", [P, P], BF16)
        row_i = ph.sb("row_i", [P, 2, COLS, EDGE_P], I32)
        same = ph.sb("same", [EDGE_P, 2, COLS, EDGE_P], BF16)
        oh_lo = ph.sb("oh_lo", [EDGE_P, 2, COLS, P], BF16)
        oh_hi = ph.sb("oh_hi", [EDGE_P, 2, COLS, NB], BF16)
        one_b = ph.sb("one_b", [EDGE_P, 1], BF16)
        above = ph.sb("above", [EDGE_P, EDGE_C])
        spare = row_i[:, :, :, :].rearrange("p h c n -> p (h c n)").bitcast(F32)[:, 0:4 * EDGE_C].rearrange("p (k n) -> p k n", k=4)
        zeros, scan, place = spare[:, 0, :], spare[:, 1:3, :], spare[0:EDGE_P, 3, :]
        tot = ph.sb("tot", [P, NB])
        cum = ph.sb("cum", [P, NB])
        look = ph.sb("look", [EDGE_P, COLS, NB])
        W = EDGE_C * EDGE_P // 2
        flat = S["state"]
        oh_loT = flat[:, 0:W + 1].bitcast(BF16)[:, 0:2 * W + 1]
        HW = (EDGE_C * NB + 1) // 2
        before = [flat[:, W + 1 + h * HW:W + 1 + (h + 1) * HW].bitcast(BF16)[:, 0:EDGE_C * NB].rearrange("p (t n) -> p t n", n=NB)
                  for h in range(2)]
        hist = before[0]
        psH = [ph.ps(f"psH{i}", [P, 512]) for i in range(2)]
        psS = ph.ps("psS", [P, 512])
        psL = [ph.ps(f"psL{i}", [P, 512]) for i in range(2)]
        s_v, s_row, s_rused, s_oh, s_H, s_hist, s_deg, s_pre, s_L, s_lk, s_bf = (ph.sem(n) for n in (
            "dve_step", "row_loaded", "row_used", "onehot_ready", "hist_summed", "hist_copied", "deg_ready",
            "prefix_done", "lookup_done", "lookup_used", "before_ready"))
        s_same = ph.sem("same_ready")
        s_row = [s_row, ph.sem("row_loaded_b")]
        IN_A, IN_B = 3, 4

        with nc.Block() as block:
            @block.sync
            def _(sp):
                def load(t, h):
                    sp.dma_start(row_i[:, h, :, :].rearrange("p c n -> p (c n)"),
                                 A["src"][bass.ds(t * (COLS * EDGE_P), COLS * EDGE_P)].rearrange("(a n) -> a n", a=1).broadcast_to([P, COLS * EDGE_P])).then_inc(s_row[h], 16)
                with sp.Fori(0, TURNS // 2) as u:
                    for h in range(2):
                        sp.wait_ge(s_rused, u * 2 + h)
                        load(u * 2 + h, h)
                sp.wait_ge(s_rused, TURNS - 1)
                load(TURNS - 1, 0)

            @block.tensor
            def _(pe):
                def histograms(t, h):
                    pe.wait_ge(s_oh, t + 1)
                    for j in range(COLS):
                        pe.matmul(psH[h][:, j * NB:(j + 1) * NB], oh_lo[:, h, j, :], oh_hi[:, h, j, :], start=True, stop=True)
                    pe.wait_ge(s_same, t + 1)
                    for j in range(COLS):
                        last = pe.matmul(psH[h][0:EDGE_P, COLS * NB + j:COLS * NB + j + 1], same[:, h, j, :], one_b[:, :], start=True, stop=True)
                    last.then_inc(s_H, 1)
                pe.nop().then_inc(s_H, 1)
                with pe.Fori(0, TURNS // 2) as u:
                    for h in range(2):
                        pe.wait_ge(s_hist, u * 2 + h)
                        histograms(u * 2 + h, h)
                histograms(TURNS - 1, 0)
                pe.wait_ge(s_deg, 1)
                pe.matmul(psS[:, 0:NB], S["tri"][:, :], S["deg2"][:, :], start=True, stop=True)
                pe.matmul(psS[:, 64:64 + NB], S["ones"][:, :], S["deg2"][:, :], start=True, stop=True).then_inc(s_pre, 1)
                pe.wait_ge(s_bf, 1)
                pe.wait_ge(s_rused, TURNS)

                def lookup(g, h):
                    for j in range(COLS):
                        for i in range(2):
                            last = pe.matmul(psL[h][0:EDGE_P, j * NB:(j + 1) * NB],
                                             oh_loT[:, bass.ds((g * COLS + j) * EDGE_P, EDGE_P)],
                                             before[i][:, bass.ds(g * COLS + j, 1), :].rearrange("p a n -> p (a n)"), start=(i == 0), stop=(i == 1))
                    last.then_inc(s_L, 1)
                lookup(0, 0)
                with pe.Fori(0, TURNS // 2) as u:
                    for h in range(2):
                        pe.wait_ge(s_lk, u * 2 + h)
                        lookup(u * 2 + (h + 1), 1 - h)

            @block.scalar
            def _(act):
                def copy(t, h):
                    hold(act, s_H, t + 2)
                    act.activation(above[:, bass.ds(t * COLS, COLS)], psH[h][0:EDGE_P, COLS * NB:COLS * (NB + 1)], ACT.Copy)
                    act.activation(hist[:, bass.ds(t * COLS, COLS), :], psH[h][:, 0:COLS * NB].rearrange("p (c n) -> p c n", n=NB), ACT.Copy).then_inc(s_hist, 1)
                with act.Fori(0, TURNS // 2) as u:
                    for h in range(2):
                        copy(u * 2 + h, h)
                copy(TURNS - 1, 0)

            @block.vector
            def _(dve):
                step = Chain(dve, s_v)
                step(dve.tensor_copy(iota_b[:, :], S["iota_c"][:, :]))
                step(dve.tensor_scalar(tri_b[:, :], S["iota_c"][:, :], S["iota_p"][:, 0:1], None, ALU.is_gt))
                step(dve.memset(one_b[:, :], 1.0))
                step(dve.tensor_copy(src_f[:, :], S["src_i"][:, :]))
                step(dve.tensor_scalar(part_i[:, :], S["src_i"][:, :], P - 1, None, ALU.bitwise_and))
                step(dve.tensor_copy(slo[:, :], part_i[:, :]))
                step(dve.tensor_scalar(part_i[:, :], S["src_i"][:, :], 7, None, ALU.logical_shift_right))
                step(dve.tensor_copy(shi[:, :], part_i[:, :]))
                n0 = step.n

                def one_hot_hi(t, h):
                    return dve.tensor_tensor(oh_hi[:, h, :, :], bc(iota_b[0:EDGE_P, 0:NB], 1, [EDGE_P, COLS, NB]),
                                             bc(shi[:, bass.ds(t * COLS, COLS)], 2, [EDGE_P, COLS, NB]), ALU.is_equal)

                def turn(t, h, half_turns):
                    step = Chain(dve, s_v, t * IN_A + n0)
                    cols = lambda ap: ap[:, bass.ds(t * COLS, COLS)]
                    hold(dve, s_H, t)
                    step(one_hot_hi(t, h))
                    dve.tensor_tensor(oh_lo[:, h, :, :], bc(iota_b[0:EDGE_P, :], 1, [EDGE_P, COLS, P]),
                                      bc(cols(slo), 2, [EDGE_P, COLS, P]), ALU.is_equal).then_inc(s_oh, 1)
                    hold(dve, s_row[h], half_turns * 16 + 16)
                    step(dve.tensor_tensor(same[:, h, :, :], row_i[0:EDGE_P, h, :, :], bc(cols(src_f), 2, [EDGE_P, COLS, EDGE_P]), ALU.is_equal))
                    rows = row_i[:, h, :, :].rearrange("p c n -> p (c n)")
                    step(dve.tensor_scalar(rows, rows, P - 1, None, ALU.bitwise_and))
                    dve.tensor_tensor(same[:, h, :, :], same[:, h, :, :], bc(tri_b[0:EDGE_P, 0:EDGE_P], 1, [EDGE_P, COLS, EDGE_P]), ALU.mult).then_inc(s_same, 1)
                    dve.nop(nofuse=True)
                    dve.tensor_scalar(oh_loT[:, bass.ds(t * (COLS * EDGE_P), COLS * EDGE_P)], rows, S["iota_p"][:, 0:1], None, ALU.is_equal).then_inc(s_rused, 1)
                    assert step.n == IN_A

                with dve.Fori(0, TURNS // 2) as u:
                    for h in range(2):
                        turn(u * 2 + h, h, u)
                turn(TURNS - 1, 0, TURNS // 2)
                step = Chain(dve, s_v, n0 + TURNS * IN_A)
                dve.wait_ge(s_rused, TURNS)
                step(dve.memset(zeros, 0.0))
                dve.wait_ge(s_hist, TURNS)
                step(dve.tensor_reduce(S["deg2"][:, :], hist[:, :, :].rearrange("p t n -> p n t"), AX.X, ALU.add))
                dve.nop().then_inc(s_deg, 1)
                dve.wait_ge(s_pre, 1)
                starts(dve, step, S["start2"], tot, cum, zeros, psS[:, 0:NB], psS[:, 64:64 + NB])
                base = step.base + step.n
                with dve.Fori(0, NB) as b:
                    step = Chain(dve, s_v, b * IN_B + base)
                    one = hist[:, :, bass.ds(b, 1)].rearrange("p t a -> p (t a)")
                    to = lambda h: before[h][:, :, bass.ds(b, 1)].rearrange("p t a -> p (t a)")
                    step(dve.tensor_tensor_scan(scan[:, 0, :], one, zeros, S["start2"][:, bass.ds(b, 1)], ALU.add, ALU.add))
                    step(dve.tensor_tensor(scan[:, 1, :], scan[:, 0, :], one, ALU.subtract))
                    step(dve.tensor_scalar(to(0), scan[:, 1, :], 0.0, None, ALU.add))
                    step(dve.tensor_tensor(to(1), scan[:, 1, :], to(0), ALU.subtract))
                    assert step.n == IN_B
                dve.nop().then_inc(s_bf, 1)
                base = base + IN_B * NB

                def found(g, h):
                    step = Chain(dve, s_v, g * 3 + base)
                    step(one_hot_hi(g, h))
                    hold(dve, s_L, g + 1)
                    step(dve.tensor_tensor(look[:, :, :], psL[h][0:EDGE_P, 0:COLS * NB].rearrange("p (j n) -> p j n", n=NB),
                                           oh_hi[:, h, :, :], ALU.mult))
                    dve.nop().then_inc(s_lk, 1)
                    dve.nop(nofuse=True)
                    step(dve.tensor_reduce(place[:, bass.ds(g * COLS, COLS)], look[:, :, :], AX.X, ALU.add))
                with dve.Fori(0, TURNS // 2) as u:
                    for h in range(2):
                        found(u * 2 + h, h)
                found(TURNS - 1, 0)
                step = Chain(dve, s_v, base + 3 * TURNS)
                step(dve.tensor_tensor(place, place, above[:, :], ALU.add))
                step(dve.tensor_copy(S["place_i"][:, :], place))
        ph.close()


def starts(dve, step, start, tot, cum, zeros, ps_within, ps_tot):
    step(dve.tensor_copy(tot[:, :], ps_tot))
    step(dve.tensor_tensor_scan(cum[:, :], tot[:, :], zeros[:, 0:NB], 0.0, ALU.add, ALU.add))
    step(dve.tensor_tensor(cum[:, :], cum[:, :], tot[:, :], ALU.subtract))
    step(dve.tensor_tensor(start[:, :], cum[:, :], ps_within, ALU.add))


class RowScatter:

    def __init__(self, ph, S, A, first, turns):
        self.S, self.first, self.turns = S, first, turns
        self.row = ph.sb("row", [EDGE_P, ROW_RING, HERE, SROW])
        self.idx = ph.sb("row_idx", [EDGE_P, ROW_RING, HERE], I32)
        self.loaded = [ph.sem(f"row_loaded{k}") for k in range(ROW_RING)]
        self.stored = [ph.sem(f"row_stored{k}") for k in range(ROW_RING)]
        self.cleared = ph.sem("rows_cleared")
        self.features = A["edge_attr_64"].rearrange("(t p) f -> p t f", p=EDGE_P)

    def clear(self, dve):
        dve.memset(self.row[:, :, :, :], 0.0).then_inc(self.cleared, 1)

    def load(self, sp):
        sp.wait_ge(self.cleared, 1)
        with sp.Fori(0, self.turns) as t:
            for k in range(ROW_RING):
                at = bass.ds((t * ROW_RING + (self.first * ROW_RING + k)) * HERE, HERE)
                hold(sp, self.stored[k], t * (16 * HERE))
                sp.dma_start(self.row[:, k, :, 0:ED], self.features[:, at, :]).then_inc(self.loaded[k], 16)
                sp.dma_start(self.row[:, k, :, ED], self.S["dst_f"][:, at], allow_slow_non_contiguous=True).then_inc(self.loaded[k], 16)
                sp.dma_start(self.idx[:, k, :], self.S["place_i"][:, at]).then_inc(self.loaded[k], 16)

    def scatter(self, pool):
        with pool.Fori(0, self.turns) as t:
            for k in range(ROW_RING):
                hold(pool, self.loaded[k], (t + 1) * 48)
                for j in range(HERE):
                    pool.indirect_dma_start(
                        out=self.S["sorted_d"][:, :], out_offset=bass.IndirectOffsetOnAxis(ap=self.idx[:, k, j:j + 1], axis=0),
                        in_=self.row[:, k, j, :], in_offset=None).then_inc(self.stored[k], 16)

    def finish(self, pool):
        for k in range(ROW_RING):
            pool.wait_ge(self.stored[k], self.turns * HERE * 16)


def order_nodes(nc, S, A):
    with ExitStack() as ctx:
        ph = Phase(nc, ctx, "order")
        part_i = ph.sb("part_i", [EDGE_P, EDGE_C], I32)
        dlo = ph.sb("dlo", [EDGE_P, EDGE_C], BF16)
        dhi = ph.sb("dhi", [EDGE_P, EDGE_C], BF16)
        iota_b = ph.sb("iota_b", [P, P], BF16)
        node_of = ph.sb("node_of", [P, NB])
        PARTS = 5
        PC = EDGE_C // PARTS
        onehot_hi = ph.sb("onehot_hi", [EDGE_P, EDGE_C, NB], BF16)
        rows = RowScatter(ph, S, A, 0, ROW_EARLY)
        pad = ph.sb("pad", [NQ * QE - N_EDGES, SROW])
        s_clear, s_pd = (ph.sem(n) for n in ("pad_cleared", "pad_stored"))
        flat = S["state"]
        W = PC * P
        onehot_lo = flat[0:EDGE_P, 0:W].bitcast(BF16).rearrange("p (a c n) -> p a c n", a=2, n=P)
        diag = flat[:, W:W + NL].rearrange("p (b n) -> p b n", n=P)
        keyrow = flat[:, W + NL:W + 2 * NL]
        above = flat[:, W + 2 * NL:W + 3 * NL]
        zeros = ph.sb("zeros_b", [EDGE_P, P], BF16)
        deg = ph.sb("deg", [P, NB])
        tot = ph.sb("tot", [P, NB])
        cum = ph.sb("cum", [P, NB])
        zrow = ph.sb("zrow", [P, NB])
        start = ph.sb("start", [P, NB])
        w0 = ph.sb("w0", [P, NB])
        w1 = ph.sb("w1", [P, NB])
        i0 = ph.sb("i0", [P, NB], I32)
        i1 = ph.sb("i1", [P, NB], I32)
        q0 = ph.sb("q0", [P, 2, NB])
        nq = ph.sb("nq", [P, 2, NB])
        key = ph.sb("key", [P, NB])
        pos = ph.sb("pos", [P, NB])
        pos_i = ph.sb("pos_i", [P, NB], I32)
        lane_w = ph.sb("lane_w", [P, NB, LANE], I32)
        lane_f = ph.sb("lane_f", [P, NB, LANE])
        wide = ph.sb("wide", [P, 64])
        mcol = ph.sb("mcol", [64, 1])
        mcols = ph.sb("mcols", [64, P])
        mrow = ph.sb("mrow", [P, 64])
        mend = ph.sb("mend", [P, 2, NB])
        lane_q = ph.sb("lane_q", [P, 3, NB])
        pk = ph.ps("pk", [P, 7 * 512])
        ph_ = ph.ps("phist", [P, 512])

        s_iota, s_v, s_part, s_used = (ph.sem(n) for n in ("iota_done", "dve_step", "part_ready", "part_used"))
        s_deg, s_pre, s_diag, s_key, s_keyrow = (ph.sem(n) for n in (
            "deg_ready", "prefix_done", "diag_ready", "key_spread", "keyrow_ready"))
        s_lane, s_scat, s_back, s_m, s_mt, s_mr, s_md = (ph.sem(n) for n in (
            "lanes_ready", "lanes_scattered", "lanes_loaded", "quads_ready", "quads_turned",
            "mcol_ready", "mrow_done"))

        with nc.Block() as block:
            @block.sync
            def _(sp):
                sp.wait_ge(s_clear, 1)
                sp.dma_start(S["sorted_d"][N_EDGES:NQ * QE, :], pad[:, :]).then_inc(s_pd, 16)
                rows.load(sp)
                sp.wait_ge(s_scat, 16 * NB)
                sp.dma_start(S["lane_i"][:, :, :], S["lane_d"].rearrange("(b p) f -> p b f", p=P)).then_inc(s_back, 16)
                sp.wait_ge(s_pd, 16)

            @block.gpsimd
            def _(pool):
                kw = dict(allow_small_or_imprecise_dtypes=True)
                pool.iota(iota_b[:, :], [[1, P]], base=0, channel_multiplier=0, **kw).then_inc(s_iota, 1)
                pool.iota(node_of[:, :], [[P, NB]], base=0, channel_multiplier=1, **kw).then_inc(s_iota, 1)
                rows.scatter(pool)
                pool.wait_ge(s_lane, 1)
                for b in range(NB):
                    pool.indirect_dma_start(
                        out=S["lane_d"][:, :], out_offset=bass.IndirectOffsetOnAxis(ap=pos_i[:, b:b + 1], axis=0),
                        in_=lane_w[:, b, :], in_offset=None).then_inc(s_scat, 16)
                rows.finish(pool)

            @block.vector
            def _(dve):
                step = Chain(dve, s_v)
                step(dve.memset(pad[:, :], 0.0))
                dve.nop().then_inc(s_clear, 1)
                rows.clear(dve)
                dve.wait_ge(s_iota, 2)
                step(dve.memset(zrow[:, :], 0.0))
                step(dve.memset(zeros[:, :], 0.0))
                step(dve.tensor_scalar(part_i[:, :], S["dst_i"][:, :], P - 1, None, ALU.bitwise_and))
                step(dve.tensor_copy(dlo[:, :], part_i[:, :]))
                step(dve.tensor_scalar(part_i[:, :], S["dst_i"][:, :], 7, None, ALU.logical_shift_right))
                step(dve.tensor_copy(dhi[:, :], part_i[:, :]))
                step(dve.tensor_tensor(onehot_hi[:, :, :], bc(iota_b[0:EDGE_P, 0:NB], 1, [EDGE_P, EDGE_C, NB]),
                                       bc(dhi[:, :], 2, [EDGE_P, EDGE_C, NB]), ALU.is_equal))
                for c in range(PARTS):
                    if c >= 2:
                        dve.wait_ge(s_used, c - 1)
                    dve.tensor_tensor(onehot_lo[:, c % 2, :, :], bc(iota_b[0:EDGE_P, :], 1, [EDGE_P, PC, P]),
                                      bc(dlo[:, c * PC:(c + 1) * PC], 2, [EDGE_P, PC, P]),
                                      ALU.is_equal).then_inc(s_part, 1)
                dve.wait_ge(s_used, PARTS)
                step(dve.tensor_copy(deg[:, :], ph_[:, 0:NB]))
                dve.nop().then_inc(s_deg, 1)
                dve.wait_ge(s_pre, 1)
                starts(dve, step, start, tot, cum, zrow, ph_[:, 64:64 + NB], ph_[:, 128:128 + NB])
                for i, (st, dg) in enumerate(((start, deg), (S["start2"], S["deg2"]))):
                    step(dve.tensor_copy(i0[:, :], st[:, :]))
                    step(dve.tensor_scalar(i1[:, :], i0[:, :], 2, None, ALU.logical_shift_right))
                    step(dve.tensor_copy(q0[:, i, :], i1[:, :]))
                    step(dve.tensor_tensor(w0[:, :], st[:, :], dg[:, :], ALU.add))
                    step(dve.tensor_scalar(w0[:, :], w0[:, :], -1.0, 0.0, ALU.add, ALU.max))
                    step(dve.tensor_copy(i0[:, :], w0[:, :]))
                    step(dve.tensor_scalar(i1[:, :], i0[:, :], 2, None, ALU.logical_shift_right))
                    step(dve.tensor_copy(w1[:, :], i1[:, :]))
                    step(dve.tensor_tensor(nq[:, i, :], w1[:, :], q0[:, i, :], ALU.subtract))
                    step(dve.tensor_scalar(w0[:, :], dg[:, :], 0.0, None, ALU.is_gt))
                    step(dve.scalar_tensor_tensor(nq[:, i, :], nq[:, i, :], 1.0, w0[:, :], ALU.add, ALU.mult))
                step(dve.scalar_tensor_tensor(key[:, :], nq[:, 0, :], KEY_MAIN, nq[:, 1, :], ALU.mult, ALU.add))
                step(dve.tensor_scalar(key[:, :], key[:, :], float(KEY_CAP), float(KEY_STEP), ALU.min, ALU.mult))
                step(dve.tensor_tensor(key[:, :], key[:, :], node_of[:, :], ALU.subtract))
                step(dve.tensor_scalar(key[:, :], key[:, :], float(KEY_STEP - 1), None, ALU.add))
                dve.tensor_tensor(diag, bc(S["ident"][:, :], 1, [P, NB, P]),
                                  bc(key[:, :], 2, [P, NB, P]), ALU.mult).then_inc(s_diag, 1)
                dve.wait_ge(s_keyrow, 1)
                for b in range(NB):
                    step(dve.tensor_scalar(above, keyrow, key[:, b:b + 1], 0.0, ALU.is_gt, ALU.add,
                                           accum_out=pos[:, b:b + 1]))
                step(dve.tensor_copy(pos_i[:, :], pos[:, :]))
                for c, v in enumerate((node_of[:, :], start[:, :], deg[:, :], q0[:, 0, :], nq[:, 0, :],
                                       S["start2"][:, :], S["deg2"][:, :], q0[:, 1, :], nq[:, 1, :])):
                    step(dve.tensor_copy(lane_w[:, :, c], v))
                dve.nop().then_inc(s_lane, 1)
                dve.wait_ge(s_back, 16)
                step(dve.tensor_copy(lane_f[:, :, :], S["lane_i"][:, :, :]))
                step(dve.tensor_copy(S["deg_l"][:, :], lane_f[:, :, 2]))
                step(dve.memset(wide[:, :], 0.0))
                for i in range(2):
                    step(dve.tensor_copy(wide[:, 32 * i:32 * i + NB], lane_f[:, :, 4 + 4 * i]))
                dve.nop().then_inc(s_m, 1)
                dve.wait_ge(s_mt, 1)
                step(dve.tensor_reduce(mcol[:, :], ph_[0:64, 192:192 + P], AX.X, ALU.max))
                step(dve.tensor_scalar(mcol[:, :], mcol[:, :], 1.0, None, ALU.max))
                step(dve.tensor_scalar(mcols[:, :], S["ones"][0:64, :], mcol[:, 0:1], None, ALU.mult))
                dve.nop().then_inc(s_mr, 1)
                dve.wait_ge(s_md, 1)
                step(dve.tensor_copy(mrow[:, :], ph_[:, 384:448]))
                for i in range(2):
                    m, me, lq = mrow[:, 32 * i:32 * i + NB], mend[:, i, :], lane_q
                    step(dve.tensor_tensor_scan(me, m, zrow[:, :], 0.0, ALU.add, ALU.add))
                    step(dve.tensor_tensor(w0[:, :], me, m, ALU.subtract))
                    first, begin, count = (lane_f[:, :, 4 * i + j] for j in (3, 1, 2))
                    step(dve.tensor_tensor(lq[:, 0, :], first, w0[:, :], ALU.subtract))
                    step(dve.tensor_copy(lq[:, 1, :], begin))
                    step(dve.tensor_tensor(lq[:, 2, :], begin, count, ALU.add))
                    step(dve.tensor_copy(S[f"block_at{i}"][:, :], w0[:, :]))
                    step(dve.tensor_copy(S[f"lane_dq{i}"][:, :, 0], lq[:, :, 0]))
                    step(dve.tensor_tensor(S[f"lane_dq{i}"][:, :, 1:NB], lq[:, :, 1:NB], lq[:, :, 0:NB - 1], ALU.subtract))
                    step(dve.tensor_scalar(w1[:, 0:1], mend[:, i, NB - 1:NB], float(AQ - 1), None, ALU.add))
                    step(dve.tensor_copy(i0[:, 0:1], w1[:, 0:1]))
                    step(dve.tensor_scalar(S[f"turns{i}"][:, :], i0[:, 0:1], AQ.bit_length() - 1, None, ALU.logical_shift_right))
                    step(dve.tensor_scalar(w1[:, 0:1], mend[:, i, NB - 1:NB], float(2 * HALF - 1), None, ALU.add))
                    step(dve.tensor_copy(i0[:, 0:1], w1[:, 0:1]))
                    step(dve.tensor_scalar(S[f"rec_turns{i}"][:, :], i0[:, 0:1], (2 * HALF).bit_length() - 1, None, ALU.logical_shift_right))
            @block.tensor
            def _(pe):
                pe.wait_ge(s_part, 1)
                pe.matmul(ph_[:, 0:NB], zeros[:, :], onehot_hi[:, 0, :], start=True, stop=False)
                for c in range(PARTS):
                    pe.wait_ge(s_part, c + 1)
                    with pe.Fori(0, PC // HERE) as t:
                        for u in range(HERE):
                            pe.matmul(ph_[:, 0:NB],
                                      onehot_lo[:, c % 2, bass.ds(t * HERE + u, 1), :].rearrange("p a f -> p (a f)"),
                                      onehot_hi[:, bass.ds(t * HERE + (c * PC + u), 1), :].rearrange("p a f -> p (a f)"),
                                      start=False, stop=False)
                    pe.matmul(ph_[:, 0:NB], zeros[:, :], onehot_hi[:, 0, :], start=False,
                              stop=(c == PARTS - 1)).then_inc(s_used, 1)
                pe.wait_ge(s_deg, 1)
                pe.matmul(ph_[:, 64:64 + NB], S["tri"][:, :], deg[:, :], start=True, stop=True)
                pe.matmul(ph_[:, 128:128 + NB], S["ones"][:, :], deg[:, :], start=True, stop=True).then_inc(s_pre, 1)
                pe.wait_ge(s_diag, 1)
                for b in range(NB):
                    last = pe.matmul(pk[:, b * P:(b + 1) * P], S["ones"][:, :], diag[:, b, :], start=True, stop=True)
                last.then_inc(s_key, 1)
                pe.wait_ge(s_m, 1)
                pe.transpose(ph_[0:64, 192:192 + P], wide[:, :], S["ident"][:, :]).then_inc(s_mt, 1)
                pe.wait_ge(s_mr, 1)
                pe.matmul(ph_[:, 384:448], mcols[:, :], S["ident"][0:64, 0:64], start=True, stop=True).then_inc(s_md, 1)

            @block.scalar
            def _(act):
                act.wait_ge(s_key, 1)
                act.activation(keyrow, pk[:, 0:NB * P], ACT.Copy).then_inc(s_keyrow, 1)
        ph.close()


def build_records(nc, S, A, i):
    with ExitStack() as ctx:
        ph = Phase(nc, ctx, f"rec{i}")
        GOT = (2 * QE, QE * SROW)[i]
        of = (A["edge_q"], S["sorted_d"].rearrange("(q e) f -> q (e f)", e=QE).bitcast(I32))[i]
        got = S["big2"].rearrange("p b f -> p (b f)")[:, 0:2 * HALF * GOT].bitcast(I32).rearrange("p (h k f) -> p h k f", h=2, f=GOT)
        place = ph.sb("place", [P, 2, HALF])
        slot = ph.sb("slot", [P, HALF, QE])
        begun = ph.sb("begun", [P, HALF, NB])
        terms = ph.sb("terms", [P, 3, HALF, NB])
        cols = ph.sb("cols", [P, 2, 3, HALF])
        block_f = ph.sb("block_f", [P, 2, HALF])
        quad = ph.sb("quad", [P, 2, HALF])
        quad_c = ph.sb("quad_c", [P, HALF])
        quad_i = ph.sb("quad_i", [P, 2, HALF], I32)
        edge = ph.sb("edge", [P, HALF, QE])
        valid = ph.sb("valid", [P, HALF, QE])
        below = ph.sb("below", [P, HALF, QE])
        src_f = ph.sb("src_f", [P, HALF, QE])
        rec = ph.sb("rec_w", [P, 2, HALF, REC], I32)
        rec_f = rec[:, :, :, :].bitcast(F32)
        s_iota, s_v, s_idx, s_rec = (ph.sem(n) for n in ("iota_done", "dve_step", "index_ready", "record_ready"))
        s_got, s_st = ([ph.sem(f"{n}{h}") for h in range(2)] for n in ("edges_gathered", "records_stored"))
        turns = lambda eng: eng.value_load(S[f"rec_turns{i}"][0:1, 0:1], min_val=1, max_val=NG_PAD // (2 * HALF))
        FIND, MAKE = 8, 12 + (i == 0)
        CH = 2 * (FIND + MAKE)

        with nc.Block() as block:
            @block.sync
            def _(sp):
                n = turns(sp)
                with sp.Fori(0, n) as t:
                    for h in range(2):
                        sp.wait_ge(s_rec, t * 2 + (h + 1))
                        sp.dma_start(S[f"rec_d{i}"][bass.ds((t * 2 + h) * HALF, HALF), :, :].rearrange("k p f -> p k f"),
                                     rec[:, h, :, :]).then_inc(s_st[h], 16)
                for h in range(2):
                    hold(sp, s_st[h], n * 16)

            @block.gpsimd
            def _(pool):
                kw = dict(allow_small_or_imprecise_dtypes=True)
                pool.iota(place[:, :, :], [[HALF, 2], [1, HALF]], base=0, channel_multiplier=0, **kw).then_inc(s_iota, 1)
                pool.iota(slot[:, :, :], [[0, HALF], [1, QE]], base=0, channel_multiplier=0, **kw).then_inc(s_iota, 1)
                n = turns(pool)
                with pool.Fori(0, n) as t:
                    for h in range(2):
                        hold(pool, s_idx, t * 2 + (h + 1))
                        for k in range(HALF):
                            pool.indirect_dma_start(
                                out=got[:, h, k, :], out_offset=None, in_=of,
                                in_offset=bass.IndirectOffsetOnAxis(ap=quad_i[:, h, k:k + 1], axis=0)).then_inc(s_got[h], 16)

            @block.vector
            def _(dve):
                def find(step, h):
                    where = place[:, h, :]
                    step(dve.tensor_tensor(begun[:, :, :], bc(where, 2, [P, HALF, NB]), bc(S[f"block_at{i}"][:, :], 1, [P, HALF, NB]), ALU.is_ge))
                    for c in range(3):
                        last = dve.tensor_tensor(terms[:, c, :, :], begun[:, :, :], bc(S[f"lane_dq{i}"][:, c, :], 1, [P, HALF, NB]), ALU.mult)
                    step(last)
                    dve.tensor_reduce(block_f[:, h, :], begun[:, :, :], AX.X, ALU.add)
                    step(dve.tensor_reduce(cols[:, h, :, :], terms[:, :, :, :], AX.X, ALU.add))
                    step(dve.tensor_tensor(quad[:, h, :], where, cols[:, h, 0, :], ALU.add))
                    step(dve.tensor_scalar(quad_c[:, :], quad[:, h, :], float(NQ - 1), None, ALU.min))
                    step(dve.tensor_copy(quad_i[:, h, :], quad_c[:, :]))
                    dve.nop().then_inc(s_idx, 1)
                    step(dve.tensor_scalar(where, where, float(2 * HALF), None, ALU.add))
                    step(dve.tensor_scalar(block_f[:, h, :], block_f[:, h, :], -1.0, None, ALU.add))

                def make(step, t, h):
                    wide = [P, HALF, QE]
                    dve.wait_ge(s_st[h], t * 16)
                    step(dve.tensor_copy(rec[:, h, :, R_QUAD], quad_i[:, h, :]))
                    step(dve.tensor_copy(rec[:, h, :, R_BLOCK], block_f[:, h, :]))
                    step(dve.scalar_tensor_tensor(edge[:, :, :], bc(quad[:, h, :], 2, wide), float(QE), slot[:, :, :], ALU.mult, ALU.add))
                    step(dve.tensor_tensor(valid[:, :, :], edge[:, :, :], bc(cols[:, h, 1, :], 2, wide), ALU.is_ge))
                    step(dve.tensor_tensor(below[:, :, :], edge[:, :, :], bc(cols[:, h, 2, :], 2, wide), ALU.is_lt))
                    step(dve.tensor_tensor(valid[:, :, :], valid[:, :, :], below[:, :, :], ALU.mult))
                    step(dve.tensor_scalar(rec_f[:, h, :, R_MASK:R_MASK + QE], valid[:, :, :], BIG, -BIG, ALU.mult, ALU.add))
                    dve.wait_ge(s_got[h], (t + 1) * (16 * HALF))
                    if i == 0:
                        step(dve.tensor_copy(rec_f[:, h, :, R_REL:R_REL + QE], got[:, h, :, QE:2 * QE]))
                    rows = got[:, h, :, 0:QE] if i == 0 else got[:, h, :, :].rearrange("p k (e f) -> p k e f", e=QE)[:, :, :, ED].bitcast(F32)
                    step(dve.tensor_copy(src_f[:, :, :], rows))
                    step(dve.scalar_tensor_tensor(src_f[:, :, :], src_f[:, :, :], float(-DUMMY), valid[:, :, :], ALU.add, ALU.mult))
                    step(dve.tensor_scalar(src_f[:, :, :], src_f[:, :, :], float(DUMMY), None, ALU.add))
                    step(dve.tensor_copy(rec[:, h, :, R_SRC:R_SRC + QE], src_f[:, :, :]))
                    step(dve.nop())
                    dve.nop().then_inc(s_rec, 1)

                pre = Chain(dve, s_v)
                dve.wait_ge(s_iota, 2)
                pre(dve.memset(rec[:, :, :, :], 0))
                n = turns(dve)
                find(pre, 0)
                with dve.Fori(0, n) as t:
                    step = Chain(dve, s_v, t * CH + (1 + FIND))
                    find(step, 1)
                    make(step, t, 0)
                    find(step, 0)
                    make(step, t, 1)
                    assert step.n == CH, (step.n, CH)
        ph.close()


def shared(nc, ctx):
    S = {}

    def sb(name, shape, dt=F32):
        S[name] = ctx.enter_context(nc.sbuf_tensor(name, shape, dt))

    def dram(name, shape, dt=F32):
        S[name] = nc.dram_tensor(name, shape, dt).ap()

    sb("state", [P, 6 * NB * D])
    part = lambda a, b: S["state"][:, a * NB * D:b * NB * D].rearrange("p (b f) -> p b f", b=NB)
    S["X"] = part(0, 1)
    S["H"] = part(1, 2)
    S["big"] = part(2, 4)
    S["big2"] = part(4, 6)
    sb("iota_c", [P, P])
    sb("iota_p", [P, 1])
    sb("ident", [P, P])
    sb("ones", [P, P])
    sb("lane_i", [P, NB, LANE], I32)
    sb("deg_l", [P, NB])
    for i in range(2):
        sb(f"block_at{i}", [P, NB])
        sb(f"lane_dq{i}", [P, 3, NB])
        sb(f"turns{i}", [P, 1], I32)
        sb(f"rec_turns{i}", [P, 1], I32)
    sb("adst", [P, NB])
    sb("m", [P, NB, 8])
    sb("l", [P, NB, 8])
    sb("dst_f", [EDGE_P, EDGE_C])
    sb("place_i", [EDGE_P, EDGE_C], I32)
    dram("lane_d", [NL, LANE], I32)
    dram("sorted_d", [NQ * QE, SROW])
    for i in range(2):
        dram(f"rec_d{i}", [NG_PAD, P, REC], I32)
    dram("tab0", [NL + 1, D2])
    dram("tab1", [NL + 1, D2])
    dram("tab2", [NL + 1, D2])
    dram("tab3", [NL + 1, XROW])
    return S


def shared_by_lists(nc, ctx, S):
    def sb(name, shape, dt=F32):
        S[name] = ctx.enter_context(nc.sbuf_tensor(name, shape, dt))

    sb("src_i", [EDGE_P, EDGE_C], I32)
    sb("dst_i", [EDGE_P, EDGE_C], I32)
    sb("tri", [P, P])
    sb("deg2", [P, NB])
    sb("start2", [P, NB])


def uses(t, q, ring):
    return t * (AQ // ring) + (q // ring + 1)


def hold(eng, sem, value):
    eng.wait_ge(sem, value)
    eng.nop(nofuse=True)


def rows_of(ap, n):
    return ap.rearrange("(a n) -> a n", a=1).broadcast_to([P, n])


def all_heads(ap, heads):
    return ap.rearrange("p b (h d) -> p b h d", h=heads)


def norm_begin(dve, step, src, dst, stat, wide):
    step(dve.tensor_reduce(stat[:, 0, :], src, AX.X, ALU.add))
    step(dve.tensor_scalar(stat[:, 0, :], stat[:, 0, :], 1.0 / D, None, ALU.mult))
    step(dve.tensor_tensor(dst, src, bc(stat[:, 0, :], 2, [P, NB, D]), ALU.subtract))
    step(dve.tensor_tensor(wide, dst, dst, ALU.mult))
    step(dve.tensor_reduce(stat[:, 1, :], wide, AX.X, ALU.add))
    step(dve.tensor_scalar(stat[:, 1, :], stat[:, 1, :], 1.0 / D, EPS, ALU.mult, ALU.add))


def norm_end(dve, step, dst, stat):
    step(dve.reciprocal(stat[:, 3, :], stat[:, 2, :]))
    step(dve.tensor_tensor(dst, dst, bc(stat[:, 3, :], 2, [P, NB, D]), ALU.mult))


def layer_input(dve, step, S, stat, wide, s_var, s_root, n):
    norm_begin(dve, step, S["X"][:, :, :], S["H"][:, :, :], stat, wide)
    dve.nop().then_inc(s_var, 1)
    dve.wait_ge(s_root, n)
    norm_end(dve, step, S["H"][:, :, :], stat)
    step(dve.tensor_scalar(S["H"][:, :, :], S["H"][:, :, :], 0.0, None, ALU.max))


def take_root(act, stat, s_var, s_root, n):
    act.wait_ge(s_var, n)
    act.activation(stat[:, 2, :], stat[:, 1, :], ACT.Sqrt).then_inc(s_root, 1)


def fetch_nodes(nc, S, A):
    with ExitStack() as ctx:
        ph = Phase(nc, ctx, "fetch")
        row = ph.sb("row", [P, NB], I32)
        row_f = ph.sb("row_f", [P, NB])
        s_row, s_x, s_v = (ph.sem(n) for n in ("rows_ready", "x_loaded", "dve_step"))
        with nc.Block() as block:
            @block.vector
            def _(dve):
                step = Chain(dve, s_v)
                step(dve.tensor_copy(row_f[:, :], S["lane_i"][:, :, 0]))
                step(dve.tensor_scalar(row_f[:, :], row_f[:, :], float(N_NODES - 1), None, ALU.min))
                dve.tensor_copy(row[:, :], row_f[:, :]).then_inc(s_row, 1)

            @block.gpsimd
            def _(pool):
                pool.wait_ge(s_row, 1)
                for b in range(NB):
                    pool.indirect_dma_start(out=S["X"][:, b, :], out_offset=None, in_=A["x"][:, :],
                                            in_offset=bass.IndirectOffsetOnAxis(ap=row[:, b:b + 1], axis=0)).then_inc(s_x, 16)
                pool.wait_ge(s_x, 16 * NB)
        ph.close()


def make_tables(nc, S, A, layer):
    heads = (1, 4, 8, 1)[layer]
    gat = layer == 3
    L = ("L0_gnn_", "L1_gnn_", "L2_gnn_", "L3_gnn_")[layer]
    NA = D + 2 if gat else D2
    NO = {0: D2, 1: D, 2: D, 3: 0}[layer]
    ROW = XROW if gat else D2
    tab = S[f"tab{layer}"]
    scale = {0: 1.0, 1: 64 ** -0.5, 2: 32 ** -0.5, 3: 1.0}[layer]
    with ExitStack() as ctx:
        ph = Phase(nc, ctx, f"make{layer}")
        stat = ph.sb("stat", [P, 4, NB])
        wide = S["big2"][:, :, 0:D]
        hst = ph.sb("hst", [P, D])
        hT = ph.sb("hT", [P, 2, P])
        w_row = ph.sb("w_row", [P, 2, NA])
        b_row = ph.sb("b_row", [P, NA])
        w_own = ph.sb("w_own", [P, 2, max(NO, 1)])
        b_own = ph.sb("b_own", [P, max(NO, 1)])
        row = ph.sb("row", [P, ROW])
        prod = ph.sb("prod", [P, D])
        prod2 = ph.sb("prod2", [P, 2, D if gat else 1])
        idx = ph.sb("idx", [P, 1], I32)
        empty = ph.sb("empty", [P, NB])
        last_row = ph.sb("last_row", [1, ROW])
        qe = ph.sb("qe", [P, 2])
        att = ph.sb("att", [P, 2, D])
        term = ph.sb("term", [P, 1])
        w_nat = ph.sb("w_nat", [P, 2, D])
        psT = ph.ps("psT", [P, 512])
        psA = ph.ps("psA", [P, 512])
        psB = ph.ps("psB", [P, 512])
        psW = ph.ps("psW", [P, 512])
        s_w, s_v, s_var, s_root, s_wr, s_h, s_hst, s_T, s_hT, s_A, s_B, s_row, s_own, s_scat, s_dummy, s_wT, s_lr = (
            ph.sem(n) for n in ("weights_loaded", "dve_step", "var_ready", "root_ready", "weights_ready",
                                "h_ready", "h_staged", "h_turned", "hT_ready", "row_sums", "own_sums",
                                "row_ready", "own_ready", "row_stored", "dummy_stored", "w_turned", "dummy_ready"))
        n_loads = {0: 3, 1: 7, 2: 6, 3: 3}[layer]
        keeps = 3 * gat
        IN_LOOP = {0: 0, 1: 1, 2: 1, 3: 3}[layer]

        with nc.Block() as block:
            @block.sync
            def _(sp):
                def load(to, of):
                    sp.dma_start(to, of, allow_slow_non_contiguous=True).then_inc(s_w, 16)
                chunks = lambda ap: ap.rearrange("(c p) n -> p c n", p=P)
                if layer == 0:
                    w = chunks(A[L + "eW1"][0:2 * D, :])
                    load(w_row[:, :, :], w[:, 0:2, :])
                    load(w_own[:, :, :], w[:, 2:4, :])
                    load(b_own[:, :], rows_of(A[L + "eb1"], D2))
                elif not gat:
                    load(w_row[:, :, 0:D], chunks(A[L + "Wk"]))
                    load(w_row[:, :, D:D2], chunks(A[L + "Wv"]))
                    load(w_own[:, :, :], chunks(A[L + "Wq"]))
                    load(b_row[:, 0:D], rows_of(A[L + "bk"], D))
                    load(b_row[:, D:D2], rows_of(A[L + "bv"], D))
                    load(b_own[:, :], rows_of(A[L + "bq"], D))
                    if layer == 1:
                        load(qe[:, :], A[L + "query_emb"].rearrange("(c p) -> p c", p=P))
                    if layer == 2:
                        load(prod[:, :], rows_of(A[L + "be"], D))
                else:
                    load(w_nat[:, :, :], chunks(A[L + "W"]))
                    load(att[:, 0, :], rows_of(A[L + "att_src"], D))
                    load(att[:, 1, :], rows_of(A[L + "att_dst"], D))
                sp.wait_ge(s_lr, 1)
                sp.dma_start(tab[DUMMY:DUMMY + 1, :], last_row[:, :]).then_inc(s_dummy, 16)
                sp.wait_ge(s_dummy, 16)

            @block.gpsimd
            def _(pool):
                pool.memset(last_row[:, :], LOW if layer == 0 else 0.0).then_inc(s_lr, 1)
                if layer in (0, 2):
                    pool.memset(S["big"][:, :, :] if layer == 0 else S["big"][:, :, D:D2], 0.0)
                with pool.Fori(0, NB) as b:
                    hold(pool, s_row, b + 2)
                    pool.indirect_dma_start(out=tab[:, :], out_offset=bass.IndirectOffsetOnAxis(ap=idx[:, 0:1], axis=0),
                                            in_=row[:, :], in_offset=None).then_inc(s_scat, 16)
                pool.wait_ge(s_scat, 16 * NB)

            @block.scalar
            def _(act):
                take_root(act, stat, s_var, s_root, 1)
                act.wait_ge(s_h, 1)
                if layer == 1:
                    act.wait_ge(s_wr, 1)
                with act.Fori(0, NB) as b:
                    act.activation(hst[:, :], blk(S["H"], b), ACT.Copy).then_inc(s_hst, 1)
                    act.wait_ge(s_T, b + 1)
                    act.wait_ge(s_own, b + 1)
                    if layer == 1:
                        act.activation(hT[:, 0, :], psT[:, 0:P], ACT.Identity, bias=qe[:, 0:1])
                        act.activation(hT[:, 1, :], psT[:, P:D], ACT.Identity, bias=qe[:, 1:2]).then_inc(s_hT, 1)
                    else:
                        act.activation(hT[:, :, :], psT[:, 0:D].rearrange("p (c n) -> p c n", c=2), ACT.Copy).then_inc(s_hT, 1)

            @block.tensor
            def _(pe):
                pe.wait_ge(s_wr, 1)
                if gat:
                    for c in range(2):
                        for k in range(2):
                            last = pe.transpose(psW[:, (2 * k + c) * P:(2 * k + c + 1) * P], w_nat[:, c, k * P:(k + 1) * P], S["ident"][:, :])
                    last.then_inc(s_wT, 1)
                    pe.wait_ge(s_h, 1)
                with pe.Fori(0, NB) as b:
                    pe.wait_ge(s_hst, b + 1)
                    pe.transpose(psT[:, 0:P], hst[:, 0:P], S["ident"][:, :])
                    pe.transpose(psT[:, P:D], hst[:, P:D], S["ident"][:, :]).then_inc(s_T, 1)
                    pe.wait_ge(s_hT, b + 1)
                    pe.wait_ge(s_row, b + 1)
                    pe.matmul(psA[:, 0:NA], hT[:, 0, :], w_row[:, 0, :], start=True, stop=False)
                    pe.matmul(psA[:, 0:NA], hT[:, 1, :], w_row[:, 1, :], start=False, stop=True).then_inc(s_A, 1)
                    if NO:
                        pe.wait_ge(s_own, b + 1)
                        pe.matmul(psB[:, 0:NO], hT[:, 0, :], w_own[:, 0, :], start=True, stop=False)
                        pe.matmul(psB[:, 0:NO], hT[:, 1, :], w_own[:, 1, :], start=False, stop=True).then_inc(s_B, 1)

            @block.vector
            def _(dve):
                step = Chain(dve, s_v)
                dve.wait_ge(s_w, 16 * n_loads + 16 * (layer == 2))
                if not gat and layer:
                    step(dve.tensor_scalar(w_own[:, :, :], w_own[:, :, :], scale, None, ALU.mult))
                    step(dve.tensor_scalar(b_own[:, :], b_own[:, :], scale, None, ALU.mult))
                if layer == 1:
                    step(dve.tensor_scalar(qe[:, :], qe[:, :], 0.1, None, ALU.mult))
                if layer == 2:
                    step(dve.tensor_tensor(b_row[:, 0:D], b_row[:, 0:D], prod[:, :], ALU.add))
                dve.nop().then_inc(s_wr, 1)
                if gat:
                    dve.wait_ge(s_wT, 1)
                    step(dve.tensor_copy(w_row[:, :, 0:D], psW[:, :].rearrange("p (k n) -> p k n", k=2)))
                    for i in range(2):
                        step(dve.tensor_tensor(prod2[:, :, :], w_row[:, :, 0:D], bc(att[:, i, :], 1, [P, 2, D]), ALU.mult))
                        step(dve.tensor_reduce(w_row[:, :, D + i:D + i + 1], prod2[:, :, :], AX.X, ALU.add))
                    step(dve.memset(row[:, :], 0.0))
                step(dve.tensor_scalar(empty[:, :], S["deg_l"][:, :], 0.0, None, ALU.is_equal))
                layer_input(dve, step, S, stat, wide, s_var, s_root, 1)
                if layer in (1, 2):
                    step(dve.memset(S["m"][:, :, :], LOW))
                    step(dve.memset(S["l"][:, :, :], 0.0))
                if layer == 1:
                    step(dve.tensor_copy(S["l"][:, :, 0:heads], bc(empty[:, :], 2, [P, NB, heads])))
                if gat:
                    step(dve.memset(S["l"][:, :, :], 1.0))
                dve.nop().then_inc(s_h, 1)
                dve.nop().then_inc(s_row, 1)
                dve.nop().then_inc(s_own, 1)
                before = step.n
                with dve.Fori(0, NB) as b:
                    step = Chain(dve, s_v, b * IN_LOOP + before)
                    hold(dve, s_scat, b * 16)
                    dve.tensor_copy(idx[:, :], S["lane_i"][:, bass.ds(b, 1), 0])
                    dve.wait_ge(s_A, b + 1)
                    if layer == 0:
                        dve.tensor_copy(row[:, :], psA[:, :]).then_inc(s_row, 1)
                    elif not gat:
                        if layer == 1:
                            step(dve.tensor_tensor(row[:, :], psA[:, :], b_row[:, :], ALU.add))
                            dve.tensor_scalar(blk(S["big"], b)[:, D:D2], row[:, D:D2], empty[:, bass.ds(b, 1)], None, ALU.mult).then_inc(s_row, 1)
                        else:
                            dve.tensor_tensor(row[:, :], psA[:, :], b_row[:, :], ALU.add).then_inc(s_row, 1)
                            step(dve.nop())
                    else:
                        dve.tensor_copy(S["adst"][:, bass.ds(b, 1)], psA[:, D + 1:D + 2])
                        step(dve.tensor_copy(row[:, 0:D + 1], psA[:, 0:D + 1]))
                        step(dve.tensor_tensor(term[:, :], row[:, D:D + 1], psA[:, D + 1:D + 2], ALU.add))
                        step(dve.scalar_tensor_tensor(S["m"][:, bass.ds(b, 1), 0], term[:, :], 0.2, term[:, :], ALU.mult, ALU.max))
                        dve.tensor_copy(blk(S["big"], b)[:, D:D2], row[:, 0:D]).then_inc(s_row, 1)
                        dve.wait_ge(s_row, b + 2)
                        dve.nop().then_inc(s_own, 1)
                    if NO:
                        hold(dve, s_B, b + 1)
                        own = blk(S["big2"], b)[:, 0:D2] if layer == 0 else blk(S["big"], b)[:, 0:D]
                        dve.tensor_tensor(own, psB[:, 0:NO], b_own[:, 0:NO], ALU.add).then_inc(s_own, 1)
                    assert step.n == IN_LOOP, step.n
        ph.close()


def edge_mlp(nc, S, A):
    with ExitStack() as ctx:
        ph = Phase(nc, ctx, "edge0")
        rec = ph.sb("rec", [P, RING_0, REC], I32)
        feat = ph.sb("feat", [P, RING_0, QE * ED])
        featT = ph.sb("featT", [P, 2, 2, P])
        ring = ph.sb("ring", [P, RING_0, QE, D2])
        w_edge = ph.sb("w_edge", [P, D2])
        psT = [ph.ps(f"psT{i}", [P, 512]) for i in range(2)]
        psX = ph.ps("psX", [P, QE, D2])
        s_rec, s_done, s_feat = ([ph.sem(f"{n}{k}") for k in range(RING_0)] for n in ("rec_loaded", "quad_done", "feat_loaded"))
        s_g = [[ph.sem(f"rows{k}_{h}") for h in range(2)] for k in range(RING_0)]
        s_w, s_v, s_T, s_fT, s_x, s_xr = (ph.sem(n) for n in (
            "weights_loaded", "dve_step", "feat_turned", "featT_ready", "sums_ready", "sums_read"))
        turns = lambda eng: eng.value_load(S["turns0"][0:1, 0:1], min_val=1, max_val=NG_PAD // AQ)
        CH = AQ * (QE + 1)

        def block_of(eng, t, q):
            k = q % RING_0
            hold(eng, s_rec[k], uses(t, q, RING_0) * 16)
            return eng.value_load(rec[0:1, k, R_BLOCK:R_BLOCK + 1], min_val=0, max_val=NB - 1)

        with nc.Block() as block:
            @block.sync
            def _(sp):
                for h in range(2):
                    sp.dma_start(w_edge[h * ED:(h + 1) * ED, :], A["L0_gnn_eW1"][2 * D:2 * D + ED, :]).then_inc(s_w, 16)
                n = turns(sp)
                with sp.Fori(0, n) as t:
                    for q in range(AQ):
                        k = q % RING_0
                        sp.wait_ge(s_done[k], uses(t, q, RING_0))
                        sp.dma_start(rec[:, k, :], S["rec_d0"][bass.ds(t * AQ + q, 1), :, :].rearrange("a p f -> p (a f)")).then_inc(s_rec[k], 16)

            @block.gpsimd
            def _(pool):
                n = turns(pool)
                with pool.Fori(0, n) as t:
                    for q in range(AQ):
                        k = q % RING_0
                        hold(pool, s_rec[k], uses(t, q, RING_0) * 16)
                        pool.indirect_dma_start(out=feat[:, k, :], out_offset=None, in_=A["feat_q"][:, :],
                                                in_offset=bass.IndirectOffsetOnAxis(ap=rec[:, k, R_QUAD:R_QUAD + 1], axis=0)).then_inc(s_feat[k], 16)
                        for s in range(QE):
                            pool.indirect_dma_start(out=ring[:, k, s, :], out_offset=None, in_=S["tab0"][:, :],
                                                    in_offset=bass.IndirectOffsetOnAxis(ap=rec[:, k, R_SRC + s:R_SRC + s + 1], axis=0)).then_inc(s_g[k][s // 2], 16)

            @block.scalar
            def _(act):
                act.nop().then_inc(s_fT, 1)
                n = turns(act)
                with act.Fori(0, n) as t:
                    for q in range(AQ):
                        k = q % RING_0
                        act.wait_ge(s_T, t * AQ + (q + 1))
                        act.activation(featT[:, k % 2, :, :], psT[k % 2][:, 0:2 * P].rearrange("p (c n) -> p c n", c=2), ACT.Copy).then_inc(s_fT, 1)

            @block.tensor
            def _(pe):
                pe.wait_ge(s_w, 32)
                n = turns(pe)
                with pe.Fori(0, n) as t:
                    b = block_of(pe, t, 0)
                    for q in range(AQ):
                        k = q % RING_0
                        pe.wait_ge(s_feat[k], uses(t, q, RING_0) * 16)
                        pe.wait_ge(s_fT, t * AQ + (q + 1))
                        pe.transpose(psT[k % 2][:, 0:P], feat[:, k, 0:P], S["ident"][:, :])
                        pe.transpose(psT[k % 2][:, P:2 * P], feat[:, k, P:2 * P], S["ident"][:, :]).then_inc(s_T, 1)
                        for h in range(2):
                            pe.wait_ge(s_xr, t * (2 * AQ) + (2 * q + h + 1))
                            for i in range(2 - h):
                                pe.matmul(psX[:, 2 * h + i, :], S["ident"][:, :], blk(S["big2"], b), start=True, stop=False)
                            if h and q < AQ - 1:
                                b = block_of(pe, t, q + 1)
                            if h == 0:
                                pe.wait_ge(s_fT, t * AQ + (q + 2))
                            for i in range(2):
                                lo = ED * i
                                last = pe.matmul(psX[:, 2 * h + i, :], featT[lo:lo + ED, k % 2, h, :], w_edge[lo:lo + ED, :],
                                                 start=(h == 1 and i == 1), stop=True)
                            last.then_inc(s_x, 1)

            @block.vector
            def _(dve):
                dve.nop().then_inc(s_xr, 2)
                for k in range(RING_0):
                    dve.nop().then_inc(s_done[k], 1)
                n = turns(dve)
                with dve.Fori(0, n) as t:
                    step = Chain(dve, s_v, t * CH)
                    b_next = block_of(dve, t, 0)
                    for q in range(AQ):
                        k, b = q % RING_0, b_next
                        for h in range(2):
                            hold(dve, s_g[k][h], uses(t, q, RING_0) * 32)
                            both = ring[:, k, 2 * h:2 * h + 2, :]
                            if h == 1:
                                step(dve.tensor_tensor(ring[:, k, QE - 1, :], ring[:, k, QE - 1, :], blk(S["big2"], b), ALU.add))
                            dve.wait_ge(s_x, t * (2 * AQ) + (2 * q + h + 1))
                            dve.tensor_tensor(both, psX[:, 2 * h:2 * h + 2, :], both, ALU.add).then_inc(s_xr, 1)
                            if h and q < AQ - 1:
                                b_next = block_of(dve, t, q + 1)
                            dve.wait_ge(s_xr, t * (2 * AQ) + (2 * q + h + 3))
                            for s in (2 * h, 2 * h + 1):
                                step(dve.scalar_tensor_tensor(blk(S["big"], b), ring[:, k, s, :], 0.0, blk(S["big"], b), ALU.max, ALU.add))
                        dve.nop().then_inc(s_done[k], 1)
        ph.close()


def laid_out(inputs):
    a = {n: np.ascontiguousarray(v) for n, v in inputs.items()}
    pad = NQ * QE - N_EDGES
    src, rel, feat = a["src"], a.pop("edge_type_64"), a["edge_attr_64"]
    quads = lambda v: np.concatenate([v, np.zeros((pad,) + v.shape[1:], v.dtype)]).reshape(NQ, -1)
    a["edge_q"] = np.concatenate([quads(src), quads(rel)], axis=1)
    a["feat_q"] = quads(feat)
    return a


def update_nodes(nc, S, A):
    L = "L0_gnn_"
    with ExitStack() as ctx:
        ph = Phase(nc, ctx, "update")
        stat = ph.sb("stat", [P, 4, NB])
        scattered = RowScatter(ph, S, A, ROW_EARLY, ROW_TURNS - ROW_EARLY)
        wide = S["big2"][:, :, D:D2]
        Y = S["big2"][:, :, 0:D]
        sums = ph.sb("sums", [P, D2])
        hst = ph.sb("hst", [P, D])
        sumsT = ph.sb("sumsT", [P, 4, P])
        hT = ph.sb("hT", [P, 2, P])
        aggT = ph.sb("aggT", [P, 2, P])
        upT = ph.sb("upT", [P, 4, P])
        eW2 = ph.sb("eW2", [P, 4, D])
        nW1 = ph.sb("nW1", [P, 4, D2])
        nW2 = ph.sb("nW2", [P, 4, D])
        eb2 = ph.sb("eb2", [1, D])
        nb1 = ph.sb("nb1", [P, 4])
        rows = ph.sb("rows", [P, 3, D])
        deg_row = S["big2"][0:1, :, D:D + P]
        deg_i = ph.sb("deg_i", [1, NL], I32)
        psR, psH, psM, psU, psY = (ph.ps(n, [P, 512]) for n in ("psR", "psH", "psM", "psU", "psY"))
        s_hT = ph.sem("hT_ready")
        s_w, s_v, s_var, s_root, s_deg, s_st, s_T, s_sT, s_M, s_mT, s_U, s_uT, s_Y, s_y = (
            ph.sem(n) for n in ("weights_loaded", "dve_step", "var_ready", "root_ready", "deg_ready",
                                "staged", "turned", "turned_copied", "agg_sums", "agg_copied", "up_sums",
                                "up_ready", "down_sums", "y_ready"))
        with nc.Block() as block:
            @block.sync
            def _(sp):
                chunks = lambda ap: ap.rearrange("(c p) n -> p c n", p=P)
                for to, of in ((eW2[:, :, :], chunks(A[L + "eW2"])), (nW1[:, :, :], chunks(A[L + "nW1"])),
                               (nW2[:, :, :], chunks(A[L + "nW2"])), (eb2[:, :], A[L + "eb2"].rearrange("(a n) -> a n", a=1)),
                               (nb1[:, :], A[L + "nb1"].rearrange("(c p) -> p c", p=P)),
                               (rows[:, 0, :], rows_of(A[L + "nb2"], D)), (rows[:, 1, :], rows_of(A[L + "ln_gamma"], D)),
                               (rows[:, 2, :], rows_of(A[L + "ln_beta"], D)),
                               (deg_i[:, :], S["lane_d"][:, 2].rearrange("(a n) -> a n", a=1))):
                    sp.dma_start(to, of, allow_slow_non_contiguous=True).then_inc(s_w, 16)
                scattered.load(sp)

            @block.gpsimd
            def _(pool):
                scattered.scatter(pool)
                scattered.finish(pool)

            @block.scalar
            def _(act):
                def turned_sums(b):
                    act.wait_ge(s_T, b + 1)
                    act.activation(sumsT[:, :, :], psR[:, :].rearrange("p (c n) -> p c n", c=4), ACT.Copy).then_inc(s_sT, 1)

                def turned_h():
                    act.activation(hT[:, :, :], psH[:, 0:D].rearrange("p (c n) -> p c n", c=2), ACT.Copy).then_inc(s_hT, 1)

                def aggregate(b):
                    act.wait_ge(s_M, b + 1)
                    act.activation(aggT[:, :, :], psM[:, 0:D].rearrange("p (c n) -> p c n", c=2), ACT.Copy).then_inc(s_mT, 1)

                def up(b):
                    act.wait_ge(s_U, b + 1)
                    for c in range(4):
                        last = act.activation(upT[:, c, :], psU[:, c * P:(c + 1) * P], ACT.Relu, bias=nb1[:, c:c + 1])
                    last.then_inc(s_uT, 1)

                act.wait_ge(s_w, 16 * 9)
                turned_sums(0)
                turned_h()
                with act.Fori(0, NB - 1) as b:
                    aggregate(b)
                    turned_sums(b + 1)
                    up(b)
                    turned_h()
                aggregate(NB - 1)
                up(NB - 1)
                take_root(act, stat, s_var, s_root, 1)

            @block.tensor
            def _(pe):
                def turn(b):
                    if not isinstance(b, int) or b:
                        pe.wait_ge(s_hT, b)
                    pe.wait_ge(s_st, b + 1)
                    for c in range(4):
                        pe.transpose(psR[:, c * P:(c + 1) * P], sums[:, c * P:(c + 1) * P], S["ident"][:, :])
                    for c in range(2):
                        last = pe.transpose(psH[:, c * P:(c + 1) * P], hst[:, c * P:(c + 1) * P], S["ident"][:, :])
                    last.then_inc(s_T, 1)

                def aggregate(b):
                    pe.wait_ge(s_sT, b + 1)
                    for f in range(2):
                        to = psM[:, f * P:(f + 1) * P]
                        for c in range(4):
                            pe.matmul(to, eW2[:, c, f * P:(f + 1) * P], sumsT[:, c, :], start=(c == 0), stop=False)
                        last = pe.matmul(to, eb2[0:1, f * P:(f + 1) * P], blk(deg_row, b), start=False, stop=True)
                    last.then_inc(s_M, 1)

                def up(b):
                    pe.wait_ge(s_mT, b + 1)
                    for f in range(4):
                        for c in range(4):
                            last = pe.matmul(psU[:, f * P:(f + 1) * P], nW1[:, c, f * P:(f + 1) * P],
                                             (hT[:, c, :] if c < 2 else aggT[:, c - 2, :]), start=(c == 0), stop=(c == 3))
                    last.then_inc(s_U, 1)

                def down(b):
                    pe.wait_ge(s_uT, b + 1)
                    pe.wait_ge(s_y, b + 1)
                    for c in range(4):
                        last = pe.matmul(psY[:, 0:D], upT[:, c, :], nW2[:, c, :], start=(c == 0), stop=(c == 3))
                    last.then_inc(s_Y, 1)

                pe.wait_ge(s_w, 16 * 9)
                pe.wait_ge(s_deg, 1)
                turn(0)
                aggregate(0)
                turn(1)
                up(0)
                with pe.Fori(0, NB - 2) as b:
                    aggregate(b + 1)
                    turn(b + 2)
                    down(b)
                    up(b + 1)
                aggregate(NB - 1)
                down(NB - 2)
                up(NB - 1)
                down(NB - 1)

            @block.vector
            def _(dve):
                scattered.clear(dve)
                step = Chain(dve, s_v)
                dve.wait_ge(s_w, 16 * 9)
                step(dve.tensor_copy(deg_row, deg_i[:, :].rearrange("a (b n) -> a b n", n=P)))
                dve.nop().then_inc(s_deg, 1)
                dve.nop().then_inc(s_y, 1)
                def stage(b):
                    dve.wait_ge(s_T, b)
                    dve.nop(nofuse=True)
                    dve.tensor_copy(sums[:, :], blk(S["big"], b))
                    dve.tensor_copy(hst[:, :], blk(S["H"], b)).then_inc(s_st, 1)

                def result(b):
                    dve.wait_ge(s_Y, b + 1)
                    dve.tensor_tensor(blk(Y, b), psY[:, 0:D], blk(S["H"], b), ALU.add).then_inc(s_y, 1)

                dve.tensor_copy(sums[:, :], blk(S["big"], 0))
                dve.tensor_copy(hst[:, :], blk(S["H"], 0)).then_inc(s_st, 1)
                stage(1)
                with dve.Fori(0, NB - 2) as b:
                    stage(b + 2)
                    result(b)
                result(NB - 2)
                result(NB - 1)
                dve.wait_ge(s_y, NB + 1)
                row = lambda i: bc(rows[:, i, :], 1, [P, NB, D])
                step(dve.tensor_tensor(Y, Y, row(0), ALU.add))
                finish_layer(dve, step, S, Y, wide, stat, s_var, s_root, row(1), row(2))
        ph.close()


def finish_layer(dve, step, S, Y, wide, stat, s_var, s_root, gamma, beta):
    norm_begin(dve, step, Y, Y, stat, wide)
    dve.nop().then_inc(s_var, 1)
    dve.wait_ge(s_root, 1)
    norm_end(dve, step, Y, stat)
    step(dve.tensor_tensor(Y, Y, gamma, ALU.mult))
    step(dve.tensor_tensor(S["X"][:, :, :], S["X"][:, :, :], beta, ALU.add))
    step(dve.tensor_tensor(S["X"][:, :, :], S["X"][:, :, :], Y, ALU.add))


def attend(nc, S, A, layer):
    heads = (None, 4, 8)[layer]
    hd = D // heads
    ROWS = QE + 1
    with ExitStack() as ctx:
        ph = Phase(nc, ctx, f"edge{layer}")
        rec = ph.sb("rec", [P, RING, REC], I32)
        FW = (None, ED, SROW)[layer]
        feat = ph.sb("feat", [P, RING, QE, FW])
        PAIR = (None, 2, 1)[layer]
        TP = PAIR * ED
        featT = ph.sb("featT", [TP, 2, QE // PAIR, P])
        IN_BIG2 = NB * D2 // (QE * D2)
        rest = ph.sb("ring", [P, RING - IN_BIG2, QE, D2])
        ring = [S["big2"].rearrange("p b f -> p (b f)")[:, k * QE * D2:(k + 1) * QE * D2].rearrange("p (s f) -> p s f", f=D2)
                for k in range(IN_BIG2)] + [rest[:, k, :, :] for k in range(RING - IN_BIG2)]
        w_edge = ph.sb("w_edge", [P, D])
        prod = ph.sb("prod", [P, QE, D])
        cat = ph.sb("cat", [P, 2, ROWS, heads])
        wgt = ph.sb("wgt", [P, 2, ROWS, heads])
        tot = ph.sb("tot", [P, heads])
        psT = [ph.ps(f"psT{i}", [P, 512]) for i in range(2)]
        psX = [ph.ps(f"psX{i}", [P, 2, QE // 2, D]) for i in range(2)]
        s_rec, s_done, s_feat, s_g = ([ph.sem(f"{n}{k}") for k in range(RING)] for n in (
            "rec_loaded", "quad_done", "feat_ready", "rows_loaded"))
        s_w, s_v, s_T, s_fT, s_x, s_xr, s_cat, s_exp, s_wr = (ph.sem(n) for n in (
            "weights_loaded", "dve_step", "feat_turned", "featT_ready", "keys_ready", "keys_read",
            "scores_ready", "weights_ready", "w_edge_ready"))
        turns = lambda eng: eng.value_load(S[f"turns{layer - 1}"][0:1, 0:1], min_val=1, max_val=NG_PAD // AQ)
        CH = 12 * AQ
        FEAT_INC = 1 if layer == 1 else 16
        PRE = 4 + (layer == 1)

        with nc.Block() as block:
            @block.sync
            def _(sp):
                for h in range(2):
                    if layer == 2:
                        sp.dma_start(w_edge[h * ED:(h + 1) * ED, :], A["L2_gnn_We"][:, :]).then_inc(s_w, 16)
                    else:
                        for i in range(heads):
                            sp.dma_start(w_edge[h * ED:(h + 1) * ED, i * hd:(i + 1) * hd], A["L1_gnn_rel_w"][:, :]).then_inc(s_w, 16)
                n = turns(sp)
                with sp.Fori(0, n) as t:
                    for q in range(AQ):
                        k = q % RING
                        sp.wait_ge(s_done[k], uses(t, q, RING))
                        sp.dma_start(rec[:, k, :], S[f"rec_d{layer - 1}"][bass.ds(t * AQ + q, 1), :, :].rearrange("a p f -> p (a f)")).then_inc(s_rec[k], 16)

            @block.gpsimd
            def _(pool):
                def features(k):
                    if layer == 2:
                        pool.indirect_dma_start(out=feat[:, k, :, :].rearrange("p s f -> p (s f)"), out_offset=None,
                                                in_=S["sorted_d"].rearrange("(q e) f -> q (e f)", e=QE),
                                                in_offset=bass.IndirectOffsetOnAxis(ap=rec[:, k, R_QUAD:R_QUAD + 1], axis=0)).then_inc(s_feat[k], 16)
                    else:
                        for s in range(QE):
                            last = pool.tensor_scalar(feat[:, k, s, :], S["iota_c"][:, 0:ED], rec[:, k, R_REL + s:R_REL + s + 1].bitcast(F32), None, ALU.is_equal)
                        last.then_inc(s_feat[k], 1)

                n = turns(pool)
                with pool.Fori(0, n) as t:
                    for q in range(AQ):
                        k = q % RING
                        hold(pool, s_rec[k], uses(t, q, RING) * 16)
                        features(k)
                        for s in range(QE):
                            pool.indirect_dma_start(out=ring[k][:, s, :], out_offset=None, in_=S[f"tab{layer}"][:, :],
                                                    in_offset=bass.IndirectOffsetOnAxis(ap=rec[:, k, R_SRC + s:R_SRC + s + 1], axis=0)).then_inc(s_g[k], 16)
                hold(pool, s_done[0], uses(n, 0, RING))
                features(0)

            @block.scalar
            def _(act):
                def copy_features(t, k, buf):
                    act.wait_ge(s_T, t * AQ + (k + 1))
                    act.activation(featT[:, buf, :, :], psT[buf][0:TP, 0:QE // PAIR * P].rearrange("p (c n) -> p c n", n=P), ACT.Copy).then_inc(s_fT, 1)

                act.nop().then_inc(s_fT, 1)
                act.nop().then_inc(s_exp, 1)
                n = turns(act)
                copy_features(0, 0, 0)
                with act.Fori(0, n) as t:
                    for k in range(AQ):
                        copy_features(t, k + 1, (k + 1) % 2)
                        act.wait_ge(s_cat, t * AQ + (k + 1))
                        act.activation(wgt[:, k % 2, :, :], cat[:, k % 2, :, :], ACT.Exp).then_inc(s_exp, 1)

            @block.tensor
            def _(pe):
                def turn_features(t, k, buf):
                    at = k % RING
                    pe.wait_ge(s_feat[at], uses(t, k, RING) * FEAT_INC)
                    hold(pe, s_fT, t * AQ + (k if k else 1))
                    for c in range(QE // PAIR):
                        slots = feat[:, at, 2 * c:2 * c + 2, :] if PAIR == 2 else feat[:, at, c, 0:ED]
                        last = pe.transpose(psT[buf][0:TP, c * P:(c + 1) * P], slots, S["ident"][:, :])
                    last.then_inc(s_T, 1)

                pe.wait_ge(s_wr, 1)
                n = turns(pe)
                turn_features(0, 0, 0)
                with pe.Fori(0, n) as t:
                    for k in range(AQ):
                        pe.wait_ge(s_g[k % RING], uses(t, k, RING) * (16 * QE))
                        pe.wait_ge(s_fT, t * AQ + (k + 2))
                        pe.wait_ge(s_xr, t * AQ + (k + 1))
                        for s in range(QE):
                            lo = ED * (s % PAIR)
                            if s == QE - 1:
                                turn_features(t, k + 1, (k + 1) % 2)
                            pe.matmul(psX[k % 2][:, s % 2, s // 2, :], featT[lo:lo + ED, k % 2, s // PAIR, :], w_edge[lo:lo + ED, :], start=True, stop=False)
                            last = pe.matmul(psX[k % 2][:, s % 2, s // 2, :], S["ident"][:, :], ring[k % RING][:, s, 0:D], start=False, stop=True)
                        last.then_inc(s_x, 1)

            @block.vector
            def _(dve):
                def block_of(q, t=None):
                    k = q % RING
                    if t is not None:
                        hold(dve, s_rec[k], uses(t, q, RING) * 16)
                    return dve.value_load(rec[0:1, k, R_BLOCK:R_BLOCK + 1], min_val=0, max_val=NB - 1)

                def last_values(step, t, k, at, b):
                    dve.wait_ge(s_exp, t * AQ + (k + 1))
                    w = wgt[:, at % 2, :, :]
                    v = ring[at][:, :, D:D2]
                    acc = blk(S["big"], b)[:, D:D2]
                    acc_h = acc.rearrange("p (h d) -> p h d", h=heads)
                    l = blk(S["l"], b)[:, 0:heads]
                    vals = v.rearrange("p s (h d) -> p s h d", h=heads)
                    dve.nop(nofuse=True)
                    dve.tensor_tensor(l, l, w[:, QE, :], ALU.mult)
                    dve.tensor_tensor(vals, vals, bc(w[:, 0:QE, :], 3, [P, QE, heads, hd]), ALU.mult)
                    step(dve.tensor_reduce(tot[:, :], w[:, 0:QE, :].rearrange("p r h -> p h r"), AX.X, ALU.add))
                    step(dve.tensor_tensor(v[:, 0:2, :], v[:, 0:2, :], v[:, 2:4, :], ALU.add))
                    dve.tensor_tensor(acc_h, acc_h, bc(w[:, QE, :], 2, [P, heads, hd]), ALU.mult)
                    dve.tensor_tensor(l, l, tot[:, :], ALU.add)
                    step(dve.tensor_tensor(v[:, 0, :], v[:, 0, :], v[:, 1, :], ALU.add))
                    step(dve.tensor_tensor(acc, acc, v[:, 0, :], ALU.add))
                    dve.nop().then_inc(s_done[at], 1)

                pre = Chain(dve, s_v)
                dve.wait_ge(s_w, 32 if layer == 2 else 32 * heads)
                pre(dve.memset(rec[:, RING - 1, :], 0))
                pre(dve.memset(ring[RING - 1][:, :, D:D2], 0.0))
                pre(dve.memset(wgt[:, 1, 0:QE, :], 0.0))
                pre(dve.memset(wgt[:, 1, QE, :], 1.0))
                if layer == 1:
                    pre(dve.tensor_scalar(w_edge[:, :], w_edge[:, :], 0.2, None, ALU.mult))
                dve.nop().then_inc(s_wr, 1)
                dve.nop().then_inc(s_xr, 2)
                for k in range(RING - 1):
                    dve.nop().then_inc(s_done[k], 1)
                n = turns(dve)
                with dve.Fori(0, n) as t:
                    step = Chain(dve, s_v, t * CH + PRE)
                    b_prev, b = block_of(RING - 1), block_of(0, t)
                    for k in range(AQ):
                        at = (k - 1) % RING
                        mask = rec[:, k % RING, R_MASK:R_MASK + QE].bitcast(F32)
                        score, m = cat[:, k % 2, :, :], blk(S["m"], b)[:, 0:heads]
                        w, v = wgt[:, at % 2, :, :], ring[at][:, :, D:D2]
                        acc, l = blk(S["big"], b_prev)[:, D:D2], blk(S["l"], b_prev)[:, 0:heads]
                        acc_h, vals = acc.rearrange("p (h d) -> p h d", h=heads), v.rearrange("p s (h d) -> p s h d", h=heads)
                        dve.wait_ge(s_x, t * AQ + (k + 1))
                        step.put(dve.tensor_scalar(score[:, QE, :], m, 0.0, None, ALU.add))
                        dve.tensor_tensor(prod[:, :, :].rearrange("p (c a) d -> p a c d", a=2), psX[k % 2][:, :, :, :],
                                          blk(S["big"], b)[:, 0:D].unsqueeze(1).unsqueeze(1).broadcast_to([P, 2, QE // 2, D]), ALU.mult).then_inc(s_xr, 1)
                        hold(dve, s_exp, t * AQ + (k + 1))
                        step.put(dve.tensor_tensor(l, l, w[:, QE, :], ALU.mult))
                        weighted = step.put(dve.tensor_tensor(vals, vals, bc(w[:, 0:QE, :], 3, [P, QE, heads, hd]), ALU.mult))
                        dve.wait_ge(s_xr, t * AQ + (k + 3))
                        scored = step.put(dve.tensor_reduce(score[:, 0:QE, :].rearrange("p s h -> p (s h)"),
                                                            prod[:, :, :].rearrange("p s (h d) -> p (s h) d", d=hd), AX.X, ALU.add))
                        b_next = block_of(k + 1, t) if k < AQ - 1 else None
                        step.put(dve.tensor_reduce(tot[:, :], w[:, 0:QE, :].rearrange("p r h -> p h r"), AX.X, ALU.add))
                        step.until(weighted)
                        halved = step.put(dve.tensor_tensor(v[:, 0:2, :], v[:, 0:2, :], v[:, 2:4, :], ALU.add))
                        step.until(scored)
                        masked = step.put(dve.tensor_tensor(score[:, 0:QE, :], score[:, 0:QE, :], bc(mask, 2, [P, QE, heads]), ALU.add))
                        step.put(dve.tensor_tensor(acc_h, acc_h, bc(w[:, QE, :], 2, [P, heads, hd]), ALU.mult))
                        step.until(masked)
                        dve.nop(nofuse=True)
                        highest = step.put(dve.tensor_reduce(m, score.rearrange("p r h -> p h r"), AX.X, ALU.max))
                        step.until(halved)
                        summed = step.put(dve.tensor_tensor(v[:, 0, :], v[:, 0, :], v[:, 1, :], ALU.add))
                        step.until(highest)
                        dve.tensor_tensor(score, score, bc(m, 1, [P, ROWS, heads]), ALU.subtract).then_inc(s_cat, 1)
                        step.put(dve.tensor_tensor(l, l, tot[:, :], ALU.add))
                        step.until(summed)
                        step(dve.tensor_tensor(acc, acc, v[:, 0, :], ALU.add))
                        dve.nop().then_inc(s_done[at], 1)
                        b_prev, b = b, b_next
                    while step.n < CH:
                        step(dve.nop())
                    assert step.n == CH, step.n
                step = Chain(dve, s_v, n * CH + PRE)
                last_values(step, n, 0, RING - 1, block_of(RING - 1))
        ph.close()


def project_out(nc, S, A):
    L, heads = "L1_gnn_", 4
    with ExitStack() as ctx:
        ph = Phase(nc, ctx, "project")
        stat = ph.sb("stat", [P, 4, NB])
        Y, wide = S["big2"][:, :, 0:D], S["big2"][:, :, D:D2]
        msg = ph.sb("msg", [P, D])
        msgT = ph.sb("msgT", [P, 2, P])
        Wo = ph.sb("Wo", [P, 2, D])
        rows = ph.sb("rows", [P, 3, D])
        rl = ph.sb("rl", [P, NB, heads])
        psT, psY = ph.ps("psT", [P, 512]), ph.ps("psY", [P, 512])
        s_w, s_v, s_var, s_root, s_n, s_st, s_T, s_mT, s_Y, s_y = (ph.sem(n) for n in (
            "weights_loaded", "dve_step", "var_ready", "root_ready", "normalised", "staged", "turned",
            "turned_copied", "out_sums", "y_ready"))
        with nc.Block() as block:
            @block.sync
            def _(sp):
                sp.dma_start(Wo[:, :, :], A[L + "Wo"].rearrange("(c p) n -> p c n", p=P)).then_inc(s_w, 16)
                for i, n in enumerate(("bo", "gamma", "beta")):
                    sp.dma_start(rows[:, i, :], rows_of(A[L + n], D)).then_inc(s_w, 16)

            @block.scalar
            def _(act):
                act.wait_ge(s_n, 1)
                with act.Fori(0, NB) as b:
                    act.activation(msg[:, :], blk(S["big"], b)[:, D:D2], ACT.Copy).then_inc(s_st, 1)
                    act.wait_ge(s_T, b + 1)
                    act.activation(msgT[:, :, :], psT[:, 0:D].rearrange("p (c n) -> p c n", c=2), ACT.Copy).then_inc(s_mT, 1)
                take_root(act, stat, s_var, s_root, 1)

            @block.tensor
            def _(pe):
                pe.wait_ge(s_w, 64)
                with pe.Fori(0, NB) as b:
                    pe.wait_ge(s_st, b + 1)
                    for c in range(2):
                        last = pe.transpose(psT[:, c * P:(c + 1) * P], msg[:, c * P:(c + 1) * P], S["ident"][:, :])
                    last.then_inc(s_T, 1)
                    pe.wait_ge(s_mT, b + 1)
                    pe.wait_ge(s_y, b + 1)
                    for c in range(2):
                        last = pe.matmul(psY[:, 0:D], msgT[:, c, :], Wo[:, c, :], start=(c == 0), stop=(c == 1))
                    last.then_inc(s_Y, 1)

            @block.vector
            def _(dve):
                step = Chain(dve, s_v)
                step(dve.reciprocal(rl[:, :, :], S["l"][:, :, 0:heads]))
                acc = all_heads(S["big"][:, :, D:D2], heads)
                step(dve.tensor_tensor(acc, acc, bc(rl[:, :, :], 3, [P, NB, heads, D // heads]), ALU.mult))
                dve.nop().then_inc(s_n, 1)
                dve.nop().then_inc(s_y, 1)
                with dve.Fori(0, NB) as b:
                    dve.wait_ge(s_Y, b + 1)
                    dve.tensor_tensor(blk(Y, b), psY[:, 0:D], blk(S["H"], b), ALU.add).then_inc(s_y, 1)
                dve.wait_ge(s_y, NB + 1)
                dve.wait_ge(s_w, 64)
                row = lambda i: bc(rows[:, i, :], 1, [P, NB, D])
                step(dve.tensor_tensor(Y, Y, row(0), ALU.add))
                finish_layer(dve, step, S, Y, wide, stat, s_var, s_root, row(1), row(2))
        ph.close()


def share_softmax(nc, S, A):
    heads = 8
    with ExitStack() as ctx:
        ph = Phase(nc, ctx, "share")
        mx = ph.sb("mx", [P, heads])
        mcol = ph.sb("mcol", [heads, 1])
        mcols = ph.sb("mcols", [heads, P])
        mall = ph.sb("mall", [P, heads])
        sc = ph.sb("sc", [P, NB, heads])
        ls = ph.sb("ls", [P, NB, heads])
        lsum = ph.sb("lsum", [P, heads])
        rz = ph.sb("rz", [P, heads])
        bias = ph.sb("bias", [P, D])
        ps1, ps2, ps3 = (ph.ps(f"ps{i}", [P, 512]) for i in range(3))
        s_w, s_v, s_mx, s_mt, s_col, s_all, s_d, s_e, s_l, s_z = (ph.sem(n) for n in (
            "bias_loaded", "dve_step", "max_ready", "max_turned", "col_ready", "max_spread", "diff_ready",
            "exp_ready", "sum_ready", "sum_spread"))
        with nc.Block() as block:
            @block.sync
            def _(sp):
                sp.dma_start(bias[:, :], rows_of(A["L2_gnn_bias"], D)).then_inc(s_w, 16)

            @block.scalar
            def _(act):
                act.wait_ge(s_d, 1)
                act.activation(sc[:, :, :], sc[:, :, :], ACT.Exp).then_inc(s_e, 1)

            @block.tensor
            def _(pe):
                pe.wait_ge(s_mx, 1)
                pe.transpose(ps1[0:heads, 0:P], mx[:, :], S["ident"][:, :]).then_inc(s_mt, 1)
                pe.wait_ge(s_col, 1)
                pe.matmul(ps2[:, 0:heads], mcols[:, :], S["ident"][0:heads, 0:heads], start=True, stop=True).then_inc(s_all, 1)
                pe.wait_ge(s_l, 1)
                pe.matmul(ps3[:, 0:heads], S["ones"][:, :], lsum[:, :], start=True, stop=True).then_inc(s_z, 1)

            @block.vector
            def _(dve):
                step = Chain(dve, s_v)
                step(dve.tensor_reduce(mx[:, :], S["m"][:, :, 0:heads].rearrange("p b h -> p h b"), AX.X, ALU.max))
                dve.nop().then_inc(s_mx, 1)
                dve.wait_ge(s_mt, 1)
                step(dve.tensor_reduce(mcol[:, :], ps1[0:heads, 0:P], AX.X, ALU.max))
                step(dve.tensor_scalar(mcols[:, :], S["ones"][0:heads, :], mcol[:, 0:1], None, ALU.mult))
                dve.nop().then_inc(s_col, 1)
                dve.wait_ge(s_all, 1)
                step(dve.tensor_copy(mall[:, :], ps2[:, 0:heads]))
                step(dve.tensor_tensor(sc[:, :, :], S["m"][:, :, 0:heads], bc(mall[:, :], 1, [P, NB, heads]), ALU.subtract))
                dve.nop().then_inc(s_d, 1)
                dve.wait_ge(s_e, 1)
                step(dve.tensor_tensor(ls[:, :, :], S["l"][:, :, 0:heads], sc[:, :, :], ALU.mult))
                step(dve.tensor_reduce(lsum[:, :], ls[:, :, :].rearrange("p b h -> p h b"), AX.X, ALU.add))
                dve.nop().then_inc(s_l, 1)
                dve.wait_ge(s_z, 1)
                step(dve.reciprocal(rz[:, :], ps3[:, 0:heads]))
                step(dve.tensor_tensor(sc[:, :, :], sc[:, :, :], bc(rz[:, :], 1, [P, NB, heads]), ALU.mult))
                acc = all_heads(S["big"][:, :, D:D2], heads)
                step(dve.tensor_tensor(acc, acc, bc(sc[:, :, :], 3, [P, NB, heads, D // heads]), ALU.mult))
                X = S["X"][:, :, :]
                step(dve.tensor_tensor(X, X, S["big"][:, :, D:D2], ALU.add))
                dve.wait_ge(s_w, 16)
                step(dve.tensor_tensor(X, X, bc(bias[:, :], 1, [P, NB, D]), ALU.add))
        ph.close()


def gat_edges(nc, S, A):
    ROWS = QE + 1
    with ExitStack() as ctx:
        ph = Phase(nc, ctx, "edge3")
        rec = ph.sb("rec", [P, RING, REC], I32)
        ring = S["big2"].rearrange("p b f -> p (b f)")[:, 0:RING * QE * XROW].rearrange("p (k s f) -> p k s f", k=RING, f=XROW)
        cat = ph.sb("cat", [P, 2, ROWS])
        wgt = ph.sb("wgt", [P, 2, ROWS])
        tot = ph.sb("tot", [P, 1])
        s_rec, s_done, s_g = ([ph.sem(f"{n}{k}") for k in range(RING)] for n in ("rec_loaded", "quad_done", "rows_loaded"))
        s_v, s_cat, s_exp = (ph.sem(n) for n in ("dve_step", "scores_ready", "weights_ready"))
        turns = lambda eng: eng.value_load(S["turns0"][0:1, 0:1], min_val=1, max_val=NG_PAD // AQ)
        CH = 12 * AQ
        PRE = 4

        with nc.Block() as block:
            @block.sync
            def _(sp):
                n = turns(sp)
                with sp.Fori(0, n) as t:
                    for q in range(AQ):
                        k = q % RING
                        sp.wait_ge(s_done[k], uses(t, q, RING))
                        sp.dma_start(rec[:, k, :], S["rec_d0"][bass.ds(t * AQ + q, 1), :, :].rearrange("a p f -> p (a f)")).then_inc(s_rec[k], 16)

            @block.gpsimd
            def _(pool):
                n = turns(pool)
                with pool.Fori(0, n) as t:
                    for q in range(AQ):
                        k = q % RING
                        hold(pool, s_rec[k], uses(t, q, RING) * 16)
                        for s in range(QE):
                            pool.indirect_dma_start(out=ring[:, k, s, :], out_offset=None, in_=S["tab3"][:, :],
                                                    in_offset=bass.IndirectOffsetOnAxis(ap=rec[:, k, R_SRC + s:R_SRC + s + 1], axis=0)).then_inc(s_g[k], 16)

            @block.scalar
            def _(act):
                act.nop().then_inc(s_exp, 1)
                n = turns(act)
                with act.Fori(0, n) as t:
                    for k in range(AQ):
                        act.wait_ge(s_cat, t * AQ + (k + 1))
                        act.activation(wgt[:, k % 2, :], cat[:, k % 2, :], ACT.Exp).then_inc(s_exp, 1)

            @block.vector
            def _(dve):
                def block_of(k):
                    return dve.value_load(rec[0:1, k, R_BLOCK:R_BLOCK + 1], min_val=0, max_val=NB - 1)

                def last_values(step, t, k, at, b):
                    dve.wait_ge(s_exp, t * AQ + (k + 1))
                    w, l = wgt[:, at % 2, :], S["l"][:, bass.ds(b, 1), 0]
                    acc = blk(S["big"], b)[:, D:D2]
                    dve.nop(nofuse=True)
                    dve.tensor_scalar(acc, acc, w[:, QE:ROWS], None, ALU.mult)
                    step(dve.tensor_reduce(tot[:, :], w[:, 0:QE], AX.X, ALU.add))
                    dve.scalar_tensor_tensor(l, l, w[:, QE:ROWS], tot[:, :], ALU.mult, ALU.add)
                    for s in range(QE):
                        step(dve.scalar_tensor_tensor(acc, ring[:, at, s, 0:D], w[:, s:s + 1], acc, ALU.mult, ALU.add))
                    dve.nop().then_inc(s_done[at], 1)

                pre = Chain(dve, s_v)
                pre(dve.memset(rec[:, RING - 1, :], 0))
                pre(dve.memset(ring[:, RING - 1, :, :], 0.0))
                pre(dve.memset(wgt[:, 1, 0:QE], 0.0))
                pre(dve.memset(wgt[:, 1, QE:ROWS], 1.0))
                for k in range(RING - 1):
                    dve.nop().then_inc(s_done[k], 1)
                n = turns(dve)
                with dve.Fori(0, n) as t:
                    step = Chain(dve, s_v, t * CH + PRE)
                    hold(dve, s_rec[0], uses(t, 0, RING) * 16)
                    b_prev, b = block_of(RING - 1), block_of(0)
                    for k in range(AQ):
                        at = (k - 1) % RING
                        mask = rec[:, k % RING, R_MASK:R_MASK + QE].bitcast(F32)
                        score, m = cat[:, k % 2, :], S["m"][:, bass.ds(b, 1), 0]
                        w, l = wgt[:, at % 2, :], S["l"][:, bass.ds(b_prev, 1), 0]
                        acc = blk(S["big"], b_prev)[:, D:D2]
                        slot = lambda s: dve.scalar_tensor_tensor(acc, ring[:, at, s, 0:D], w[:, s:s + 1], acc, ALU.mult, ALU.add)
                        dve.wait_ge(s_g[k % RING], uses(t, k, RING) * (16 * QE))
                        step.put(dve.tensor_scalar(score[:, QE:ROWS], m, 0.0, None, ALU.add))
                        raw = step.put(dve.tensor_scalar(score[:, 0:QE], ring[:, k % RING, :, D], S["adst"][:, bass.ds(b, 1)], None, ALU.add))
                        hold(dve, s_exp, t * AQ + (k + 1))
                        rescaled = step.put(dve.tensor_scalar(acc, acc, w[:, QE:ROWS], None, ALU.mult))
                        step.until(raw)
                        leaky = step.put(dve.scalar_tensor_tensor(score[:, 0:QE], score[:, 0:QE], 0.2, score[:, 0:QE], ALU.mult, ALU.max))
                        step.until(rescaled)
                        slot_0 = step.put(slot(0))
                        step.until(leaky)
                        masked = step.put(dve.tensor_tensor(score[:, 0:QE], score[:, 0:QE], mask, ALU.add))
                        step.put(dve.tensor_reduce(tot[:, :], w[:, 0:QE], AX.X, ALU.add))
                        step.until(slot_0)
                        slot_1 = step.put(slot(1))
                        step.until(masked)
                        dve.nop(nofuse=True)
                        highest = step.put(dve.tensor_reduce(m, score, AX.X, ALU.max))
                        step.until(slot_1)
                        slot_2 = step.put(slot(2))
                        step.until(highest)
                        dve.tensor_scalar(score, score, m, None, ALU.subtract).then_inc(s_cat, 1)
                        step.put(dve.scalar_tensor_tensor(l, l, w[:, QE:ROWS], tot[:, :], ALU.mult, ALU.add))
                        b_next = None
                        if k < AQ - 1:
                            hold(dve, s_rec[(k + 1) % RING], uses(t, k + 1, RING) * 16)
                            b_next = block_of((k + 1) % RING)
                        step.until(slot_2)
                        step(slot(3))
                        dve.nop().then_inc(s_done[at], 1)
                        b_prev, b = b, b_next
                    while step.n < CH:
                        step(dve.nop())
                    assert step.n == CH, step.n
                step = Chain(dve, s_v, n * CH + PRE)
                last_values(step, n, 0, RING - 1, block_of(RING - 1))
        ph.close()


def gate_nodes(nc, S, A, out):
    L = "L3_gnn_"
    GATES = (0, 2, 3)
    with ExitStack() as ctx:
        ph = Phase(nc, ctx, "gate")
        bias = ph.sb("bias", [P, D])
        w_nat = ph.sb("w_nat", [P, 6, D])
        wT = ph.sb("wT", [P, 2, 3 * D])
        rl = ph.sb("rl", [P, NB])
        hb = ph.sb("hb", [P, D])
        hbT = ph.sb("hbT", [P, 2, P])
        gi, gc, go, cell = (ph.sb(n, [P, D]) for n in ("gi", "gc", "go", "cell"))
        res = ph.sb("res", [P, D])
        idx = ph.sb("idx", [P, 1], I32)
        psW = [ph.ps(f"psW{i}", [P, 512]) for i in range(3)]
        psT, psA, psB = (ph.ps(n, [P, 512]) for n in ("psT", "psA", "psB"))
        s_w, s_v, s_wT, s_wc, s_n, s_st, s_T, s_hT, s_A, s_g, s_c, s_t, s_res, s_out = (ph.sem(n) for n in (
            "weights_loaded", "dve_step", "w_turned", "w_copied", "normalised", "staged", "turned",
            "turned_copied", "gate_sums", "gates_ready", "cell_ready", "cell_tanh", "result_ready", "rows_stored"))
        IN_LOOP = 3
        with nc.Block() as block:
            @block.sync
            def _(sp):
                sp.dma_start(bias[:, :], rows_of(A[L + "bias"], D)).then_inc(s_w, 16)
                for i, g in enumerate(GATES):
                    sp.dma_start(w_nat[:, 2 * i:2 * i + 2, :], A[L + "W_ih"][g * D:(g + 1) * D, :].rearrange("(c p) n -> p c n", p=P)).then_inc(s_w, 16)

            @block.gpsimd
            def _(pool):
                with pool.Fori(0, NB) as b:
                    hold(pool, s_res, b + 1)
                    pool.indirect_dma_start(out=out[:, :], out_offset=bass.IndirectOffsetOnAxis(ap=idx[:, 0:1], axis=0),
                                            in_=res[:, :], in_offset=None, bounds_check=N_NODES - 1, oob_is_err=False).then_inc(s_out, 16)
                pool.wait_ge(s_out, 16 * NB)

            @block.scalar
            def _(act):
                def stage(b):
                    if not isinstance(b, int) or b:
                        act.wait_ge(s_T, b)
                        act.nop(nofuse=True)
                    act.activation(hb[:, :], blk(S["big"], b)[:, D:D2], ACT.Tanh).then_inc(s_st, 1)

                def turned(b):
                    act.wait_ge(s_T, b + 1)
                    act.activation(hbT[:, :, :], psT[:, 0:D].rearrange("p (c n) -> p c n", c=2), ACT.Copy).then_inc(s_hT, 1)

                def gates(b):
                    act.wait_ge(s_A, b + 1)
                    if not isinstance(b, int) or b:
                        act.wait_ge(s_res, b)
                    act.activation(gi[:, :], psA[:, 0:D], ACT.Sigmoid)
                    act.activation(gc[:, :], psA[:, D:D2], ACT.Tanh)
                    act.activation(go[:, :], psB[:, 0:D], ACT.Sigmoid).then_inc(s_g, 1)

                def squash(b):
                    act.wait_ge(s_c, b + 1)
                    act.activation(cell[:, :], gc[:, :], ACT.Tanh).then_inc(s_t, 1)

                act.wait_ge(s_n, 1)
                stage(0)
                turned(0)
                stage(1)
                with act.Fori(0, NB - 2) as b:
                    gates(b)
                    turned(b + 1)
                    stage(b + 2)
                    squash(b)
                gates(NB - 2)
                turned(NB - 1)
                squash(NB - 2)
                gates(NB - 1)
                squash(NB - 1)

            @block.tensor
            def _(pe):
                pe.wait_ge(s_w, 64)
                for i in range(6):
                    for k in range(2):
                        last = pe.transpose(psW[i // 2][:, ((i % 2) * 2 + k) * P:((i % 2) * 2 + k + 1) * P], w_nat[:, i, k * P:(k + 1) * P], S["ident"][:, :])
                last.then_inc(s_wT, 1)
                pe.wait_ge(s_wc, 1)
                def turn(b):
                    if not isinstance(b, int) or b:
                        pe.wait_ge(s_hT, b)
                    pe.wait_ge(s_st, b + 1)
                    for c in range(2):
                        last = pe.transpose(psT[:, c * P:(c + 1) * P], hb[:, c * P:(c + 1) * P], S["ident"][:, :])
                    last.then_inc(s_T, 1)

                def gates(b):
                    pe.wait_ge(s_hT, b + 1)
                    if not isinstance(b, int) or b:
                        pe.wait_ge(s_g, b)
                    for c in range(2):
                        pe.matmul(psA[:, :], hbT[:, c, :], wT[:, c, 0:D2], start=(c == 0), stop=(c == 1))
                    for c in range(2):
                        last = pe.matmul(psB[:, 0:D], hbT[:, c, :], wT[:, c, D2:3 * D], start=(c == 0), stop=(c == 1))
                    last.then_inc(s_A, 1)

                turn(0)
                gates(0)
                turn(1)
                with pe.Fori(0, NB - 2) as b:
                    gates(b + 1)
                    turn(b + 2)
                gates(NB - 1)

            @block.vector
            def _(dve):
                step = Chain(dve, s_v)
                dve.wait_ge(s_w, 64)
                dve.wait_ge(s_wT, 1)
                for i in range(6):
                    step(dve.tensor_copy(wT[:, :, i * P:(i + 1) * P], psW[i // 2][:, (i % 2) * D:(i % 2 + 1) * D].rearrange("p (k n) -> p k n", k=2)))
                dve.nop().then_inc(s_wc, 1)
                step(dve.reciprocal(rl[:, :], S["l"][:, :, 0]))
                acc = S["big"][:, :, D:D2]
                step(dve.tensor_tensor(acc, acc, bc(rl[:, :], 2, [P, NB, D]), ALU.mult))
                step(dve.tensor_tensor(acc, acc, bc(bias[:, :], 1, [P, NB, D]), ALU.add))
                dve.nop().then_inc(s_n, 1)
                before = step.n
                with dve.Fori(0, NB) as b:
                    step = Chain(dve, s_v, b * IN_LOOP + before)
                    dve.wait_ge(s_g, b + 1)
                    step(dve.tensor_tensor(gc[:, :], gi[:, :], gc[:, :], ALU.mult))
                    dve.nop().then_inc(s_c, 1)
                    dve.wait_ge(s_t, b + 1)
                    step(dve.tensor_tensor(cell[:, :], cell[:, :], go[:, :], ALU.mult))
                    hold(dve, s_out, b * 16)
                    step(dve.tensor_copy(idx[:, :], S["lane_i"][:, bass.ds(b, 1), 0]))
                    dve.tensor_tensor(res[:, :], cell[:, :], blk(S["X"], b), ALU.add).then_inc(s_res, 1)
                    assert step.n == IN_LOOP
        ph.close()


def graph_network(nc, A, out):
    with ExitStack() as ctx:
        S = shared(nc, ctx)
        with ExitStack() as lists:
            shared_by_lists(nc, lists, S)
            first_steps(nc, S, A)
            rank_edges(nc, S, A)
            order_nodes(nc, S, A)
        build_records(nc, S, A, 0)
        fetch_nodes(nc, S, A)
        make_tables(nc, S, A, 0)
        edge_mlp(nc, S, A)
        update_nodes(nc, S, A)
        build_records(nc, S, A, 1)
        make_tables(nc, S, A, 1)
        attend(nc, S, A, 1)
        project_out(nc, S, A)
        make_tables(nc, S, A, 2)
        attend(nc, S, A, 2)
        share_softmax(nc, S, A)
        make_tables(nc, S, A, 3)
        gat_edges(nc, S, A)
        gate_nodes(nc, S, A, out)


def kernel(**inputs):
    import concourse.bacc as _bacc
    from concourse.bass_utils import run_bass_kernel_spmd as _run

    nc = _bacc.Bacc("TRN2", target_bir_lowering=False, num_devices=1)
    arrays, args = {}, {}
    for name, a in laid_out(inputs).items():
        if name == "L3_gnn_W_hh":
            continue
        arrays[f"in_{name}"] = a
        args[name] = nc.dram_tensor(f"in_{name}", list(a.shape), mybir.dt.from_np(a.dtype), kind="ExternalInput").ap()
    out = nc.dram_tensor("out_0", [N_NODES, D], F32, kind="ExternalOutput").ap()
    graph_network(nc, args, out)
    r = _run(nc, [arrays], core_ids=[0])
    return r.results[0]["out_0"]
```
